# Optimizing a Trainium2 kernel written in Bass

```python
import numpy as np
import jax
import jax.numpy as jnp

def _softmax(x, axis=-1):
    return jax.nn.softmax(x, axis=axis)

def _gelu(x):
    return jax.nn.gelu(x, approximate=True)

def _silu(x):
    return jax.nn.silu(x)

def _sigmoid(x):
    return jax.nn.sigmoid(x)

def _layernorm(x, axis=-1, eps=1e-05):
    m = jnp.mean(x, axis=axis, keepdims=True)
    v = jnp.var(x, axis=axis, keepdims=True)
    return (x - m) / jnp.sqrt(v + eps)

def _scatter_add(tgt, idx, src, axis=0):
    return tgt.at[idx].add(src)

def _segment_sum(src, seg, n):
    return jax.ops.segment_sum(src, seg, n)
kernel_name = 'mk_decoder_postln_d1_seqx_r4_51a430'

def setup_inputs(seed: int=0):
    np.random.seed(seed)
    _w = jnp.asarray

    def _rec_inputs():
        import jax
        import jax.numpy as jnp
        _rk = jax.random.key(seed)
        x = -0.0002928 + 1 * jax.random.normal(jax.random.fold_in(_rk, 1), (4, 1024, 256), jnp.float32)
        _lenS = 1024 - jax.random.randint(jax.random.fold_in(_rk, 7), (4,), 0, max(1, 1024 // 4) + 1, jnp.int32)
        _lenS2 = 154 - jax.random.randint(jax.random.fold_in(_rk, 8), (4,), 0, max(1, 154 // 4) + 1, jnp.int32)
        _ctx_1024P = jax.random.normal(jax.random.fold_in(_rk, 11), (4, 16, 256), jnp.float32)
        _ctx_1024c = jax.random.dirichlet(jax.random.fold_in(_rk, 511), 0.3 * jnp.ones((16,), jnp.float32), (4, 154))
        _ctx_1024t = jnp.einsum('bsk,bkd->bsd', _ctx_1024c, _ctx_1024P)
        _ctx_1024t = _ctx_1024t * jax.lax.rsqrt(jnp.mean(jnp.square(_ctx_1024t)) + 1e-12) * 0.953939
        ctx_1024 = -1.39393e-06 + 0.999914 * (_ctx_1024t + 0.3 * jax.random.normal(jax.random.fold_in(_rk, 611), (4, 154, 256), jnp.float32))
        return (x, ctx_1024)
    x, ctx_1024 = _rec_inputs()

    def _L0_attn_setup():
        import jax, jax.numpy as jnp
        import numpy as np
        D_MODEL = 256
        D_STATE = 16
        D_CONV = 4
        EXPAND = 2
        D_INNER = D_MODEL * EXPAND

        def _forward(x, W_in, conv_w, conv_b, W_x, A_log, D_param, W_dt, b_dt, W_out):
            B, L, _ = x.shape
            xz = x @ W_in.T
            x_ssm, z = jnp.split(xz, 2, axis=-1)
            xc = jnp.transpose(x_ssm, (0, 2, 1))
            xc = jax.lax.conv_general_dilated(xc, conv_w, window_strides=(1,), padding=[(D_CONV - 1, 0)], feature_group_count=D_INNER, dimension_numbers=('NCH', 'OIH', 'NCH'))
            xc = xc + conv_b[None, :, None]
            x_ssm = jax.nn.silu(jnp.transpose(xc, (0, 2, 1)))
            proj = x_ssm @ W_x.T
            B_ssm = proj[..., :D_STATE]
            C_ssm = proj[..., D_STATE:2 * D_STATE]
            dt = jax.nn.softplus(proj[..., -1:] * W_dt[:, 0] + b_dt)
            A = -jnp.exp(A_log)

            def step(h, inp):
                dt_t, Bt, Ct, xt = inp
                dA = jnp.exp(dt_t[..., None] * A)
                h = dA * h + (xt * dt_t)[..., None] * Bt[:, None, :]
                y = jnp.einsum('bdn,bn->bd', h, Ct)
                return (h, y)
            h0 = jnp.zeros((B, D_INNER, D_STATE), x.dtype)
            inputs = (jnp.transpose(dt, (1, 0, 2)), jnp.transpose(B_ssm, (1, 0, 2)), jnp.transpose(C_ssm, (1, 0, 2)), jnp.transpose(x_ssm, (1, 0, 2)))
            _, ys = jax.lax.scan(step, h0, inputs)
            y = jnp.transpose(ys, (1, 0, 2)) + x_ssm * D_param
            y = y * jax.nn.silu(z)
            return y @ W_out.T
        key = jax.random.key(seed)
        ks = jax.random.split(key, 10)
        B, L = (2, 512)
        x = jax.random.normal(ks[0], (B, L, D_MODEL), jnp.float32)
        W_in = jax.random.normal(ks[1], (2 * D_INNER, D_MODEL), jnp.float32) * (1.0 / np.sqrt(D_MODEL))
        conv_w = jax.random.normal(ks[2], (D_INNER, 1, D_CONV), jnp.float32) * (1.0 / np.sqrt(D_CONV))
        conv_b = jax.random.normal(ks[3], (D_INNER,), jnp.float32) * 0.1
        W_x = jax.random.normal(ks[4], (2 * D_STATE + 1, D_INNER), jnp.float32) * (1.0 / np.sqrt(D_INNER))
        A_log = jnp.log(jnp.abs(jax.random.normal(ks[5], (D_INNER, D_STATE), jnp.float32)) + 0.0001)
        D_param = jnp.ones((D_INNER,), jnp.float32)
        W_dt = jax.random.normal(ks[6], (D_INNER, 1), jnp.float32)
        b_dt = jax.random.normal(ks[7], (D_INNER,), jnp.float32) * 0.1
        W_out = jax.random.normal(ks[8], (D_MODEL, D_INNER), jnp.float32) * (1.0 / np.sqrt(D_INNER))
        return {'x': x, 'W_in': W_in, 'conv_w': conv_w, 'conv_b': conv_b, 'W_x': W_x, 'A_log': A_log, 'D_param': D_param, 'W_dt': W_dt, 'b_dt': b_dt, 'W_out': W_out}
    _L0_attn_all = _L0_attn_setup()
    _L0_attn_in = {k: v for k, v in _L0_attn_all.items() if k in ('W_in', 'conv_w', 'conv_b', 'W_x', 'A_log', 'D_param', 'W_dt', 'b_dt', 'W_out')}
    del _L0_attn_all

    def _L0_xattn_setup():
        import jax, jax.numpy as jnp
        import numpy as np
        D_MODEL = 256
        N_HEADS = 16
        HEAD_DIM = D_MODEL // N_HEADS
        key = jax.random.key(seed)
        ks = jax.random.split(key, 10)
        B, S = (2, 512)
        scale_in = 1.0 / np.sqrt(D_MODEL)
        inp = {'inputs_q': jax.random.normal(ks[0], (B, S, D_MODEL), jnp.float32), 'inputs_kv': jax.random.normal(ks[1], (B, S, D_MODEL), jnp.float32), 'Wq': jax.random.normal(ks[2], (D_MODEL, N_HEADS, HEAD_DIM), jnp.float32) * scale_in, 'Wk': jax.random.normal(ks[3], (D_MODEL, N_HEADS, HEAD_DIM), jnp.float32) * scale_in, 'Wv': jax.random.normal(ks[4], (D_MODEL, N_HEADS, HEAD_DIM), jnp.float32) * scale_in, 'bq': jnp.zeros((N_HEADS, HEAD_DIM), jnp.float32), 'bk': jnp.zeros((N_HEADS, HEAD_DIM), jnp.float32), 'bv': jnp.zeros((N_HEADS, HEAD_DIM), jnp.float32), 'Wo': jax.random.normal(ks[5], (N_HEADS, HEAD_DIM, D_MODEL), jnp.float32) * scale_in, 'bo': jnp.zeros((D_MODEL,), jnp.float32)}
        return inp
    _L0_xattn_all = _L0_xattn_setup()
    _L0_xattn_in = {k: v for k, v in _L0_xattn_all.items() if k in ('Wq', 'Wk', 'Wv', 'bq', 'bk', 'bv', 'Wo', 'bo')}
    del _L0_xattn_all

    def _L0_ffn_setup():
        import jax, jax.numpy as jnp
        import numpy as np
        LN_EPS = 1e-05

        def _layernorm(x, g, b):
            m = jnp.mean(x, axis=-1, keepdims=True)
            v = jnp.mean(jnp.square(x - m), axis=-1, keepdims=True)
            return (x - m) * jax.lax.rsqrt(v + LN_EPS) * g + b
        K_TOP = 2
        key = jax.random.key(seed)
        ks = jax.random.split(key, 4)
        B, N, D, E = (8, 512, 256, 4)
        s = 0.02
        return {'x': jax.random.normal(ks[0], (B, N, D), dtype=jnp.float32), 'gate_W': jax.random.normal(ks[1], (D, E), dtype=jnp.float32) * s, 'gate_b': jnp.zeros((E,), jnp.float32), 'W1': jax.random.normal(ks[2], (E, D, D), dtype=jnp.float32) * s, 'b1': jnp.zeros((E, D), jnp.float32), 'g1': jnp.ones((E, D), jnp.float32), 'be1': jnp.zeros((E, D), jnp.float32), 'W2': jax.random.normal(ks[3], (E, D, D), dtype=jnp.float32) * s, 'b2': jnp.zeros((E, D), jnp.float32), 'g2': jnp.ones((E, D), jnp.float32), 'be2': jnp.zeros((E, D), jnp.float32)}
    _L0_ffn_all = _L0_ffn_setup()
    _L0_ffn_in = {k: v for k, v in _L0_ffn_all.items() if k in ('gate_W', 'gate_b', 'W1', 'b1', 'g1', 'be1', 'W2', 'b2', 'g2', 'be2')}
    del _L0_ffn_all
    return {'x': x, 'ctx_1024': ctx_1024, 'L0_attn_W_in': _L0_attn_in['W_in'], 'L0_attn_conv_w': _L0_attn_in['conv_w'], 'L0_attn_conv_b': _L0_attn_in['conv_b'], 'L0_attn_W_x': _L0_attn_in['W_x'], 'L0_attn_A_log': _L0_attn_in['A_log'], 'L0_attn_D_param': _L0_attn_in['D_param'], 'L0_attn_W_dt': _L0_attn_in['W_dt'], 'L0_attn_b_dt': _L0_attn_in['b_dt'], 'L0_attn_W_out': _L0_attn_in['W_out'], 'L0_xattn_Wq': _L0_xattn_in['Wq'], 'L0_xattn_Wk': _L0_xattn_in['Wk'], 'L0_xattn_Wv': _L0_xattn_in['Wv'], 'L0_xattn_bq': _L0_xattn_in['bq'], 'L0_xattn_bk': _L0_xattn_in['bk'], 'L0_xattn_bv': _L0_xattn_in['bv'], 'L0_xattn_Wo': _L0_xattn_in['Wo'], 'L0_xattn_bo': _L0_xattn_in['bo'], 'L0_ffn_gate_W': _L0_ffn_in['gate_W'], 'L0_ffn_gate_b': _L0_ffn_in['gate_b'], 'L0_ffn_W1': _L0_ffn_in['W1'], 'L0_ffn_b1': _L0_ffn_in['b1'], 'L0_ffn_g1': _L0_ffn_in['g1'], 'L0_ffn_be1': _L0_ffn_in['be1'], 'L0_ffn_W2': _L0_ffn_in['W2'], 'L0_ffn_b2': _L0_ffn_in['b2'], 'L0_ffn_g2': _L0_ffn_in['g2'], 'L0_ffn_be2': _L0_ffn_in['be2']}

def reference(x, ctx_1024, L0_attn_W_in, L0_attn_conv_w, L0_attn_conv_b, L0_attn_W_x, L0_attn_A_log, L0_attn_D_param, L0_attn_W_dt, L0_attn_b_dt, L0_attn_W_out, L0_xattn_Wq, L0_xattn_Wk, L0_xattn_Wv, L0_xattn_bq, L0_xattn_bk, L0_xattn_bv, L0_xattn_Wo, L0_xattn_bo, L0_ffn_gate_W, L0_ffn_gate_b, L0_ffn_W1, L0_ffn_b1, L0_ffn_g1, L0_ffn_be1, L0_ffn_W2, L0_ffn_b2, L0_ffn_g2, L0_ffn_be2):
    import jax
    import jax.numpy as jnp

    def _L0_attn_ref(x, W_in, conv_w, conv_b, W_x, A_log, D_param, W_dt, b_dt, W_out):
        import jax, jax.numpy as jnp
        import numpy as np
        D_MODEL = 256
        D_STATE = 16
        D_CONV = 4
        EXPAND = 2
        D_INNER = D_MODEL * EXPAND

        def _forward(x, W_in, conv_w, conv_b, W_x, A_log, D_param, W_dt, b_dt, W_out):
            B, L, _ = x.shape
            xz = x @ W_in.T
            x_ssm, z = jnp.split(xz, 2, axis=-1)
            xc = jnp.transpose(x_ssm, (0, 2, 1))
            xc = jax.lax.conv_general_dilated(xc, conv_w, window_strides=(1,), padding=[(D_CONV - 1, 0)], feature_group_count=D_INNER, dimension_numbers=('NCH', 'OIH', 'NCH'))
            xc = xc + conv_b[None, :, None]
            x_ssm = jax.nn.silu(jnp.transpose(xc, (0, 2, 1)))
            proj = x_ssm @ W_x.T
            B_ssm = proj[..., :D_STATE]
            C_ssm = proj[..., D_STATE:2 * D_STATE]
            dt = jax.nn.softplus(proj[..., -1:] * W_dt[:, 0] + b_dt)
            A = -jnp.exp(A_log)

            def step(h, inp):
                dt_t, Bt, Ct, xt = inp
                dA = jnp.exp(dt_t[..., None] * A)
                h = dA * h + (xt * dt_t)[..., None] * Bt[:, None, :]
                y = jnp.einsum('bdn,bn->bd', h, Ct)
                return (h, y)
            h0 = jnp.zeros((B, D_INNER, D_STATE), x.dtype)
            inputs = (jnp.transpose(dt, (1, 0, 2)), jnp.transpose(B_ssm, (1, 0, 2)), jnp.transpose(C_ssm, (1, 0, 2)), jnp.transpose(x_ssm, (1, 0, 2)))
            _, ys = jax.lax.scan(step, h0, inputs)
            y = jnp.transpose(ys, (1, 0, 2)) + x_ssm * D_param
            y = y * jax.nn.silu(z)
            return y @ W_out.T
        return _forward(x, W_in, conv_w, conv_b, W_x, A_log, D_param, W_dt, b_dt, W_out)

    def _L0_xattn_ref(inputs_q, inputs_kv, Wq, Wk, Wv, bq, bk, bv, Wo, bo):
        import jax, jax.numpy as jnp
        import numpy as np
        D_MODEL = 256
        N_HEADS = 16
        HEAD_DIM = D_MODEL // N_HEADS
        q = jnp.einsum('bsd,dhf->bshf', inputs_q, Wq) + bq
        k = jnp.einsum('bsd,dhf->bshf', inputs_kv, Wk) + bk
        v = jnp.einsum('bsd,dhf->bshf', inputs_kv, Wv) + bv
        q = q / jnp.sqrt(jnp.asarray(HEAD_DIM, q.dtype))
        attn = jnp.einsum('bqhf,bkhf->bhqk', q, k)
        attn = jax.nn.softmax(attn, axis=-1)
        ctx = jnp.einsum('bhqk,bkhf->bqhf', attn, v)
        out = jnp.einsum('bqhf,hfd->bqd', ctx, Wo) + bo
        return out

    def _L0_ffn_ref(x, gate_W, gate_b, W1, b1, g1, be1, W2, b2, g2, be2):
        import jax, jax.numpy as jnp
        import numpy as np
        LN_EPS = 1e-05

        def _layernorm(x, g, b):
            m = jnp.mean(x, axis=-1, keepdims=True)
            v = jnp.mean(jnp.square(x - m), axis=-1, keepdims=True)
            return (x - m) * jax.lax.rsqrt(v + LN_EPS) * g + b
        K_TOP = 2
        B, N, D = x.shape
        BN = B * N
        xf = x.reshape(BN, D)
        gate_scores = xf @ gate_W + gate_b
        topk_scores, topk_idx = jax.lax.top_k(gate_scores, K_TOP)
        weights = jax.nn.softmax(topk_scores, axis=-1)

        def expert(w1, bb1, gg1, bbe1, w2, bb2, gg2, bbe2):
            h = jax.nn.relu(_layernorm(xf @ w1 + bb1, gg1, bbe1))
            return _layernorm(h @ w2 + bb2, gg2, bbe2)
        all_out = jax.vmap(expert)(W1, b1, g1, be1, W2, b2, g2, be2)
        exp_out = all_out[topk_idx, jnp.arange(BN)[:, None]]
        out = jnp.sum(weights[..., None] * exp_out, axis=1)
        return (out + xf).reshape(B, N, D)
    x = _layernorm(x + _L0_attn_ref(x, L0_attn_W_in, L0_attn_conv_w, L0_attn_conv_b, L0_attn_W_x, L0_attn_A_log, L0_attn_D_param, L0_attn_W_dt, L0_attn_b_dt, L0_attn_W_out), axis=-1)
    x = _layernorm(x + _L0_xattn_ref(x, ctx_1024, L0_xattn_Wq, L0_xattn_Wk, L0_xattn_Wv, L0_xattn_bq, L0_xattn_bk, L0_xattn_bv, L0_xattn_Wo, L0_xattn_bo), axis=-1)
    x = _layernorm(x + _L0_ffn_ref(x, L0_ffn_gate_W, L0_ffn_gate_b, L0_ffn_W1, L0_ffn_b1, L0_ffn_g1, L0_ffn_be1, L0_ffn_W2, L0_ffn_b2, L0_ffn_g2, L0_ffn_be2), axis=-1)
    return x

_drawn_inputs = setup_inputs


def setup_inputs(seed=0):
    import zlib

    import numpy as np

    out = dict(_drawn_inputs(seed))
    spreads = {'L0_attn_D_param': (1.0, 0.2),
     'L0_xattn_bq': (0.0, 0.1),
     'L0_xattn_bk': (0.0, 0.1),
     'L0_xattn_bv': (0.0, 0.1),
     'L0_xattn_bo': (0.0, 0.1),
     'L0_ffn_gate_b': (0.0, 0.1),
     'L0_ffn_b1': (0.0, 0.1),
     'L0_ffn_g1': (1.0, 0.2),
     'L0_ffn_be1': (0.0, 0.1),
     'L0_ffn_b2': (0.0, 0.1),
     'L0_ffn_g2': (1.0, 0.2),
     'L0_ffn_be2': (0.0, 0.1)}
    factors = {}
    for name, (base, spread) in spreads.items():
        noise = np.random.default_rng([zlib.crc32(name.encode()), seed]).standard_normal(out[name].shape)
        drawn = base * np.exp(spread * noise) if base else spread * noise
        out[name] = jnp.asarray(drawn.astype(out[name].dtype))
    for name, factor in factors.items():
        out[name] = (out[name] * factor).astype(out[name].dtype)
    return out
```

```python
import concourse.bass as bass
from concourse import mybir
from contextlib import ExitStack
import numpy as np

F32 = mybir.dt.float32
BF16 = mybir.dt.bfloat16
ALU = mybir.AluOpType
ACT = mybir.ActivationFunctionType
AX = mybir.AxisListType

P = 128
BATCH, L, DM = 4, 1024, 256
DI, NS, TAPS = 512, 16, 4
CT = DI // P
KT = DM // P
HALF = 512
TT = L // P
PARTS = 3
BC = 2 * NS
PROJ = PARTS * BC + 1
LN_EPS = 1e-5

PAR = {"A_log": (0, NS), "conv_w": (64, TAPS), "conv_b": (80, 1), "D": (84, 1), "W_dt": (88, 1), "b_dt": (92, 1)}
PAR_COLS = 96
NL = L // HALF
NH, HD, S = 16, 16, 154
BLK = 32
HG = P // BLK
G = NH // HG
SM = P
SR = S - SM
E = 4
TG = 4


def mamba_block(nc, x, xT, w_in, w_x, w_out, par, ident, sel_bc, sel_p, c_dram, x1):
    STEPS = CT * NS
    RB, RA, RH, RC = 3, 3, 3, 3
    EVAC = 2

    with ExitStack() as ctx:
        def sb(name, shape, dt=F32):
            return ctx.enter_context(nc.sbuf_tensor(name, shape, dt))

        def sem(name):
            return ctx.enter_context(nc.semaphore(name))

        w_in_sb = sb("w_in_sb", [P, KT, 2 * DI])
        w_x_sb = sb("w_x_sb", [P, CT, PROJ])
        w_out_sb = sb("w_out_sb", [P, CT, DM])
        par_sb = sb("par_sb", [P, PAR_COLS])
        negA = sb("negA", [P, CT * NS])
        ident_sb = sb("ident_sb", [P, P])
        sel_bc_sb = sb("sel_bc_sb", [PARTS * BC, NS, P], BF16)
        sel_p_sb = sb("sel_p_sb", [PROJ, P])
        xT_sb = sb("xT_sb", [P, KT, L])
        xs = sb("xs", [P, CT, L])
        gate = sb("gate", [P, CT, L])
        dt_sb = sb("dt_sb", [P, CT, L])
        u_sb = sb("u_sb", [P, CT, L])
        c_bc = sb("c_bc", [P, NS, L])
        decay = sb("decay", [P, RA, L])
        state = sb("state", [P, RH, L])
        state_c = sb("state_c", [P, RC, L])
        tmp = state_c
        step_bc = state[:, 0, :]
        rest = state[0:PARTS * BC, 1, :]
        proj = sb("proj", [PROJ, L])
        parts = sb("parts", [PARTS * BC, L], BF16)
        res = sb("res", [P, TT, DM])
        stats = sb("stats", [P, TT, 6])
        mean = sb("mean", [P, TT])
        var = sb("var", [P, TT])
        lnv = sb("lnv", [P, TT])
        rstd = sb("rstd", [P, TT])
        newt = sb("newt", [P, TT])

        pair = [ctx.enter_context(nc.psum_tensor(f"pair{i}", [P, L], F32)) for i in range(RB)]
        y_ps = ctx.enter_context(nc.psum_tensor("y_ps", [P, L], F32))

        def col(name, j, k=0):
            first, per = PAR[name]
            return par_sb[:, first + j * per + k:first + j * per + k + 1]

        s_const = sem("s_const")
        s_xT = sem("s_xT")
        s_res = sem("s_res")
        s_par = sem("s_par")
        s_in = sem("s_in")
        s_conv0 = sem("s_conv0")
        s_conv = sem("s_conv")
        s_tanh = sem("s_tanh")
        s_gated = sem("s_gated")
        s_proj = sem("s_proj")
        s_projc = sem("s_projc")
        s_split = sem("s_split")
        s_stepp = sem("s_stepp")
        s_step = sem("s_step")
        s_sp = sem("s_sp")
        s_dt = sem("s_dt")
        s_u = sem("s_u")
        s_cst = sem("s_cst")
        s_cb = [sem(f"s_cb{q}") for q in range(4)]
        s_b = sem("s_b")
        s_decay = sem("s_decay")
        s_bu = sem("s_bu")
        s_scan = sem("s_scan")
        s_sc = sem("s_sc")
        s_sum = sem("s_sum")
        s_yfree = sem("s_yfree")
        s_y = sem("s_y")
        s_out = sem("s_out")
        s_r = sem("s_r")
        s_st = sem("s_st")
        s_mv = sem("s_mv")
        s_nw = sem("s_nw")
        s_ln = sem("s_ln")
        s_norm = sem("s_norm")
        s_x1 = sem("s_x1")

        block = ctx.enter_context(nc.Block())

        @block.sync
        def _(sp):
            sp.dma_start(w_in_sb[:, :, :], w_in.rearrange("(k p) n -> p k n", p=P)).then_inc(s_const, 16)
            sp.dma_start(par_sb[:, :], par).then_inc(s_const, 16)
            sp.dma_start(w_x_sb[:, :, :], w_x.rearrange("(k p) n -> p k n", p=P)).then_inc(s_const, 16)
            sp.dma_start(sel_bc_sb[:, :, :], sel_bc.bitcast(BF16)).then_inc(s_const, 16)
            sp.dma_start(sel_p_sb[:, :], sel_p).then_inc(s_const, 16)
            sp.dma_start(ident_sb[:, :], ident).then_inc(s_const, 16)
            sp.dma_start(w_out_sb[:, :, :], w_out.rearrange("(k p) n -> p k n", p=P)).then_inc(s_const, 16)

            def load_xT(b):
                sp.dma_start(xT_sb[:, :, :], xT[:, bass.ds(b * L, L)].rearrange("(k p) n -> p k n", p=P)).then_inc(s_xT, 16)

            def load_res(b):
                sp.dma_start(res[:, :, :], x[bass.ds(b * L, L), :].rearrange("(t p) n -> p t n", p=P)).then_inc(s_res, 16)

            def c_and_x1(b, more):
                sp.wait_ge(s_projc, b * 2 + 1)
                sp.dma_start(c_dram[bass.ds(b * NS, NS), :], proj[NS:BC, :]).then_inc(s_cst, 16)
                sp.wait_ge(s_cst, b * 16 + 16)
                for q in range(4):
                    sp.dma_start(c_bc[:, 4 * q:4 * q + 4, :],
                                 c_dram[bass.ds(b * NS + 4 * q, 4), :].partition_broadcast(P)).then_inc(s_cb[q], 16)
                if more:
                    sp.wait_ge(s_in, b * 2 * CT + 2 * CT)
                    load_xT(b + 1)
                sp.wait_ge(s_norm, b * TT + TT)
                sp.dma_start(x1[bass.ds(b * L, L), :].rearrange("(t p) n -> p t n", p=P), res[:, :, :]).then_inc(s_x1, 16)
                if more:
                    sp.wait_ge(s_x1, b * 16 + 16)
                    load_res(b + 1)

            load_xT(0)
            load_res(0)
            with sp.Fori(0, BATCH - 1) as b:
                c_and_x1(b, True)
            c_and_x1(BATCH - 1, False)
            sp.wait_ge(s_x1, BATCH * 16)

        @block.tensor
        def _(pe):
            pe.wait_ge(s_const, 7 * 16)
            with pe.Fori(0, BATCH) as b:
                def pair_read(i):
                    if i < CT:
                        pe.wait_ge(s_conv, b * 3 * CT + 3 * i + 3)
                    else:
                        pe.wait_ge(s_gated, b * 2 * CT + i + 1)

                pe.wait_ge(s_xT, b * 16 + 16)
                for i in range(2 * CT):
                    if i >= RB:
                        pair_read(i - RB)
                    for h in range(2):
                        for k in range(KT):
                            last = nc.tensor.matmul(pair[i % RB][:, h * HALF:(h + 1) * HALF],
                                                    w_in_sb[:, k, i * P:(i + 1) * P],
                                                    xT_sb[:, k, h * HALF:(h + 1) * HALF],
                                                    start=k == 0, stop=k == KT - 1)
                    last.then_inc(s_in, 1)
                pe.wait_ge(s_gated, b * 2 * CT + CT)
                pair_read(5)
                for h in range(2):
                    for k in range(CT):
                        last = nc.tensor.matmul(pair[2][0:PROJ, h * HALF:(h + 1) * HALF], w_x_sb[:, k, :],
                                                xs[:, k, h * HALF:(h + 1) * HALF], start=k == 0, stop=k == CT - 1)
                last.then_inc(s_proj, 1)
                pe.wait_ge(s_projc, b * 2 + 1)
                pair_read(7)
                for h in range(2):
                    last = nc.tensor.matmul(pair[1][:, h * HALF:(h + 1) * HALF], sel_p_sb[:, :],
                                            proj[:, h * HALF:(h + 1) * HALF], start=True, stop=True)
                last.then_inc(s_stepp, 1)

                def b_rows(s):
                    for h in range(2):
                        last = nc.tensor.matmul(pair[s % RB][:, h * HALF:(h + 1) * HALF], sel_bc_sb[:, s % NS, :],
                                                parts[:, h * HALF:(h + 1) * HALF], start=True, stop=True)
                    last.then_inc(s_b, 1)

                pe.wait_ge(s_split, b * 5 + 5)
                b_rows(0)
                pe.wait_ge(s_step, b + 1)
                b_rows(1)
                b_rows(2)
                for s in range(STEPS):
                    if s + RB < STEPS:
                        pe.wait_ge(s_scan, b * STEPS + s + 1)
                        b_rows(s + RB)
                    if s and s % NS == 0:
                        pe.wait_ge(s_yfree, b * CT + s // NS)
                    pe.wait_ge(s_sc, b * STEPS + s + 1)
                    for h in range(2):
                        last = nc.tensor.matmul(y_ps[:, h * HALF:(h + 1) * HALF], ident_sb[:, :],
                                                state_c[:, s % RC, h * HALF:(h + 1) * HALF],
                                                start=s % NS == 0, stop=s % NS == NS - 1)
                    last.then_inc(s_sum, 1)
                pe.wait_ge(s_y, b * CT + CT)
                for t in range(TT):
                    if t >= RB:
                        pe.wait_ge(s_r, b * TT + t - RB + 1)
                    for k in range(CT):
                        last = nc.tensor.matmul(pair[t % RB][:, 0:DM], xs[:, k, t * P:(t + 1) * P],
                                                w_out_sb[:, k, :], start=k == 0, stop=k == CT - 1)
                    last.then_inc(s_out, 1)
                pe.wait_ge(s_r, b * TT + TT)

        @block.scalar
        def _(act):
            act.wait_ge(s_const, 7 * 16)
            nc.scalar.activation(negA[:, :], par_sb[:, 0:CT * NS], ACT.Exp).then_inc(s_par, 1)
            act.wait_ge(s_par, 3)
            with act.Fori(0, BATCH) as b:
                def first_tap(j):
                    act.wait_ge(s_in, b * 2 * CT + j + 1)
                    nc.scalar.activation(xs[:, j, :], pair[j % RB][:, :], ACT.Identity,
                                         scale=col("conv_w", j, TAPS - 1), bias=col("conv_b", j)).then_inc(s_conv0, 1)

                def tanh_x(j):
                    act.wait_ge(s_conv, b * 3 * CT + 3 * j + 3)
                    if j >= 2:
                        act.wait_ge(s_gated, b * 2 * CT + j - 1)
                    nc.scalar.activation(tmp[:, j % 2, :], xs[:, j, :], ACT.Tanh).then_inc(s_tanh, 1)

                first_tap(0)
                for j in range(CT):
                    if j + 1 < CT:
                        first_tap(j + 1)
                    tanh_x(j)
                for j in range(CT):
                    act.wait_ge(s_in, b * 2 * CT + CT + j + 1)
                    act.wait_ge(s_gated, b * 2 * CT + CT + j - 1)
                    nc.scalar.activation(tmp[:, j % 2, :], pair[(CT + j) % RB][:, :], ACT.Tanh,
                                         scale=0.5).then_inc(s_tanh, 1)
                act.wait_ge(s_proj, b + 1)
                nc.scalar.activation(proj[:, :], pair[2][0:PROJ, :], ACT.Copy).then_inc(s_projc, 1)
                nc.scalar.activation(parts[:, :], pair[2][0:PARTS * BC, :], ACT.Copy).then_inc(s_projc, 1)
                act.wait_ge(s_stepp, b + 1)
                nc.scalar.activation(step_bc, pair[1][:, :], ACT.Copy).then_inc(s_step, 1)
                nc.scalar.preload_act_table_set("natural_log_exp_and_others")
                act.wait_ge(s_step, b + 1)
                act.wait_ge(s_gated, b * 2 * CT + 2 * CT)
                for j in range(CT):
                    first = b * 3 * CT + 3 * j
                    nc.scalar.activation(dt_sb[:, j, :], step_bc, ACT.Abs,
                                         scale=col("W_dt", j), bias=col("b_dt", j)).then_inc(s_sp, 1)
                    if j >= 2:
                        act.wait_ge(s_dt, b * CT + j - 1)
                    nc.scalar.activation(tmp[:, j % 2, :], step_bc, ACT.Relu,
                                         scale=col("W_dt", j), bias=col("b_dt", j))
                    act.wait_ge(s_sp, first + 1)
                    nc.scalar.activation(dt_sb[:, j, :], dt_sb[:, j, :], ACT.Exp, scale=-1.0).then_inc(s_sp, 1)
                    act.wait_ge(s_sp, first + 2)
                    nc.scalar.activation(dt_sb[:, j, :], dt_sb[:, j, :], ACT.Ln, bias=1.0).then_inc(s_sp, 1)
                for s in range(STEPS):
                    if s % NS == 0:
                        act.wait_ge(s_dt, b * CT + s // NS + 1)
                    if s >= RA:
                        act.wait_ge(s_scan, b * STEPS + s - RA + 1)
                    nc.scalar.activation(decay[:, s % RA, :], dt_sb[:, s // NS, :], ACT.Exp,
                                         scale=negA[:, s:s + 1]).then_inc(s_decay, 1)
                act.wait_ge(s_nw, b * 5 + 1)
                nc.scalar.activation(lnv[:, :], var[:, :], ACT.Ln).then_inc(s_ln, 1)
                act.wait_ge(s_ln, b * 2 + 1)
                nc.scalar.activation(rstd[:, :], lnv[:, :], ACT.Exp, scale=-0.5).then_inc(s_ln, 1)

        @block.gpsimd
        def _(pool):
            with pool.Fori(0, BATCH) as b:
                for j in range(CT):
                    pool.wait_ge(s_sp, b * 3 * CT + 3 * j + 3)
                    nc.gpsimd.tensor_tensor(dt_sb[:, j, :], dt_sb[:, j, :], tmp[:, j % 2, :], ALU.add).then_inc(s_dt, 1)
                    pool.wait_ge(s_dt, b * CT + j + 1)
                    nc.gpsimd.tensor_tensor(u_sb[:, j, :], dt_sb[:, j, :], xs[:, j, :], ALU.mult).then_inc(s_u, 1)
                for s in range(STEPS):
                    if s < NS and s % 4 == 0:
                        pool.wait_ge(s_cb[s // 4], b * 16 + 16)
                    pool.wait_ge(s_scan, b * STEPS + s + 1)
                    if s >= RC:
                        pool.wait_ge(s_sum, b * STEPS + s - RC + 1)
                    nc.gpsimd.tensor_tensor(state_c[:, s % RC, :], state[:, s % RH, :], c_bc[:, s % NS, :],
                                            ALU.mult).then_inc(s_sc, 1)

        @block.vector
        def _(dve):
            dve.wait_ge(s_par, 1)
            nc.vector.tensor_scalar(negA[:, :], negA[:, :], -1.0, None, ALU.mult).then_inc(s_par, 1)
            nc.vector.tensor_scalar(par_sb[:, 64:84], par_sb[:, 64:84], 0.5, None, ALU.mult).then_inc(s_par, 1)
            dve.wait_ge(s_par, 3)
            with dve.Fori(0, BATCH) as b:
                def taps(j):
                    dve.wait_ge(s_conv0, b * CT + j + 1)
                    for n, k in enumerate((1, 2, 3)):
                        if n:
                            dve.wait_ge(s_conv, b * 3 * CT + 3 * j + n)
                        last = nc.vector.scalar_tensor_tensor(
                            out=xs[:, j, k:L], in0=pair[j % RB][:, 0:L - k], scalar=col("conv_w", j, TAPS - 1 - k),
                            in1=xs[:, j, k:L], op0=ALU.mult, op1=ALU.add)
                        last.then_inc(s_conv, 1)

                def silu_x(j):
                    dve.wait_ge(s_tanh, b * 2 * CT + j + 1)
                    nc.vector.scalar_tensor_tensor(out=xs[:, j, :], in0=tmp[:, j % 2, :], scalar=1.0,
                                                   in1=xs[:, j, :], op0=ALU.add, op1=ALU.mult).then_inc(s_gated, 1)

                taps(0)
                for j in range(CT):
                    if j + 1 < CT:
                        taps(j + 1)
                    silu_x(j)
                for j in range(CT):
                    dve.wait_ge(s_tanh, b * 2 * CT + CT + j + 1)
                    nc.vector.scalar_tensor_tensor(out=gate[:, j, :], in0=tmp[:, j % 2, :], scalar=1.0,
                                                   in1=pair[(CT + j) % RB][:, :], op0=ALU.add,
                                                   op1=ALU.mult).then_inc(s_gated, 1)
                dve.wait_ge(s_projc, b * 2 + 2)
                nc.vector.tensor_tensor(rest, proj[0:PARTS * BC, :], parts[:, :], ALU.subtract).then_inc(s_split, 1)
                dve.wait_ge(s_split, b * 5 + 1)
                nc.vector.tensor_copy(parts[BC:2 * BC, :], state[BC:2 * BC, 1, :]).then_inc(s_split, 1)
                nc.vector.tensor_copy(parts[2 * BC:3 * BC, :], state[2 * BC:3 * BC, 1, :]).then_inc(s_split, 1)
                dve.wait_ge(s_split, b * 5 + 3)
                nc.vector.tensor_tensor(state[2 * BC:3 * BC, 1, :], state[2 * BC:3 * BC, 1, :],
                                        parts[2 * BC:3 * BC, :], ALU.subtract).then_inc(s_split, 1)
                dve.wait_ge(s_split, b * 5 + 4)
                nc.vector.tensor_copy(parts[2 * BC:3 * BC, :], state[2 * BC:3 * BC, 1, :]).then_inc(s_split, 1)

                def take_y(j):
                    dve.wait_ge(s_sum, b * STEPS + NS * (j + 1))
                    nc.vector.scalar_tensor_tensor(out=xs[:, j, :], in0=xs[:, j, :], scalar=col("D", j),
                                                   in1=y_ps[:, :], op0=ALU.mult, op1=ALU.add).then_inc(s_yfree, 1)
                    dve.wait_ge(s_yfree, b * CT + j + 1)
                    nc.vector.scalar_tensor_tensor(out=xs[:, j, :], in0=xs[:, j, :], scalar=0.5,
                                                   in1=gate[:, j, :], op0=ALU.mult, op1=ALU.mult).then_inc(s_y, 1)

                for s in range(STEPS):
                    j, now = s // NS, b * STEPS + s
                    if s % NS == 0:
                        dve.wait_ge(s_u, b * CT + j + 1)
                    if s % NS == EVAC and j:
                        take_y(j - 1)
                    dve.wait_ge(s_b, now + 1)
                    nc.vector.tensor_tensor(pair[s % RB][:, :], u_sb[:, j, :], pair[s % RB][:, :],
                                            ALU.mult).then_inc(s_bu, 1)
                    dve.wait_ge(s_decay, now + 1)
                    if s >= RH:
                        dve.wait_ge(s_sc, now - RH + 1)
                    dve.wait_ge(s_bu, now + 1)
                    nc.vector.tensor_tensor_scan(state[:, s % RH, :], decay[:, s % RA, :], pair[s % RB][:, :],
                                                 0.0, ALU.mult, ALU.add).then_inc(s_scan, 1)
                take_y(CT - 1)
                dve.wait_ge(s_res, b * 16 + 16)
                for t in range(TT):
                    dve.wait_ge(s_out, b * TT + t + 1)
                    nc.vector.tensor_tensor(res[:, t, :], res[:, t, :], pair[t % RB][:, 0:DM], ALU.add).then_inc(s_r, 1)
                    dve.wait_ge(s_r, b * TT + t + 1)
                    nc.vector.bn_stats(stats[:, t, :], res[:, t, :]).then_inc(s_st, 1)
                dve.wait_ge(s_st, b * TT + TT)
                nc.vector.tensor_tensor(mean[:, :], stats[:, :, 1], stats[:, :, 4], ALU.add).then_inc(s_mv, 1)
                nc.vector.tensor_tensor(newt[:, :], stats[:, :, 1], stats[:, :, 4], ALU.subtract).then_inc(s_mv, 1)
                nc.vector.tensor_tensor(var[:, :], stats[:, :, 2], stats[:, :, 5], ALU.add).then_inc(s_mv, 1)
                dve.wait_ge(s_mv, b * 6 + 2)
                nc.vector.tensor_tensor(newt[:, :], newt[:, :], newt[:, :], ALU.mult).then_inc(s_mv, 1)
                dve.wait_ge(s_mv, b * 6 + 3)
                nc.vector.tensor_scalar(var[:, :], var[:, :], 1.0 / DM, LN_EPS, ALU.mult, ALU.add).then_inc(s_mv, 1)
                nc.vector.tensor_scalar(mean[:, :], mean[:, :], 0.5, None, ALU.mult).then_inc(s_mv, 1)
                dve.wait_ge(s_mv, b * 6 + 5)
                nc.vector.scalar_tensor_tensor(out=var[:, :], in0=newt[:, :], scalar=0.25, in1=var[:, :],
                                               op0=ALU.mult, op1=ALU.add).then_inc(s_nw, 1)
                dve.wait_ge(s_ln, b * 2 + 2)
                nc.vector.tensor_tensor(newt[:, :], rstd[:, :], rstd[:, :], ALU.mult).then_inc(s_nw, 1)
                dve.wait_ge(s_nw, b * 5 + 2)
                nc.vector.tensor_tensor(newt[:, :], newt[:, :], var[:, :], ALU.mult).then_inc(s_nw, 1)
                dve.wait_ge(s_nw, b * 5 + 3)
                nc.vector.tensor_scalar(newt[:, :], newt[:, :], -0.5, 1.5, ALU.mult, ALU.add).then_inc(s_nw, 1)
                dve.wait_ge(s_nw, b * 5 + 4)
                nc.vector.tensor_tensor(rstd[:, :], rstd[:, :], newt[:, :], ALU.mult).then_inc(s_nw, 1)
                dve.wait_ge(s_nw, b * 5 + 5)
                for t in range(TT):
                    nc.vector.tensor_scalar(res[:, t, :], res[:, t, :], mean[:, t:t + 1], rstd[:, t:t + 1],
                                            ALU.subtract, ALU.mult).then_inc(s_norm, 1)


def attn_ffn_block(nc, x1, ctxT, wq, wk, wv, wo, bqk, bv, ident, swap, w1, w2, gw, gb, lnp, bias_rows,
                   ones3, g2, be2, before, out):
    U = G * NL
    NT = TT // TG

    with ExitStack() as ctx:
        def sb(name, shape, dt=F32):
            return ctx.enter_context(nc.sbuf_tensor(name, shape, dt))

        def sem(name):
            return ctx.enter_context(nc.semaphore(name))

        wq_sb = sb("wq_sb", [P, KT, G * P])
        wk_sb = sb("wk_sb", [P, KT, G * P])
        wv_sb = sb("wv_sb", [P, KT, G * P])
        wo_sb = sb("wo_sb", [P, G, DM])
        bqk_sb = sb("bqk_sb", [P, 2 * G])
        bv_sb = sb("bv_sb", [P, G * P])
        ident_sb = sb("ident2_sb", [P, P])
        swap_sb = sb("swap_sb", [P, P])
        w1_sb = sb("w1_sb", [P, KT, E * DM])
        w2_sb = sb("w2_sb", [P, E * KT, DM])
        gw_sb = sb("gw_sb", [P, KT, E])
        gb_sb = sb("gb_sb", [P, E])
        lnp_sb = sb("lnp_sb", [P, 2 * E * KT])
        g2_sb = sb("g2_sb", [P, E * DM])
        be2_sb = sb("be2_sb", [P, E * DM])
        before_sb = sb("before_sb", [P, E * E])
        ones3_sb = sb("ones3_sb", [3 * BLK, P], BF16)
        brow = sb("brow", [3 * BLK, 2 * E * DM], BF16)
        xt = sb("xt", [P, TT, DM])
        xT = sb("xT2_sb", [P, KT, L])
        ctx_sb = sb("ctx_sb", [P, KT, S])
        qT = sb("qT", [P, G, L])
        kTm = sb("kTm", [P, NH, S])
        kTr = sb("kTr", [P, G, P])
        v_sb = sb("v_sb", [P, NH, BLK])
        v_rem = sb("v_rem", [P, G, P])
        big = sb("big", [P, 2, TG, E * DM])
        neg = big[:, 0, :, :].rearrange("p a (t c) -> p (a t) c", c=P)
        pT = big[:, 1, :, :].rearrange("p a (c n) -> p (a c) n", n=HALF)
        pT_rem = sb("pT_rem", [P, 2, HALF])
        oT = sb("oT", [P, G, L])
        hT = sb("hT", [P, E * KT, HALF])
        raw = sb("raw", [P, 2, HALF])
        lnd = sb("lnd", [P, 2, HALF])
        stats = sb("stats2", [P, TG * E, 6])
        mean = sb("mean2", [P, TG * E])
        var = sb("var2", [P, TG * E])
        lnv = sb("lnv2", [P, TG * E])
        rstd = sb("rstd2", [P, TG * E])
        newt = sb("newt2", [P, TG * E])
        sc = sb("sc", [P, TT, E])
        smax = sb("smax", [P, TT])
        cmp1 = sb("cmp1", [P, TT, E, E])
        cmp2 = sb("cmp2", [P, TT, E, E])
        rank = sb("rank", [P, TT, E])
        wgt = sb("wgt", [P, TT, E])
        wsum = sb("wsum", [P, TT])
        acc = sb("acc", [P, TT, DM])
        scale2 = sb("scale2", [P, TG * E])

        ps = ctx.enter_context(nc.psum_tensor("ps", [P, 8, HALF], F32))

        s_const = sem("a_const")
        s_prep = sem("a_prep")
        s_split = sem("a_split")
        s_brow = sem("a_brow")
        s_x = sem("a_x")
        s_ctx = sem("a_ctx")
        s_tr = sem("a_tr")
        s_trc = sem("a_trc")
        s_kv = sem("a_kv")
        s_kvc = sem("a_kvc")
        s_q = sem("a_q")
        s_qc = sem("a_qc")
        s_s1 = sem("a_s1")
        s_max = sem("a_max")
        s_mt = sem("a_mt")
        s_qm = sem("a_qm")
        s_s2 = sem("a_s2")
        s_exp = sem("a_exp")
        s_pv = sem("a_pv")
        s_raw = sem("a_raw")
        s_den = sem("a_den")
        s_lnd = sem("a_lnd")
        s_o = sem("a_o")
        s_proj = sem("a_proj")
        s_r = sem("a_r")
        s_st = sem("a_st")
        s_mv = sem("a_mv")
        s_nw = sem("a_nw")
        s_ln = sem("a_ln")
        s_x2 = sem("a_x2")
        s_gate = sem("a_gate")
        s_gd = sem("a_gd")
        s_ge = sem("a_ge")
        s_l1 = sem("a_l1")
        s_l1c = sem("a_l1c")
        s_n1 = sem("a_n1")
        s_h = sem("a_h")
        s_hc = sem("a_hc")
        s_l2 = sem("a_l2")
        s_l2c = sem("a_l2c")
        s_n2 = sem("a_n2")
        s_scale = sem("a_scale")
        s_gm = sem("a_gm")
        s_acc = sem("a_acc")
        s_sum = sem("a_sum")
        s_fin = sem("a_fin")
        s_out = sem("a_out")

        TRB, NWB, LNB = 2 * KT * NL, 5 * (2 + 2 * NT), 2 * (2 + 2 * NT)
        MVB = TT + 2 * TT * E + TT
        NORMS = 2 + 2 * NT
        NMB = 6 * NORMS
        KVB, GDB, ACB = 2 + 3 * HG, 12, TT * (E + 1)

        block = ctx.enter_context(nc.Block())
        LOADS = 17

        @block.sync
        def _(sp):
            def load(dst, src):
                sp.dma_start(dst, src).then_inc(s_const, 16)
            load(ident_sb[:, :], ident)
            load(wk_sb[:, :, :], wk.rearrange("(k p) n -> p k n", p=P))
            load(wv_sb[:, :, :], wv.rearrange("(k p) n -> p k n", p=P))
            load(wq_sb[:, :, :], wq.rearrange("(k p) n -> p k n", p=P))
            load(bqk_sb[:, :], bqk)
            load(bv_sb[:, :], bv.partition_broadcast(P))
            load(wo_sb[:, :, :], wo.rearrange("(g p) n -> p g n", p=P))
            load(swap_sb[:, :], swap)
            load(w1_sb[:, :, :], w1.rearrange("(k p) n -> p k n", p=P))
            load(w2_sb[:, :, :], w2.rearrange("(k p) n -> p k n", p=P))
            load(gw_sb[:, :, :], gw.rearrange("(k p) n -> p k n", p=P))
            load(gb_sb[:, :], gb.partition_broadcast(P))
            load(lnp_sb[:, :], lnp)
            load(g2_sb[:, :], g2.partition_broadcast(P))
            load(be2_sb[:, :], be2.partition_broadcast(P))
            load(before_sb[:, :], before.partition_broadcast(P))
            load(ones3_sb[:, :], ones3.bitcast(BF16))
            sp.dma_start(big[0:3 * BLK, 0, 0:2, :], bias_rows.rearrange("q (a n) -> q a n", a=2)).then_inc(s_brow, 16)

            def load_x1(b):
                sp.dma_start(xt[:, :, :], x1[bass.ds(b * L, L), :].rearrange("(t p) n -> p t n", p=P)).then_inc(s_x, 16)

            def load_ctx(b):
                sp.dma_start(ctx_sb[:, :, :], ctxT[:, bass.ds(b * S, S)].rearrange("(k p) n -> p k n", p=P)).then_inc(s_ctx, 16)

            def store_out(b):
                sp.wait_ge(s_fin, b * TT + TT)
                sp.dma_start(out[bass.ds(b * L, L), :].rearrange("(t p) n -> p t n", p=P), xt[:, :, :]).then_inc(s_out, 16)

            load_ctx(0)
            load_x1(0)
            with sp.Fori(0, BATCH - 1) as b:
                sp.wait_ge(s_kv, b * 3 + 3)
                load_ctx(b + 1)
                store_out(b)
                sp.wait_ge(s_out, b * 16 + 16)
                load_x1(b + 1)
            store_out(BATCH - 1)
            sp.wait_ge(s_out, BATCH * 16)

        @block.tensor
        def _(pe):
            pe.wait_ge(s_const, LOADS * 16)
            pe.wait_ge(s_prep, 4)
            pe.wait_ge(s_split, 6)

            def transposes(first, b):
                for u in range(NL * KT):
                    half, k = u // KT, u % KT
                    for i in range(TG):
                        last = nc.tensor.transpose(ps[:, u, i * P:(i + 1) * P],
                                                   xt[:, half * TG + i, k * P:(k + 1) * P], ident_sb[:, :])
                    last.then_inc(s_tr, 1)

            with pe.Fori(0, BATCH) as b:
                pe.wait_ge(s_ctx, b * 16 + 16)
                for g in range(G):
                    for k in range(KT):
                        last = nc.tensor.matmul(ps[:, 4 + g // 2, (g % 2) * 256:(g % 2) * 256 + S],
                                                wk_sb[:, k, g * P:(g + 1) * P], ctx_sb[:, k, :],
                                                start=k == 0, stop=k == KT - 1)
                last.then_inc(s_kv, 1)
                for k in range(KT):
                    last = nc.tensor.matmul(ps[:, 6, :], ctx_sb[:, k, 0:SM], wv_sb[:, k, :],
                                            start=k == 0, stop=k == KT - 1)
                last.then_inc(s_kv, 1)
                for j in range(HG):
                    for k in range(KT):
                        last = nc.tensor.matmul(
                            ps[BLK * j:BLK * j + SR, 7, 0:P].rearrange("p (g c) -> p g c", c=BLK),
                            ctx_sb[:, k, SM:S],
                            wv_sb[:, k, :].rearrange("p (g j c) -> p g j c", j=HG, c=BLK)[:, :, j, :],
                            start=k == 0, stop=k == KT - 1)
                last.then_inc(s_kv, 1)
                pe.wait_ge(s_x, b * 16 + 16)
                transposes(0, b)
                for u in range(U):
                    g, half = u // NL, u % NL
                    if u < NL * KT:
                        pe.wait_ge(s_trc, b * TRB + NL * KT)
                    else:
                        pe.wait_ge(s_qc, b * U + u - 3)
                    for k in range(KT):
                        last = nc.tensor.matmul(ps[:, u % 4, :], wq_sb[:, k, g * P:(g + 1) * P],
                                                xT[:, k, half * HALF:(half + 1) * HALF],
                                                start=k == 0, stop=k == KT - 1)
                    last.then_inc(s_q, 1)
                pe.wait_ge(s_kvc, b * KVB + KVB)
                pe.wait_ge(s_qc, b * U + U)
                for u in range(TT * G):
                    t, g = u // G, u % G
                    if u >= 4:
                        pe.wait_ge(s_max, b * TT * G + u - 3)
                    for i in range(2):
                        last = nc.tensor.matmul(ps[:, 2 * (u % 4) + i, 0:2 * S], qT[:, g, t * P:(t + 1) * P],
                                                kTm[:, HG * g + 2 * i:HG * g + 2 * i + 2, :], start=True, stop=True)
                    last.then_inc(s_s1, 1)
                pe.wait_ge(s_max, b * TT * G + TT * G)
                for u in range(U):
                    g, half = u // NL, u % NL
                    for i in range(TG):
                        last = nc.tensor.transpose(ps[:, u, i * P:(i + 1) * P], neg[:, (half * TG + i) * G + g, :],
                                                   ident_sb[:, :])
                    last.then_inc(s_mt, 1)

                def scores(u):
                    g, half = u // NL, u % NL
                    q = qT[:, g, half * HALF:(half + 1) * HALF]
                    if u == 0:
                        pe.wait_ge(s_qm, b * U + U)
                    for j in range(HG):
                        if u and j % 2 == 0:
                            pe.wait_ge(s_exp, b * 3 * U + 3 * (u - 1) + j // 2 + 1)
                        last = nc.tensor.matmul(ps[:, j, :], kTm[:, HG * g + j, 0:SM], q, start=True, stop=True)
                        if j % 2:
                            last.then_inc(s_s2, 1)
                    if u:
                        pe.wait_ge(s_exp, b * 3 * U + 3 * u)
                    nc.tensor.matmul(ps[:, 4, :], kTr[:, g, :], q, start=True, stop=True).then_inc(s_s2, 1)

                def values(u):
                    g = u // NL
                    pe.wait_ge(s_exp, b * 3 * U + 3 * u + 3)
                    if u >= 2:
                        pe.wait_ge(s_raw, b * U + u - 1)
                    nc.tensor.matmul(ps[:, 5 + u % 2, :], v_rem[:, g, :], pT_rem[:, u % 2, :],
                                     start=True, stop=False, skip_group_check=True)
                    for j in range(HG):
                        last = nc.tensor.matmul(ps[BLK * j:BLK * (j + 1), 5 + u % 2, :], v_sb[:, HG * g + j, :],
                                                pT[:, HG * (u % 2) + j, :], start=False, stop=True,
                                                skip_group_check=True)
                    last.then_inc(s_pv, 1)

                def sums(u):
                    pe.wait_ge(s_raw, b * U + u + 1)
                    if u:
                        pe.wait_ge(s_lnd, b * 2 * U + 2 * u - 1)
                    nc.tensor.matmul(ps[:, 7, :], swap_sb[:, :], raw[:, u % 2, :], start=True, stop=True).then_inc(s_den, 1)

                for u in range(U + 2):
                    if u < U:
                        scores(u)
                    if 1 <= u <= U:
                        values(u - 1)
                    if u >= 2:
                        sums(u - 2)
                pe.wait_ge(s_o, b * U + U)
                for t in range(TT):
                    if t >= 4:
                        pe.wait_ge(s_r, b * TT + t - 3)
                    for g in range(G):
                        last = nc.tensor.matmul(ps[:, t % 4, 0:DM], oT[:, g, t * P:(t + 1) * P], wo_sb[:, g, :],
                                                start=g == 0, stop=g == G - 1)
                    last.then_inc(s_proj, 1)
                pe.wait_ge(s_x2, b * TT + TT)
                transposes(1, b)
                pe.wait_ge(s_trc, b * TRB + TRB)
                for t in range(TT):
                    for k in range(KT):
                        last = nc.tensor.matmul(ps[:, 7, t * E:(t + 1) * E], xT[:, k, t * P:(t + 1) * P], gw_sb[:, k, :],
                                                start=k == 0, stop=k == KT - 1)
                last.then_inc(s_gate, 1)
                for t in range(TT):
                    if t >= 2:
                        pe.wait_ge(s_l1c, b * TT + t - 1)
                    for h in range(2):
                        dst = ps[:, 2 * (t % 2) + h, :]
                        nc.tensor.matmul(dst, ones3_sb[:, :], brow[:, h * HALF:(h + 1) * HALF], start=True, stop=False)
                        for k in range(KT):
                            last = nc.tensor.matmul(dst, xT[:, k, t * P:(t + 1) * P], w1_sb[:, k, h * HALF:(h + 1) * HALF],
                                                    start=False, stop=k == KT - 1)
                    last.then_inc(s_l1, 1)
                for n in range(NT):
                    pe.wait_ge(s_n1, b * TT + TG * (n + 1))
                    for c in range(E * KT):
                        m = n * E * KT + c
                        if m >= 3:
                            pe.wait_ge(s_hc, b * NT * E * KT + m - 2)
                        for i in range(TG):
                            last = nc.tensor.transpose(ps[:, 4 + m % 3, i * P:(i + 1) * P],
                                                       big[:, n, i, c * P:(c + 1) * P], ident_sb[:, :])
                        last.then_inc(s_h, 1)
                    pe.wait_ge(s_hc, b * NT * E * KT + E * KT * (n + 1))
                    for i in range(TG):
                        t = n * TG + i
                        if t >= 2:
                            pe.wait_ge(s_l2c, b * TT + t - 1)
                        else:
                            pe.wait_ge(s_l1c, b * TT + TT)
                        for e in range(E):
                            dst = ps[:, 2 * (t % 2) + e // 2, (e % 2) * DM:(e % 2 + 1) * DM]
                            if e % 2 == 0:
                                nc.tensor.matmul(ps[:, 2 * (t % 2) + e // 2, :], ones3_sb[:, :],
                                                 brow[:, E * DM + e * DM:E * DM + (e + 2) * DM],
                                                 start=True, stop=False, skip_group_check=True)
                            for k in range(KT):
                                last = nc.tensor.matmul(dst, hT[:, e * KT + k, i * P:(i + 1) * P],
                                                        w2_sb[:, e * KT + k, :], start=False, stop=k == KT - 1,
                                                        skip_group_check=True)
                        last.then_inc(s_l2, 1)
                pe.wait_ge(s_l2c, b * TT + TT)

        @block.scalar
        def _(act):
            act.wait_ge(s_const, LOADS * 16)
            nc.scalar.preload_act_table_set("natural_log_exp_and_others")
            nc.scalar.mul(bqk_sb[:, 0:G], bqk_sb[:, 0:G], HD ** -0.5).then_inc(s_prep, 1)
            act.wait_ge(s_prep, 4)
            with act.Fori(0, BATCH) as b:
                norms = [0]

                def guess():
                    n = norms[0]
                    norms[0] += 1
                    cols = TT if n in (0, NORMS - 1) else TG * E
                    act.wait_ge(s_nw, b * NWB + 5 * n + 1)
                    nc.scalar.activation(lnv[:, 0:cols], var[:, 0:cols], ACT.Ln).then_inc(s_ln, 1)
                    act.wait_ge(s_ln, b * LNB + 2 * n + 1)
                    nc.scalar.activation(rstd[:, 0:cols], lnv[:, 0:cols], ACT.Exp, scale=-0.5).then_inc(s_ln, 1)

                for u in range(U):
                    g, half = u // NL, u % NL
                    act.wait_ge(s_q, b * U + u + 1)
                    nc.scalar.activation(qT[:, g, half * HALF:(half + 1) * HALF], ps[:, u % 4, :], ACT.Identity,
                                         scale=HD ** -0.5, bias=bqk_sb[:, g:g + 1]).then_inc(s_qc, 1)

                def exps(u):
                    if u >= 2:
                        act.wait_ge(s_pv, b * U + u - 1)
                    for i in range(2):
                        act.wait_ge(s_s2, b * 3 * U + 3 * u + i + 1)
                        nc.scalar.activation(pT[:, HG * (u % 2) + 2 * i:HG * (u % 2) + 2 * i + 2, :],
                                             ps[:, 2 * i:2 * i + 2, :], ACT.Exp).then_inc(s_exp, 1)
                    act.wait_ge(s_s2, b * 3 * U + 3 * u + 3)
                    nc.scalar.activation(pT_rem[:, u % 2, :], ps[:, 4, :], ACT.Exp).then_inc(s_exp, 1)

                def inverse(u):
                    act.wait_ge(s_den, b * U + u + 1)
                    if u >= 2:
                        act.wait_ge(s_o, b * U + u - 1)
                    nc.scalar.activation(lnd[:, u % 2, :], ps[:, 7, :], ACT.Ln).then_inc(s_lnd, 1)
                    act.wait_ge(s_lnd, b * 2 * U + 2 * u + 1)
                    nc.scalar.activation(lnd[:, u % 2, :], lnd[:, u % 2, :], ACT.Exp, scale=-1.0).then_inc(s_lnd, 1)

                for u in range(U + 2):
                    if u < U:
                        exps(u)
                    if u >= 2:
                        inverse(u - 2)
                guess()
                act.wait_ge(s_gd, b * GDB + 5)
                nc.scalar.activation(wgt[:, :, :], wgt[:, :, :], ACT.Exp).then_inc(s_ge, 1)
                for t in range(TT):
                    act.wait_ge(s_l1, b * TT + t + 1)
                    nc.scalar.activation(big[:, t // TG, t % TG, :].rearrange("p (a n) -> p a n", a=2),
                                         ps[:, 2 * (t % 2):2 * (t % 2) + 2, :], ACT.Copy).then_inc(s_l1c, 1)
                    if t % TG == TG - 1:
                        guess()
                for n in range(NT):
                    for c in range(E * KT):
                        m = n * E * KT + c
                        act.wait_ge(s_h, b * NT * E * KT + m + 1)
                        if n:
                            act.wait_ge(s_l2, b * TT + TG * n)
                        nc.scalar.activation(hT[:, c, :], ps[:, 4 + m % 3, :], ACT.Relu, scale=lnp_sb[:, c:c + 1],
                                             bias=lnp_sb[:, E * KT + c:E * KT + c + 1]).then_inc(s_hc, 1)
                    for i in range(TG):
                        t = n * TG + i
                        act.wait_ge(s_l2, b * TT + t + 1)
                        nc.scalar.activation(big[:, n, i, :].rearrange("p (a n) -> p a n", a=2),
                                             ps[:, 2 * (t % 2):2 * (t % 2) + 2, :], ACT.Copy).then_inc(s_l2c, 1)
                    guess()
                guess()

        @block.gpsimd
        def _(pool):
            nc.gpsimd.memset(kTm[:, :, :], 0.0).then_inc(s_prep, 1)
            nc.gpsimd.memset(kTr[:, :, :], 0.0).then_inc(s_prep, 1)
            nc.gpsimd.memset(v_rem[:, :, :], 0.0).then_inc(s_prep, 1)
            pool.wait_ge(s_const, LOADS * 16)
            with pool.Fori(0, BATCH) as b:
                for t in range(TT):
                    tile = big[:, t // TG, t % TG, :]
                    pool.wait_ge(s_n2, b * TT + t + 1)
                    nc.gpsimd.tensor_tensor(tile, tile, g2_sb[:, :], ALU.mult).then_inc(s_gm, 1)
                    pool.wait_ge(s_gm, b * TT + t + 1)
                    pool.wait_ge(s_acc, b * ACB + ACB)
                    for e in range(E):
                        nc.gpsimd.tensor_tensor(acc[:, t, :], acc[:, t, :], tile[:, e * DM:(e + 1) * DM],
                                                ALU.add).then_inc(s_sum, 1)
                        pool.wait_ge(s_sum, b * TT * E + E * t + e + 1)

        @block.vector
        def _(dve):
            dve.wait_ge(s_const, LOADS * 16)
            dve.wait_ge(s_brow, 16)
            row = big[0:3 * BLK, 0, 0:2, :].rearrange("p a n -> p (a n)")
            left = big[0:3 * BLK, 0, 2:4, :].rearrange("p a n -> p (a n)")
            nc.vector.tensor_copy(brow[:, :], row).then_inc(s_split, 1)
            dve.wait_ge(s_split, 1)
            nc.vector.tensor_tensor(left, row, brow[:, :], ALU.subtract).then_inc(s_split, 1)
            dve.wait_ge(s_split, 2)
            for q in (1, 2):
                nc.vector.tensor_copy(brow[BLK * q:BLK * q + BLK, :], left[BLK * q:BLK * q + BLK, :]).then_inc(s_split, 1)
            dve.wait_ge(s_split, 4)
            nc.vector.tensor_tensor(left[2 * BLK:3 * BLK, :], left[2 * BLK:3 * BLK, :], brow[2 * BLK:3 * BLK, :],
                                    ALU.subtract).then_inc(s_split, 1)
            dve.wait_ge(s_split, 5)
            nc.vector.tensor_copy(brow[2 * BLK:3 * BLK, :], left[2 * BLK:3 * BLK, :]).then_inc(s_split, 1)
            dve.wait_ge(s_split, 6)
            dve.wait_ge(s_prep, 4)
            with dve.Fori(0, BATCH) as b:
                norms, mvs = [0], [0]

                def newton():
                    n = norms[0]
                    norms[0] += 1
                    cols = TT if n in (0, NORMS - 1) else TG * E
                    at = b * NWB + 5 * n
                    v, r, w = var[:, 0:cols], rstd[:, 0:cols], newt[:, 0:cols]
                    dve.wait_ge(s_ln, b * LNB + 2 * n + 2)
                    nc.vector.tensor_tensor(w, r, r, ALU.mult).then_inc(s_nw, 1)
                    dve.wait_ge(s_nw, at + 2)
                    nc.vector.tensor_tensor(w, w, v, ALU.mult).then_inc(s_nw, 1)
                    dve.wait_ge(s_nw, at + 3)
                    nc.vector.tensor_scalar(w, w, -0.5, 1.5, ALU.mult, ALU.add).then_inc(s_nw, 1)
                    dve.wait_ge(s_nw, at + 4)
                    nc.vector.tensor_tensor(r, r, w, ALU.mult).then_inc(s_nw, 1)
                    dve.wait_ge(s_nw, at + 5)

                def aggregate(count):
                    mvs[0] += count
                    at = b * NMB + 6 * norms[0]
                    m, v, w, st = mean[:, 0:count], var[:, 0:count], newt[:, 0:count], stats[:, 0:count, :]
                    dve.wait_ge(s_st, b * MVB + mvs[0])
                    nc.vector.tensor_tensor(m, st[:, :, 1], st[:, :, 4], ALU.add).then_inc(s_mv, 1)
                    nc.vector.tensor_tensor(w, st[:, :, 1], st[:, :, 4], ALU.subtract).then_inc(s_mv, 1)
                    nc.vector.tensor_tensor(v, st[:, :, 2], st[:, :, 5], ALU.add).then_inc(s_mv, 1)
                    dve.wait_ge(s_mv, at + 2)
                    nc.vector.tensor_tensor(w, w, w, ALU.mult).then_inc(s_mv, 1)
                    dve.wait_ge(s_mv, at + 3)
                    nc.vector.tensor_scalar(v, v, 1.0 / DM, LN_EPS, ALU.mult, ALU.add).then_inc(s_mv, 1)
                    nc.vector.tensor_scalar(m, m, 0.5, None, ALU.mult).then_inc(s_mv, 1)
                    dve.wait_ge(s_mv, at + 5)
                    nc.vector.scalar_tensor_tensor(out=v, in0=w, scalar=0.25, in1=v, op0=ALU.mult,
                                                   op1=ALU.add).then_inc(s_nw, 1)

                def copy_transposed(first):
                    for u in range(NL * KT):
                        half, k = u // KT, u % KT
                        dve.wait_ge(s_tr, b * TRB + first + u + 1)
                        nc.vector.tensor_copy(xT[:, k, half * HALF:(half + 1) * HALF], ps[:, u, :]).then_inc(s_trc, 1)

                nc.vector.memset(neg[:, :, :], 0.0).then_inc(s_kvc, 1)
                dve.wait_ge(s_kv, b * 3 + 3)
                keys = ps[:, 4:6, :].rearrange("p a (g n) -> p (a g) n", n=256)
                for j in range(HG):
                    rows = slice(BLK * j, BLK * (j + 1))
                    heads = kTm[rows, :, :].rearrange("p (g j) n -> p g j n", j=HG)[:, :, j, :]
                    nc.vector.tensor_tensor(heads, keys[rows, :, 0:S],
                                            bqk_sb[rows, G:2 * G].unsqueeze(2).to_broadcast([BLK, G, S]),
                                            ALU.add).then_inc(s_kvc, 1)
                for j in range(HG):
                    rows = slice(BLK * j, BLK * (j + 1))
                    heads = kTm[rows, :, :].rearrange("p (g j) n -> p g j n", j=HG)[:, :, j, :]
                    dve.wait_ge(s_kvc, b * KVB + 2 + j)
                    nc.vector.tensor_copy(kTr[rows, :, BLK * j:BLK * j + SR], heads[:, :, SM:S]).then_inc(s_kvc, 1)
                nc.vector.tensor_tensor(v_sb[:, :, :].rearrange("p h c -> p (h c)"), ps[:, 6, :], bv_sb[:, :],
                                        ALU.add).then_inc(s_kvc, 1)
                for j in range(HG):
                    rows = slice(BLK * j, BLK * j + SR)
                    nc.vector.tensor_tensor(
                        v_rem[rows, :, BLK * j:BLK * (j + 1)], ps[rows, 7, 0:P].rearrange("p (g c) -> p g c", c=BLK),
                        bv_sb[rows, :].rearrange("p (g j c) -> p g j c", j=HG, c=BLK)[:, :, j, :],
                        ALU.add).then_inc(s_kvc, 1)
                copy_transposed(0)
                for u in range(TT * G):
                    t, g = u // G, u % G
                    dve.wait_ge(s_s1, b * TT * G + u + 1)
                    nc.vector.tensor_reduce(neg[:, u, :].rearrange("p (j c) -> p j c", c=BLK)[:, :, HD],
                                            ps[:, 2 * (u % 4):2 * (u % 4) + 2, 0:2 * S].rearrange("p a (h n) -> p a h n", n=S),
                                            AX.X, ALU.max).then_inc(s_max, 1)
                for u in range(U):
                    g, half = u // NL, u % NL
                    q = qT[:, g, half * HALF:(half + 1) * HALF]
                    dve.wait_ge(s_mt, b * U + u + 1)
                    nc.vector.tensor_tensor(q, q, ps[:, u, :], ALU.subtract).then_inc(s_qm, 1)

                def take(u):
                    dve.wait_ge(s_pv, b * U + u + 1)
                    if u >= 2:
                        dve.wait_ge(s_o, b * U + u - 1)
                    nc.vector.tensor_copy(raw[:, u % 2, :], ps[:, 5 + u % 2, :]).then_inc(s_raw, 1)

                def divide(u):
                    g, half = u // NL, u % NL
                    dve.wait_ge(s_lnd, b * 2 * U + 2 * u + 2)
                    nc.vector.tensor_tensor(oT[:, g, half * HALF:(half + 1) * HALF], raw[:, u % 2, :], lnd[:, u % 2, :],
                                            ALU.mult).then_inc(s_o, 1)

                for u in range(U + 2):
                    if u >= 2:
                        divide(u - 2)
                    if u < U:
                        take(u)
                for t in range(TT):
                    dve.wait_ge(s_proj, b * TT + t + 1)
                    nc.vector.tensor_tensor(xt[:, t, :], xt[:, t, :], ps[:, t % 4, 0:DM], ALU.add).then_inc(s_r, 1)
                    dve.wait_ge(s_r, b * TT + t + 1)
                    nc.vector.bn_stats(stats[:, t, :], xt[:, t, :]).then_inc(s_st, 1)
                aggregate(TT)
                newton()
                for t in range(TT):
                    nc.vector.tensor_scalar(xt[:, t, :], xt[:, t, :], mean[:, t:t + 1], rstd[:, t:t + 1],
                                            ALU.subtract, ALU.mult).then_inc(s_x2, 1)
                copy_transposed(NL * KT)
                gd = b * GDB
                dve.wait_ge(s_gate, b + 1)
                nc.vector.tensor_tensor(sc[:, :, :], ps[:, 7, 0:TT * E].rearrange("p (t e) -> p t e", e=E),
                                        gb_sb[:, :].unsqueeze(1).to_broadcast([P, TT, E]), ALU.add).then_inc(s_gd, 1)
                dve.wait_ge(s_gd, gd + 1)
                own = sc[:, :, :].unsqueeze(3).to_broadcast([P, TT, E, E])
                other = sc[:, :, :].unsqueeze(2).to_broadcast([P, TT, E, E])
                nc.vector.tensor_reduce(smax[:, :], sc[:, :, :], AX.X, ALU.max).then_inc(s_gd, 1)
                nc.vector.tensor_tensor(cmp1[:, :, :, :], other, own, ALU.is_gt).then_inc(s_gd, 1)
                nc.vector.tensor_tensor(cmp2[:, :, :, :], other, own, ALU.is_equal).then_inc(s_gd, 1)
                dve.wait_ge(s_gd, gd + 2)
                nc.vector.tensor_tensor(wgt[:, :, :], sc[:, :, :], smax[:, :].unsqueeze(2).to_broadcast([P, TT, E]),
                                        ALU.subtract).then_inc(s_gd, 1)
                flat1 = cmp1[:, :, :, :].rearrange("p t e f -> p t (e f)")
                flat2 = cmp2[:, :, :, :].rearrange("p t e f -> p t (e f)")
                dve.wait_ge(s_gd, gd + 4)
                nc.vector.tensor_tensor(flat2, flat2, before_sb[:, :].unsqueeze(1).to_broadcast([P, TT, E * E]),
                                        ALU.mult).then_inc(s_gd, 1)
                dve.wait_ge(s_gd, gd + 6)
                nc.vector.tensor_tensor(flat1, flat1, flat2, ALU.add).then_inc(s_gd, 1)
                dve.wait_ge(s_gd, gd + 7)
                nc.vector.tensor_reduce(rank[:, :, :].rearrange("p t e -> p (t e)"),
                                        cmp1[:, :, :, :].rearrange("p t e f -> p (t e) f"), AX.X,
                                        ALU.add).then_inc(s_gd, 1)
                dve.wait_ge(s_ge, b + 1)
                dve.wait_ge(s_gd, gd + 8)
                nc.vector.scalar_tensor_tensor(out=wgt[:, :, :], in0=rank[:, :, :], scalar=1.5, in1=wgt[:, :, :],
                                               op0=ALU.is_lt, op1=ALU.mult).then_inc(s_gd, 1)
                dve.wait_ge(s_gd, gd + 9)
                nc.vector.tensor_reduce(wsum[:, :], wgt[:, :, :], AX.X, ALU.add).then_inc(s_gd, 1)
                dve.wait_ge(s_gd, gd + 10)
                nc.vector.reciprocal(wsum[:, :], wsum[:, :]).then_inc(s_gd, 1)
                dve.wait_ge(s_gd, gd + 11)
                nc.vector.tensor_tensor(wgt[:, :, :], wgt[:, :, :], wsum[:, :].unsqueeze(2).to_broadcast([P, TT, E]),
                                        ALU.mult).then_inc(s_gd, 1)
                dve.wait_ge(s_gd, gd + 12)
                for t in range(TT):
                    nc.vector.tensor_scalar(acc[:, t, :], xt[:, t, :], 2.0, None, ALU.mult).then_inc(s_acc, 1)
                for e in range(E):
                    for t in range(TT):
                        dve.wait_ge(s_acc, b * ACB + TT * e + t + 1)
                        nc.vector.scalar_tensor_tensor(out=acc[:, t, :], in0=be2_sb[:, e * DM:(e + 1) * DM],
                                                       scalar=wgt[:, t, e:e + 1], in1=acc[:, t, :], op0=ALU.mult,
                                                       op1=ALU.add).then_inc(s_acc, 1)

                def normalise(n, ready, done, scales):
                    for i in range(TG):
                        dve.wait_ge(ready, b * TT + TG * n + i + 1)
                        for e in range(E):
                            nc.vector.bn_stats(stats[:, i * E + e, :], big[:, n, i, e * DM:(e + 1) * DM]).then_inc(s_st, 1)
                    aggregate(TG * E)
                    newton()
                    if scales is not rstd:
                        nc.vector.tensor_tensor(scales[:, :], rstd[:, :],
                                                wgt[:, TG * n:TG * (n + 1), :].rearrange("p t e -> p (t e)"),
                                                ALU.mult).then_inc(s_scale, 1)
                        dve.wait_ge(s_scale, b * NT + n + 1)
                    for i in range(TG):
                        for e in range(E):
                            c = i * E + e
                            tile = big[:, n, i, e * DM:(e + 1) * DM]
                            last = nc.vector.tensor_scalar(tile, tile, mean[:, c:c + 1], scales[:, c:c + 1],
                                                           ALU.subtract, ALU.mult)
                        last.then_inc(done, 1)

                for n in range(NT):
                    normalise(n, s_l1c, s_n1, rstd)
                for n in range(NT):
                    normalise(n, s_l2c, s_n2, scale2)
                for t in range(TT):
                    dve.wait_ge(s_sum, b * TT * E + E * (t + 1))
                    nc.vector.bn_stats(stats[:, t, :], acc[:, t, :]).then_inc(s_st, 1)
                aggregate(TT)
                newton()
                for t in range(TT):
                    nc.vector.tensor_scalar(xt[:, t, :], acc[:, t, :], mean[:, t:t + 1], rstd[:, t:t + 1],
                                            ALU.subtract, ALU.mult).then_inc(s_fin, 1)


def decoder_block(nc, x, xT, w_in, w_x, w_out, par, ident, sel_bc, sel_p, ctxT, wq, wk, wv, wo, bqk, bv, swap,
                  w1, w2, gw, gb, lnp, bias_rows, ones3, g2, be2, before, out):
    c_dram = nc.dram_tensor("c_scratch", (BATCH * NS, L), F32).ap()
    x1 = nc.dram_tensor("x1_scratch", (BATCH * L, DM), F32).ap()
    mamba_block(nc, x, xT, w_in, w_x, w_out, par, ident, sel_bc, sel_p, c_dram, x1)
    attn_ffn_block(nc, x1, ctxT, wq, wk, wv, wo, bqk, bv, ident, swap, w1, w2, gw, gb, lnp, bias_rows, ones3,
                   g2, be2, before, out)


def _constants():
    one = 0x3F80
    sel_bc = np.zeros((PARTS * BC, NS, P), np.uint16)
    for q in range(PARTS):
        for n in range(NS):
            sel_bc[BC * q + n, n, :] = one
    sel_p = np.zeros((PROJ, P), np.float32)
    sel_p[PROJ - 1] = 1
    swap = np.zeros((P, P), np.float32)
    for j in range(HG):
        for i in range(HD):
            swap[BLK * j + HD + i, BLK * j + i] = 1
            swap[BLK * j + HD + i, BLK * j + HD + i] = 1
    ones3 = np.zeros((3 * BLK, P), np.uint16)
    ones3[0::BLK] = one
    before = np.tri(E, k=-1, dtype=np.float32).reshape(E * E)
    return dict(ident=np.eye(P, dtype=np.float32), sel_bc=sel_bc, sel_p=sel_p, swap=swap, ones3=ones3, before=before)


def _layout(inputs):
    f32 = np.float32
    attn = lambda n: np.asarray(inputs["L0_attn_" + n])
    xatt = lambda n: np.asarray(inputs["L0_xattn_" + n])
    ffn = lambda n: np.asarray(inputs["L0_ffn_" + n])
    per_channel = lambda a: a.reshape(CT, P, -1).transpose(1, 0, 2).reshape(P, -1)

    def heads(w, spare=0):
        o = np.zeros(w.shape[:-1] + (BLK,), f32)
        o[..., :HD] = w
        if spare:
            o[..., HD:HD + spare] = 1
        return o.reshape(w.shape[:-2] + (NH * BLK,))

    x = np.asarray(inputs["x"]).reshape(BATCH * L, DM)
    par = np.zeros((P, PAR_COLS), f32)
    par[:, 0:PAR_COLS] = np.concatenate([per_channel(attn(n)) for n in
                                         ("A_log", "conv_w", "conv_b", "D_param", "W_dt", "b_dt")], 1)
    w_x = attn("W_x").T
    wo = np.zeros((NH, BLK, DM), f32)
    wo[:, :HD] = xatt("Wo")
    wo[0, HD] = xatt("bo")
    bias_rows = np.zeros((3 * BLK, 2 * E * DM), f32)
    bias_rows[0::BLK] = np.concatenate([ffn("b1").reshape(-1), ffn("b2").reshape(-1)])
    return dict(
        x=x, xT=x.T, w_in=attn("W_in").T,
        w_x=np.concatenate([w_x[:, :BC]] * PARTS + [w_x[:, BC:]], 1), w_out=attn("W_out").T, par=par,
        ctxT=np.asarray(inputs["ctx_1024"]).reshape(BATCH * S, DM).T,
        wq=heads(xatt("Wq")), wk=heads(xatt("Wk")), wv=heads(xatt("Wv")), wo=wo.reshape(NH * BLK, DM),
        bqk=np.concatenate([heads(xatt("bq")).reshape(G, P).T, heads(xatt("bk"), 1).reshape(G, P).T], 1),
        bv=heads(xatt("bv"), HD),
        w1=ffn("W1").transpose(1, 0, 2).reshape(DM, E * DM), w2=ffn("W2").reshape(E * DM, DM),
        gw=ffn("gate_W"), gb=ffn("gate_b"),
        lnp=np.concatenate([ffn("g1").reshape(E * KT, P).T, ffn("be1").reshape(E * KT, P).T], 1),
        bias_rows=bias_rows, g2=ffn("g2").reshape(-1), be2=ffn("be2").reshape(-1), **_constants())


_ARGS = ["x", "xT", "w_in", "w_x", "w_out", "par", "ident", "sel_bc", "sel_p", "ctxT", "wq", "wk", "wv", "wo",
         "bqk", "bv", "swap", "w1", "w2", "gw", "gb", "lnp", "bias_rows", "ones3", "g2", "be2", "before"]


def kernel(**inputs):
    import concourse.bacc as bacc
    from concourse.bass_utils import run_bass_kernel_spmd
    nc = bacc.Bacc("TRN2", target_bir_lowering=False, num_devices=1)
    data = _layout(inputs)
    arrays, args = {}, []
    for name in _ARGS:
        a = np.ascontiguousarray(data[name])
        arrays["in_" + name] = a
        args.append(nc.dram_tensor("in_" + name, a.shape, mybir.dt.from_np(a.dtype), kind="ExternalInput").ap())
    out = nc.dram_tensor("out_x", (BATCH * L, DM), F32, kind="ExternalOutput").ap()
    decoder_block(nc, *args, out)
    r = run_bass_kernel_spmd(nc, [arrays], core_ids=[0])
    return r.results[0]["out_x"].reshape(BATCH, L, DM)
```

```python
import concourse.bass as bass
from concourse import mybir
from contextlib import ExitStack
import numpy as np

F32 = mybir.dt.float32
BF16 = mybir.dt.bfloat16
ALU = mybir.AluOpType
ACT = mybir.ActivationFunctionType
AX = mybir.AxisListType

P = 128
BATCH, L, DM = 4, 1024, 256
DI, NS, TAPS = 512, 16, 4
CT = DI // P
KT = DM // P
HALF = 512
TT = L // P
TC = 256
HALO = TAPS - 1
CPB = L // TC
NCH = BATCH * CPB
CTT = TC // P
PARTS = 3
BC = 2 * NS
PROJ = PARTS * BC + 1
LN_EPS = 1e-5

PAR = {"A_log": (0, NS), "conv_w": (64, TAPS), "conv_b": (80, 1), "D": (84, 1), "W_dt": (88, 1), "b_dt": (92, 1)}
PAR_COLS = 96
NL = L // HALF
NH, HD, S = 16, 16, 154
BLK = 32
HG = P // BLK
G = NH // HG
SM = P
SR = S - SM
E = 4
TG = 4


def mamba_block(nc, x, xT, w_in, w_x, w_out, par, ident, sel_bc, sel_p, c_dram, x1):
    with ExitStack() as ctx:
        def sb(name, shape, dt=F32):
            return ctx.enter_context(nc.sbuf_tensor(name, shape, dt))

        def sem(name):
            return ctx.enter_context(nc.semaphore(name))

        RING = 4
        LAG = 2

        w_in_sb = sb("w_in_sb", [P, KT, 2 * DI])
        w_x_sb = sb("w_x_sb", [P, CT, PROJ])
        w_out_sb = sb("w_out_sb", [P, CT, DM])
        par_sb = sb("par_sb", [P, PAR_COLS])
        negA = sb("negA", [P, CT * NS])
        diag_D = sb("diag_D", [P, CT, P])
        ident_sb = sb("ident_sb", [P, P])
        sel_bc_sb = sb("sel_bc_sb", [PARTS * BC, NS, P], BF16)
        sel_p_sb = sb("sel_p_sb", [PROJ, P])
        xT_sb = sb("xT_sb", [P, 2, KT, HALO + TC])
        xs = sb("xs", [P, 2, CT, TC])
        x_raw = sb("x_raw", [P, CT, HALO + TC])
        tnh = sb("tnh", [P, CT, TC])
        tnh_z = sb("tnh_z", [P, CT, TC])
        gate = sb("gate", [P, 2, CT, TC])
        relu = sb("relu", [P, CT, TC])
        dt_sb = sb("dt_sb", [P, 2, CT, TC])
        u_sb = sb("u_sb", [P, 2, CT, TC])
        c_bc = sb("c_bc", [P, 2, NS, TC])
        decay = sb("decay", [P, RING, CT, TC])
        state = sb("state", [P, RING, CT, TC])
        state_c = sb("state_c", [P, RING, CT, TC])
        carry = sb("carry", [P, NS, CT])
        rest = sb("rest", [PARTS * BC, TC])
        proj = sb("proj", [PROJ, 2, TC])
        parts = sb("parts", [PARTS * BC, 2, TC], BF16)
        y_sb = sb("y_sb", [P, CT, TC])
        res = sb("res", [P, 2, CTT, DM])
        stats = sb("stats", [P, CTT, 6])
        mean = sb("mean", [P, CTT])
        var = sb("var", [P, CTT])
        lnv = sb("lnv", [P, CTT])
        rstd = sb("rstd", [P, CTT])
        newt = sb("newt", [P, CTT])
        coef = sb("coef", [P, 4, CTT])

        def bank(name, n=1):
            return ctx.enter_context(nc.psum_tensor(name, [P, n * HALF], F32))

        b_ps = [bank("b_ps0"), bank("b_ps1")]
        bu_ps = [bank(f"bu_ps{k}") for k in range(3)]
        y_ps = bank("y_ps", 2)
        w_ps = bank("w_ps")

        def col(name, j, k=0):
            first, per = PAR[name]
            return par_sb[:, first + j * per + k:first + j * per + k + 1]

        s_const = sem("s_const")
        s_xT = [sem(f"s_xT{q}") for q in range(2)]
        s_res = [sem(f"s_res{q}") for q in range(2)]
        s_cb = [[sem(f"s_cb{q}{h}") for h in range(2)] for q in range(2)]
        s_x1 = [sem(f"s_x1{q}") for q in range(2)]
        s_cst = sem("s_cst")
        s_par = sem("s_par")
        s_coef = sem("s_coef")
        s_in = sem("s_in")
        s_conv0 = sem("s_conv0")
        s_conv = sem("s_conv")
        s_tanh = sem("s_tanh")
        s_silu = sem("s_silu")
        s_gate = sem("s_gate")
        s_proj = sem("s_proj")
        s_projc = sem("s_projc")
        s_split = sem("s_split")
        s_step = sem("s_step")
        s_abs = sem("s_abs")
        s_sp = sem("s_sp")
        s_dt = sem("s_dt")
        s_u = sem("s_u")
        s_b = sem("s_b")
        s_decay = sem("s_decay")
        s_bu = sem("s_bu")
        s_scan = sem("s_scan")
        s_carry = sem("s_carry")
        s_sc = sem("s_sc")
        s_sum = sem("s_sum")
        s_y = sem("s_y")
        s_out = sem("s_out")
        s_r = sem("s_r")
        s_st = sem("s_st")
        s_mv = sem("s_mv")
        s_nw = sem("s_nw")
        s_ln = sem("s_ln")
        s_norm = sem("s_norm")

        def at(i, per, more=0):
            b, r = i
            return r * per + more if b is None else b * (CPB * per) + (r * per + more)

        def shift(i, n):
            return (i[0], i[1] + n)

        def is_first(i):
            return i[0] is None and i[1] == 0

        def loads(i):
            b, r = i
            n = 16 * (r // 2 + 1)
            return n if b is None else b * (16 * CPB // 2) + n

        def tokens(i, more=0, count=TC):
            return bass.ds(at(i, TC, more), count)

        def turns(eng, turn):
            turn((None, 0), prepare=True, finish=False, settle=False)
            turn((None, 1), prepare=True, finish=True, settle=False)
            with eng.Fori(0, BATCH - 1) as b:
                for r in range(2, CPB + 2):
                    turn((b, r), prepare=True, finish=True, settle=True)
            for r in range(NCH - CPB + 2, NCH):
                turn((None, r), prepare=r + 1 < NCH, finish=True, settle=True)

        block = ctx.enter_context(nc.Block())

        @block.sync
        def _(sp):
            def load_xT(k):
                q, skip = k[1] % 2, HALO if k[1] % CPB == 0 else 0
                sp.dma_start(xT_sb[:, q, :, skip:],
                             xT[:, tokens(k, skip - HALO, HALO + TC - skip)].rearrange("(k p) n -> p k n", p=P))\
                  .then_inc(s_xT[q], 16)

            def load_res(k):
                q = k[1] % 2
                sp.dma_start(res[:, q, :, :], x[tokens(k), :].rearrange("(t p) n -> p t n", p=P)).then_inc(s_res[q], 16)

            def load_c(k):
                q = k[1] % 2
                sp.wait_ge(s_projc, at(k, 2, 1))
                sp.dma_start(c_dram[bass.ds(at(k, NS), NS), :], proj[NS:BC, q, :]).then_inc(s_cst, 16)
                count = at(k, 16, 16)
                sp.wait_ge(s_cst, count)
                sp.wait_ge(s_y, count)
                for h in range(2):
                    n = NS // 2
                    sp.dma_start(c_bc[:, q, h * n:(h + 1) * n, :],
                                 c_dram[bass.ds(at(k, NS, h * n), n), :].partition_broadcast(P)).then_inc(s_cb[q][h], 16)

            def turn(i, prepare, finish, settle):
                k = shift(i, 1)
                if i[0] is not None or i[1] + 2 < NCH:
                    sp.wait_ge(s_in, at(i, 6, 6))
                    load_xT(shift(i, 2))
                if prepare:
                    load_c(k)
                if settle:
                    store_x1(shift(i, -2))
                    sp.wait_ge(s_x1[i[1] % 2], loads(shift(i, -2)))
                    load_res(i)

            def store_x1(k):
                q = k[1] % 2
                sp.wait_ge(s_norm, at(k, CTT, 2 * CTT))
                sp.dma_start(x1[tokens(k), :].rearrange("(t p) n -> p t n", p=P), res[:, q, :, :]).then_inc(s_x1[q], 16)

            sp.dma_start(w_in_sb[:, :, :], w_in.rearrange("(k p) n -> p k n", p=P)).then_inc(s_const, 16)
            load_xT((None, 0))
            sp.dma_start(par_sb[:, :], par).then_inc(s_const, 16)
            sp.dma_start(w_x_sb[:, :, :], w_x.rearrange("(k p) n -> p k n", p=P)).then_inc(s_const, 16)
            sp.dma_start(sel_p_sb[:, :], sel_p).then_inc(s_const, 16)
            sp.dma_start(sel_bc_sb[:, :, :], sel_bc.bitcast(BF16)).then_inc(s_const, 16)
            sp.dma_start(ident_sb[:, :], ident).then_inc(s_const, 16)
            sp.dma_start(w_out_sb[:, :, :], w_out.rearrange("(k p) n -> p k n", p=P)).then_inc(s_const, 16)
            load_xT((None, 1))
            load_res((None, 0))
            load_res((None, 1))
            load_c((None, 0))
            turns(sp, turn)
            store_x1((None, NCH - 2))
            store_x1((None, NCH - 1))
            sp.wait_ge(s_x1[0], 16 * NCH // 2)
            sp.wait_ge(s_x1[1], 16 * NCH // 2)

        @block.tensor
        def _(pe):
            def x_tile(k, j):
                q, skip = k[1] % 2, HALO if k[1] % CPB == 0 else 0
                if j == 0:
                    pe.wait_ge(s_xT[q], loads(k))
                    if not is_first(k):
                        pe.wait_ge(s_abs, at(k, 2 * CT, 0))
                        pe.wait_ge(s_r, at(k, CTT, 0))
                else:
                    pe.wait_ge(s_conv0, at(k, 2 * CT, 2 * j))
                for c in range(KT):
                    last = nc.tensor.matmul(w_ps[:, skip:HALO + TC], w_in_sb[:, c, j * P:(j + 1) * P],
                                            xT_sb[:, q, c, skip:HALO + TC], start=c == 0, stop=c == KT - 1)
                last.then_inc(s_in, 1)

            def z_pair(k, h):
                if h == 0:
                    pe.wait_ge(s_conv0, at(k, 2 * CT, 2 * CT))
                else:
                    pe.wait_ge(s_gate, at(k, 2, 1))
                for e in range(2):
                    m = CT + 2 * h + e
                    for c in range(KT):
                        last = nc.tensor.matmul(w_ps[:, e * TC:(e + 1) * TC], w_in_sb[:, c, m * P:(m + 1) * P],
                                                xT_sb[:, k[1] % 2, c, HALO:HALO + TC], start=c == 0, stop=c == KT - 1)
                last.then_inc(s_in, 1)

            def project(k):
                pe.wait_ge(s_silu, at(k, 1, 1))
                pe.wait_ge(s_gate, at(k, 2, 2))
                for j in range(CT):
                    last = nc.tensor.matmul(w_ps[0:PROJ, 0:TC], w_x_sb[:, j, :], xs[:, k[1] % 2, j, :],
                                            start=j == 0, stop=j == CT - 1)
                last.then_inc(s_proj, 1)

            def step_row(k):
                pe.wait_ge(s_projc, at(k, 2, 2))
                nc.tensor.matmul(w_ps[:, 0:TC], sel_p_sb[:, :], proj[:, k[1] % 2, :], start=True, stop=True)\
                  .then_inc(s_step, 1)

            def out_tile(k, t):
                if t == 0:
                    more = k[0] is not None or k[1] + 2 < NCH
                    pe.wait_ge(s_y, at(k, 16, 48))
                    pe.wait_ge(s_abs, at(k, 2 * CT, 6 * CT) if more else 2 * CT * NCH)
                else:
                    pe.wait_ge(s_r, at(k, CTT, 2 * CTT + 1))
                for j in range(CT):
                    last = nc.tensor.matmul(w_ps[:, 0:DM], y_sb[:, j, t * P:(t + 1) * P], w_out_sb[:, j, :],
                                            start=j == 0, stop=j == CT - 1)
                last.then_inc(s_out, 1)

            def b_row(i, n):
                if n == 0:
                    pe.wait_ge(s_split, at(i, 5, 5))
                pe.wait_ge(s_bu, at(i, 2 * NS, 2 * n + 2))
                nc.tensor.matmul(b_ps[n % 2][:, 0:TC], sel_bc_sb[:, n, :], parts[:, i[1] % 2, :], start=True, stop=True)\
                  .then_inc(s_b, 1)

            def add_state(i, n):
                if n == 0:
                    pe.wait_ge(s_y, at(i, 16, 32))
                    for j in range(CT):
                        nc.tensor.matmul(y_ps[:, j * TC:(j + 1) * TC], diag_D[:, j, :], xs[:, i[1] % 2, j, :],
                                         start=j % 2 == 0, stop=False)
                pe.wait_ge(s_sc, at(i, NS, RING + n + 1))
                for h in range(2):
                    last = nc.tensor.matmul(y_ps[:, h * HALF:(h + 1) * HALF], ident_sb[:, :],
                                            state_c[:, n % RING, 2 * h:2 * h + 2, :],
                                            start=False, stop=n == NS - 1)
                last.then_inc(s_sum, 1)

            def turn(i, prepare, finish, settle):
                k, last = shift(i, 1), shift(i, -1)
                work = {}
                if prepare:
                    work = {0: [lambda: x_tile(k, 0)], 1: [lambda: x_tile(k, 1)], 2: [lambda: x_tile(k, 2)],
                            3: [lambda: x_tile(k, 3)], 4: [lambda: z_pair(k, 0)], 6: [lambda: z_pair(k, 1)],
                            8: [lambda: project(k)], 9: [lambda: step_row(k)]}
                if finish:
                    work[11] = [lambda: out_tile(last, 0)]
                    work[12] = [lambda: out_tile(last, 1)]
                for n in range(NS):
                    if n + 2 < NS:
                        b_row(i, n + 2)
                    elif prepare:
                        b_row(k, n + 2 - NS)
                    if n >= LAG:
                        add_state(i, n - LAG)
                    elif finish:
                        add_state(last, NS + n - LAG)
                    for w in work.get(n, []):
                        w()

            pe.sem_inc(s_r, 2 * CTT)
            pe.wait_ge(s_const, 7 * 16)
            first = (None, 0)
            for j in range(CT):
                x_tile(first, j)
            z_pair(first, 0)
            z_pair(first, 1)
            project(first)
            step_row(first)
            b_row(first, 0)
            b_row(first, 1)
            pe.wait_ge(s_par, 3 + CT)
            turns(pe, turn)
            for n in range(NS - LAG, NS):
                add_state((None, NCH - 1), n)
            out_tile((None, NCH - 1), 0)
            out_tile((None, NCH - 1), 1)

        @block.scalar
        def _(act):
            def first_tap(k, j):
                act.wait_ge(s_in, at(k, 6, j + 1))
                if j == 0 and (k[0] is not None or k[1] >= 2):
                    act.wait_ge(s_sum, at(k, NS, RING + 1 - 2 * NS))
                if not is_first(k):
                    act.wait_ge(s_conv, at(k, 3 * CT, 3 * (j + 1 - CT)))
                skip = HALO if k[1] % CPB == 0 else 0
                nc.scalar.activation(x_raw[:, j, skip:], w_ps[:, skip:HALO + TC], ACT.Copy).then_inc(s_conv0, 1)
                nc.scalar.activation(xs[:, k[1] % 2, j, :], w_ps[:, HALO:HALO + TC], ACT.Identity,
                                     scale=col("conv_w", j, TAPS - 1), bias=col("conv_b", j)).then_inc(s_conv0, 1)

            def tanh_x(k):
                act.wait_ge(s_conv, at(k, 3 * CT, 3 * CT))
                if not is_first(k):
                    act.wait_ge(s_silu, at(k, 1, 0))
                nc.scalar.activation(tnh[:, :, :], xs[:, k[1] % 2, :, :], ACT.Tanh).then_inc(s_tanh, 1)
                act.wait_ge(s_tanh, at(k, 4, 2))
                nc.scalar.activation(tnh[:, :, :], tnh[:, :, :], ACT.Copy, bias=1.0).then_inc(s_tanh, 1)

            def tanh_z(k, h):
                if h == 0:
                    nc.scalar.preload_act_table_set("exp_and_others")
                act.wait_ge(s_in, at(k, 6, CT + h + 1))
                nc.scalar.activation(tnh_z[:, 2 * h:2 * h + 2, :], w_ps[:, :], ACT.Tanh, scale=0.5).then_inc(s_tanh, 1)

            def copies(k):
                act.wait_ge(s_proj, at(k, 1, 1))
                nc.scalar.activation(proj[:, k[1] % 2, :], w_ps[0:PROJ, 0:TC], ACT.Copy).then_inc(s_projc, 1)
                nc.scalar.activation(parts[:, k[1] % 2, :], w_ps[0:PARTS * BC, 0:TC], ACT.Copy).then_inc(s_projc, 1)

            def terms(k, j):
                if j == 0:
                    act.wait_ge(s_step, at(k, 1, 1))
                nc.scalar.activation(dt_sb[:, k[1] % 2, j, :], w_ps[:, 0:TC], ACT.Abs,
                                     scale=col("W_dt", j), bias=col("b_dt", j)).then_inc(s_abs, 1)
                nc.scalar.activation(relu[:, j, :], w_ps[:, 0:TC], ACT.Relu,
                                     scale=col("W_dt", j), bias=col("b_dt", j)).then_inc(s_abs, 1)

            def softplus(k):
                d = dt_sb[:, k[1] % 2, :, :]
                act.wait_ge(s_abs, at(k, 2 * CT, 2 * CT))
                nc.scalar.activation(d, d, ACT.Exp, scale=-1.0).then_inc(s_sp, 1)
                nc.scalar.preload_act_table_set("natural_log_exp_and_others")
                act.wait_ge(s_sp, at(k, 2, 1))
                nc.scalar.activation(d, d, ACT.Ln, bias=1.0).then_inc(s_sp, 1)

            def guess(k):
                act.wait_ge(s_nw, at(k, 6, 1))
                nc.scalar.activation(lnv[:, :], var[:, :], ACT.Ln).then_inc(s_ln, 1)
                act.wait_ge(s_ln, at(k, 2, 1))
                nc.scalar.activation(rstd[:, :], lnv[:, :], ACT.Exp, scale=-0.5).then_inc(s_ln, 1)

            def step(i, n):
                for j in range(CT):
                    if j == 0:
                        if n == 0:
                            act.wait_ge(s_dt, at(i, 1, 1))
                        act.wait_ge(s_scan, at(i, NS * CT, n * CT + CT))
                        if n >= RING or not is_first(i):
                            nc.scalar.activation(carry[:, (n - RING) % NS, :], state[:, n % RING, :, TC - 1],
                                                 ACT.Copy).then_inc(s_carry, 1)
                    nc.scalar.activation(decay[:, n % RING, j, :], dt_sb[:, i[1] % 2, j, :], ACT.Exp,
                                         scale=negA[:, j * NS + n:j * NS + n + 1]).then_inc(s_decay, 1)

            def turn(i, prepare, finish, settle):
                k = shift(i, 1)
                work = {}
                if prepare:
                    work = {3: [lambda: first_tap(k, 0)], 4: [lambda: first_tap(k, 1)], 5: [lambda: first_tap(k, 2)],
                            6: [lambda: first_tap(k, 3)], 7: [lambda: tanh_z(k, 0)], 8: [lambda: tanh_x(k)],
                            9: [lambda: tanh_z(k, 1)], 11: [lambda: copies(k)],
                            12: [lambda: terms(k, 0), lambda: terms(k, 1), lambda: terms(k, 2), lambda: terms(k, 3),
                                 lambda: softplus(k)]}
                if settle:
                    work[2] = [lambda: guess(shift(i, -2))]
                for n in range(NS):
                    step(i, n)
                    for w in work.get(n, []):
                        w()

            act.sem_inc(s_scan, RING * CT)
            act.sem_inc(s_y, 32)
            act.wait_ge(s_const, 7 * 16)
            nc.scalar.activation(negA[:, :], par_sb[:, 0:CT * NS], ACT.Exp).then_inc(s_par, 1)
            act.wait_ge(s_par, 3)
            first = (None, 0)
            for j in range(CT):
                first_tap(first, j)
            tanh_z(first, 0)
            tanh_x(first)
            tanh_z(first, 1)
            copies(first)
            for j in range(CT):
                terms(first, j)
            softplus(first)
            turns(act, turn)
            guess((None, NCH - 2))
            guess((None, NCH - 1))

        @block.gpsimd
        def _(pool):
            def make_dt(k):
                q = k[1] % 2
                pool.wait_ge(s_sp, at(k, 2, 2))
                nc.gpsimd.tensor_tensor(dt_sb[:, q, :, :], dt_sb[:, q, :, :], relu[:, :, :], ALU.add).then_inc(s_dt, 1)

            def make_u(k):
                q = k[1] % 2
                pool.wait_ge(s_dt, at(k, 1, 1))
                nc.gpsimd.tensor_tensor(u_sb[:, q, :, :], dt_sb[:, q, :, :], xs[:, q, :, :], ALU.mult).then_inc(s_u, 1)

            def silu_x(k):
                pool.wait_ge(s_tanh, at(k, 4, 3))
                nc.gpsimd.tensor_tensor(xs[:, k[1] % 2, :, :], xs[:, k[1] % 2, :, :], tnh[:, :, :], ALU.mult)\
                  .then_inc(s_silu, 1)

            def variance(k):
                pool.wait_ge(s_norm, at(k, CTT, CTT))
                pool.wait_ge(s_st, at(k, CTT, CTT))
                nc.gpsimd.tensor_tensor(mean[:, :], stats[:, :, 1], stats[:, :, 4], ALU.add).then_inc(s_mv, 1)
                nc.gpsimd.tensor_tensor(newt[:, :], stats[:, :, 1], stats[:, :, 4], ALU.subtract).then_inc(s_mv, 1)
                nc.gpsimd.tensor_tensor(var[:, :], stats[:, :, 2], stats[:, :, 5], ALU.add).then_inc(s_mv, 1)
                pool.wait_ge(s_mv, at(k, 8, 3))
                nc.gpsimd.tensor_tensor(newt[:, :], newt[:, :], half, ALU.mult).then_inc(s_mv, 1)
                nc.gpsimd.tensor_tensor(mean[:, :], mean[:, :], half, ALU.mult).then_inc(s_mv, 1)
                nc.gpsimd.tensor_tensor(var[:, :], var[:, :], per_dm, ALU.mult).then_inc(s_mv, 1)
                pool.wait_ge(s_mv, at(k, 8, 6))
                nc.gpsimd.tensor_tensor(newt[:, :], newt[:, :], newt[:, :], ALU.mult).then_inc(s_mv, 1)
                nc.gpsimd.tensor_tensor(var[:, :], var[:, :], eps, ALU.add).then_inc(s_mv, 1)
                pool.wait_ge(s_mv, at(k, 8, 8))
                nc.gpsimd.tensor_tensor(var[:, :], newt[:, :], var[:, :], ALU.add).then_inc(s_nw, 1)

            def newton(k):
                pool.wait_ge(s_ln, at(k, 2, 2))
                nc.gpsimd.tensor_tensor(newt[:, :], rstd[:, :], rstd[:, :], ALU.mult).then_inc(s_nw, 1)
                pool.wait_ge(s_nw, at(k, 6, 2))
                nc.gpsimd.tensor_tensor(newt[:, :], newt[:, :], var[:, :], ALU.mult).then_inc(s_nw, 1)
                pool.wait_ge(s_nw, at(k, 6, 3))
                nc.gpsimd.tensor_tensor(newt[:, :], newt[:, :], half, ALU.mult).then_inc(s_nw, 1)
                pool.wait_ge(s_nw, at(k, 6, 4))
                nc.gpsimd.tensor_tensor(newt[:, :], one_half, newt[:, :], ALU.subtract).then_inc(s_nw, 1)
                pool.wait_ge(s_nw, at(k, 6, 5))
                nc.gpsimd.tensor_tensor(rstd[:, :], rstd[:, :], newt[:, :], ALU.mult).then_inc(s_nw, 1)

            def turn(i, prepare, finish, settle):
                k, last, q = shift(i, 1), shift(i, -1), i[1] % 2
                work = {}
                if prepare:
                    work = {5: [lambda: silu_x(k)], 11: [lambda: make_dt(k)], 12: [lambda: make_u(k)]}
                if settle:
                    work[2] = [lambda: newton(shift(i, -2))]
                if finish:
                    work[14] = [lambda: variance(last)]
                for n in range(NS):
                    if n % (NS // 2) == 0:
                        pool.wait_ge(s_cb[q][n // (NS // 2)], loads(i))
                    pool.wait_ge(s_scan, at(i, NS * CT, (RING + n + 1) * CT))
                    pool.wait_ge(s_sum, at(i, NS, n + 1))
                    nc.gpsimd.tensor_tensor(state_c[:, n % RING, :, :], state[:, n % RING, :, :],
                                            c_bc[:, q, n, :].unsqueeze(1).to_broadcast([P, CT, TC]),
                                            ALU.mult).then_inc(s_sc, 1)
                    for w in work.get(n, []):
                        w()

            for c, value in enumerate((0.5, 1.5, 1.0 / DM, LN_EPS)):
                nc.gpsimd.memset(coef[:, c, :], value).then_inc(s_coef, 1)
            half, one_half, per_dm, eps = (coef[:, c, :] for c in range(4))
            pool.sem_inc(s_sum, RING)
            pool.sem_inc(s_norm, CTT)
            pool.wait_ge(s_coef, 4)
            silu_x((None, 0))
            make_dt((None, 0))
            make_u((None, 0))
            turns(pool, turn)
            newton((None, NCH - 2))
            variance((None, NCH - 1))
            newton((None, NCH - 1))

        @block.vector
        def _(dve):
            def tap(k, j, back):
                if back == 1:
                    dve.wait_ge(s_conv0, at(k, 2 * CT, 2 * j + 2))
                else:
                    dve.wait_ge(s_conv, at(k, 3 * CT, 3 * j + back - 1))
                skip = back if k[1] % CPB == 0 else 0
                out = xs[:, k[1] % 2, j, skip:TC]
                nc.vector.scalar_tensor_tensor(out=out, in0=x_raw[:, j, HALO + skip - back:HALO + TC - back],
                                               scalar=col("conv_w", j, TAPS - 1 - back), in1=out,
                                               op0=ALU.mult, op1=ALU.add).then_inc(s_conv, 1)

            def gate_z(k, h):
                if h == 0 and (k[0] is not None or k[1] >= 2):
                    dve.wait_ge(s_y, at(k, 16, 16))
                dve.wait_ge(s_tanh, at(k, 4, 3 * h + 1))
                nc.vector.scalar_tensor_tensor(out=gate[:, k[1] % 2, 2 * h:2 * h + 2, :].rearrange("p j n -> p (j n)"),
                                               in0=tnh_z[:, 2 * h:2 * h + 2, :].rearrange("p j n -> p (j n)"), scalar=1.0,
                                               in1=w_ps[:, :], op0=ALU.add, op1=ALU.mult).then_inc(s_gate, 1)

            def split(k, step):
                q = k[1] % 2
                mid, low = slice(BC, 2 * BC), slice(2 * BC, 3 * BC)
                if step == 0:
                    dve.wait_ge(s_projc, at(k, 2, 2))
                    nc.vector.tensor_tensor(rest[:, :], proj[0:PARTS * BC, q, :], parts[:, q, :], ALU.subtract)\
                      .then_inc(s_split, 1)
                elif step == 1:
                    dve.wait_ge(s_split, at(k, 5, 1))
                    nc.vector.tensor_copy(parts[mid, q, :], rest[mid, :]).then_inc(s_split, 1)
                    nc.vector.tensor_copy(parts[low, q, :], rest[low, :]).then_inc(s_split, 1)
                elif step == 2:
                    dve.wait_ge(s_split, at(k, 5, 3))
                    nc.vector.tensor_tensor(rest[low, :], rest[low, :], parts[low, q, :], ALU.subtract).then_inc(s_split, 1)
                else:
                    dve.wait_ge(s_split, at(k, 5, 4))
                    nc.vector.tensor_copy(parts[low, q, :], rest[low, :]).then_inc(s_split, 1)

            def take_y(k):
                q = k[1] % 2
                dve.wait_ge(s_sum, at(k, NS, RING + NS))
                nc.vector.scalar_tensor_tensor(out=y_sb[:, :, :].rearrange("p j n -> p (j n)"), in0=y_ps[:, :], scalar=0.5,
                                               in1=gate[:, q, :, :].rearrange("p j n -> p (j n)"),
                                               op0=ALU.mult, op1=ALU.mult).then_inc(s_y, 16)

            def residual(k, t):
                q = k[1] % 2
                if t == 0:
                    dve.wait_ge(s_res[q], loads(k))
                dve.wait_ge(s_out, at(k, CTT, t + 1))
                nc.vector.tensor_tensor(res[:, q, t, :], res[:, q, t, :], w_ps[:, 0:DM], ALU.add).then_inc(s_r, 1)

            def moments(k, t):
                q = k[1] % 2
                dve.wait_ge(s_r, at(k, CTT, 2 * CTT + t + 1))
                nc.vector.bn_stats(stats[:, t, :], res[:, q, t, :]).then_inc(s_st, 1)

            def normalise(k):
                q = k[1] % 2
                dve.wait_ge(s_nw, at(k, 6, 6))
                for t in range(CTT):
                    nc.vector.tensor_scalar(res[:, q, t, :], res[:, q, t, :], mean[:, t:t + 1], rstd[:, t:t + 1],
                                            ALU.subtract, ALU.mult).then_inc(s_norm, 1)

            def make_bu(i, n, h):
                m = 2 * n + h
                if m == 0:
                    dve.wait_ge(s_u, at(i, 1, 1))
                if h == 0:
                    dve.wait_ge(s_b, at(i, NS, n + 1))
                dve.wait_ge(s_scan, at(i, NS * CT, RING * CT + 2 * (m - (1 if m < 2 else 2))))
                nc.vector.tensor_tensor(bu_ps[m % 3][:, :].rearrange("p (j n) -> p j n", j=2),
                                        u_sb[:, i[1] % 2, 2 * h:2 * h + 2, :],
                                        b_ps[n % 2][:, 0:TC].unsqueeze(1).to_broadcast([P, 2, TC]),
                                        ALU.mult).then_inc(s_bu, 1)

            def scans(i, n, h):
                m, c = 2 * n + h, i[1] % CPB
                if h == 0:
                    dve.wait_ge(s_sc, at(i, NS, n + 1))
                    if c:
                        dve.wait_ge(s_carry, at(i, NS, n + 1 - NS))
                dve.wait_ge(s_bu, at(i, 2 * NS, 4 + m + 1))
                for e in range(2):
                    j = 2 * h + e
                    dve.wait_ge(s_decay, at(i, NS * CT, n * CT + j + 1))
                    nc.vector.tensor_tensor_scan(state[:, n % RING, j, :], decay[:, n % RING, j, :],
                                                 bu_ps[m % 3][:, e * TC:(e + 1) * TC],
                                                 carry[:, n, j:j + 1] if c else 0.0, ALU.mult, ALU.add).then_inc(s_scan, 1)

            def step(i, n, prepare, between):
                make_bu(i, n, 1)
                between(4 * n)
                scans(i, n, 0)
                between(4 * n + 1)
                if n + 1 < NS:
                    make_bu(i, n + 1, 0)
                elif prepare:
                    make_bu(shift(i, 1), 0, 0)
                between(4 * n + 2)
                scans(i, n, 1)
                between(4 * n + 3)

            def turn(i, prepare, finish, settle):
                k, last = shift(i, 1), shift(i, -1)
                work = []
                if prepare:
                    for j in range(CT):
                        for back in (1, 2, 3):
                            work.append((4 * (j + 2) + back - 1, lambda j=j, back=back: tap(k, j, back)))
                    work += [(4 * 6 + 3, lambda: gate_z(k, 0)), (4 * 8 + 2, lambda: gate_z(k, 1))]
                    for m in range(4):
                        work.append((4 * 10 + m, lambda m=m: split(k, m)))
                if settle:
                    work.append((4 * 7, lambda: normalise(shift(i, -2))))
                if finish:
                    work += [(4 * 2, lambda: take_y(last)),
                             (4 * 12 + 2, lambda: residual(last, 0)), (4 * 13, lambda: moments(last, 0)),
                             (4 * 13 + 2, lambda: residual(last, 1)), (4 * 14, lambda: moments(last, 1))]

                def between(place):
                    for p, what in work:
                        if p == place:
                            what()

                for n in range(NS):
                    step(i, n, prepare, between)

            dve.sem_inc(s_bu, 4)
            dve.sem_inc(s_sc, RING)
            dve.wait_ge(s_par, 1)
            nc.vector.tensor_scalar(negA[:, :], negA[:, :], -1.0, None, ALU.mult).then_inc(s_par, 1)
            first_col, end_col = PAR["conv_w"][0], PAR["D"][0]
            nc.vector.tensor_scalar(par_sb[:, first_col:end_col], par_sb[:, first_col:end_col], 0.5, None,
                                    ALU.mult).then_inc(s_par, 1)
            dve.wait_ge(s_par, 3)
            for j in range(CT):
                nc.vector.tensor_scalar(diag_D[:, j, :], ident_sb[:, :], col("D", j), None, ALU.mult).then_inc(s_par, 1)
            first = (None, 0)
            for j in range(CT):
                for back in (1, 2, 3):
                    tap(first, j, back)
            gate_z(first, 0)
            gate_z(first, 1)
            for m in range(4):
                split(first, m)
            make_bu(first, 0, 0)
            turns(dve, turn)
            last = (None, NCH - 1)
            take_y(last)
            normalise((None, NCH - 2))
            for t in range(CTT):
                residual(last, t)
                moments(last, t)
            normalise(last)


def attn_ffn_block(nc, x1, ctxT, wq, wk, wv, wo, bqk, bv, ident, swap, w1, w2, gw, gb, lnp, bias_rows,
                   ones3, g2, be2, before, out):
    U = G * NL
    NT = TT // TG

    with ExitStack() as ctx:
        def sb(name, shape, dt=F32):
            return ctx.enter_context(nc.sbuf_tensor(name, shape, dt))

        def sem(name):
            return ctx.enter_context(nc.semaphore(name))

        wq_sb = sb("wq_sb", [P, KT, G * P])
        wk_sb = sb("wk_sb", [P, KT, G * P])
        wv_sb = sb("wv_sb", [P, KT, G * P])
        wo_sb = sb("wo_sb", [P, G, DM])
        bqk_sb = sb("bqk_sb", [P, 2 * G])
        bv_sb = sb("bv_sb", [P, G * P])
        ident_sb = sb("ident2_sb", [P, P])
        swap_sb = sb("swap_sb", [P, P])
        w1_sb = sb("w1_sb", [P, KT, E * DM])
        w2_sb = sb("w2_sb", [P, E * KT, DM])
        gw_sb = sb("gw_sb", [P, KT, E])
        gb_sb = sb("gb_sb", [P, E])
        lnp_sb = sb("lnp_sb", [P, 2 * E * KT])
        g2_sb = sb("g2_sb", [P, E * DM])
        be2_sb = sb("be2_sb", [P, E * DM])
        before_sb = sb("before_sb", [P, E * E])
        ones3_sb = sb("ones3_sb", [3 * BLK, P], BF16)
        brow = sb("brow", [3 * BLK, 2 * E * DM], BF16)
        xa = sb("xa", [P, TT, DM])
        xt = sb("xt", [P, TT, DM])
        x1T = sb("x1T_sb", [P, KT, L])
        xT = sb("xT2_sb", [P, KT, L])
        ctx_sb = sb("ctx_sb", [P, KT, S])
        qT = sb("qT", [P, G, L])
        kTm = sb("kTm", [P, NH, S])
        kTr = sb("kTr", [P, G, P])
        v_sb = sb("v_sb", [P, NH, BLK])
        v_rem = sb("v_rem", [P, G, P])
        big = sb("big", [P, 2, TG, E * DM])
        stage = big[:, 0, 0:2, :].rearrange("p a (t n) -> p (a t) n", n=DM)
        pT_rem = sb("pT_rem", [P, 2, HALF])
        oT = sb("oT", [P, G, L])
        neg = oT[:, :, :].rearrange("p g (t c) -> p (g t) c", c=P)
        hT = sb("hT", [P, E * KT, HALF])
        pT = hT
        raw = sb("raw", [P, 2, HALF])
        lnd = sb("lnd", [P, 2, HALF])
        stats = sb("stats2", [P, TG * E, 6])
        mean = sb("mean2", [P, TG * E])
        var = sb("var2", [P, TG * E])
        lnv = sb("lnv2", [P, TG * E])
        rstd = sb("rstd2", [P, TG * E])
        newt = sb("newt2", [P, TG * E])
        sc = sb("sc", [P, TT, E])
        smax = sb("smax", [P, TT])
        cmp1 = sb("cmp1", [P, TT, E, E])
        cmp2 = sb("cmp2", [P, TT, E, E])
        rank = sb("rank", [P, TT, E])
        wgt = sb("wgt", [P, TT, E])
        wsum = sb("wsum", [P, TT])
        acc = sb("acc", [P, TT, DM])
        scale2 = sb("scale2", [P, TG * E])
        zero = sb("zero", [P, TT * G])
        shift2 = sb("shift2", [P, TG * E])

        ps = ctx.enter_context(nc.psum_tensor("ps", [P, 8, HALF], F32))

        s_front = sem("a_front")
        s_const = sem("a_const")
        s_prep = sem("a_prep")
        s_split = sem("a_split")
        s_brow = sem("a_brow")
        s_x = sem("a_x")
        s_stage = sem("a_stage")
        s_zero = sem("a_zero")
        s_zero1 = sem("a_zero1")
        s_ctx = sem("a_ctx")
        s_xt = sem("a_xt")
        s_xtc = sem("a_xtc")
        s_yt = sem("a_yt")
        s_ytc = sem("a_ytc")
        s_kv = sem("a_kv")
        s_kvc = sem("a_kvc")
        s_q = sem("a_q")
        s_qc = sem("a_qc")
        s_s1 = sem("a_s1")
        s_max = sem("a_max")
        s_mt = sem("a_mt")
        s_qm = sem("a_qm")
        s_s2 = sem("a_s2")
        s_exp = sem("a_exp")
        s_pv = sem("a_pv")
        s_raw = sem("a_raw")
        s_den = sem("a_den")
        s_lnd = sem("a_lnd")
        s_o = sem("a_o")
        s_proj = sem("a_proj")
        s_r = sem("a_r")
        s_st = sem("a_st")
        s_mv = sem("a_mv")
        s_nw = sem("a_nw")
        s_ln = sem("a_ln")
        s_x2 = sem("a_x2")
        s_gate = sem("a_gate")
        s_gd = sem("a_gd")
        s_ge = sem("a_ge")
        s_l1 = sem("a_l1")
        s_l1c = sem("a_l1c")
        s_n1 = sem("a_n1")
        s_h = sem("a_h")
        s_hc = sem("a_hc")
        s_l2 = sem("a_l2")
        s_l2c = sem("a_l2c")
        s_n2 = sem("a_n2")
        s_shift = sem("a_shift")
        s_scale = sem("a_scale")
        s_gm = sem("a_gm")
        s_acc = sem("a_acc")
        s_sum = sem("a_sum")
        s_fin = sem("a_fin")
        s_out = sem("a_out")

        TRB, NWB, LNB = KT * NL, 5 * (2 + 2 * NT), 2 * (2 + 2 * NT)
        MVB = TT + 2 * TT * E + TT
        NORMS = 2 + 2 * NT
        NMB = 6 * NORMS
        KVB, GDB, ACB = 1 + 3 * HG, 12, TT * (E + 1)

        block = ctx.enter_context(nc.Block())
        FRONT, LOADS = 6, 11

        def turns(eng, turn):
            with eng.Fori(0, BATCH - 1) as b:
                turn(b, True)
            turn(BATCH - 1, False)

        @block.sync
        def _(sp):
            def load(dst, src, ready=s_const):
                sp.dma_start(dst, src).then_inc(ready, 16)

            def load_x1(b, dst, ready):
                sp.dma_start(dst, x1[bass.ds(b * L, L), :].rearrange("(t p) n -> p t n", p=P)).then_inc(ready, 16)

            def load_ctx(b):
                sp.dma_start(ctx_sb[:, :, :], ctxT[:, bass.ds(b * S, S)].rearrange("(k p) n -> p k n", p=P)).then_inc(s_ctx, 16)

            load_x1(0, stage, s_stage)
            load(ident_sb[:, :], ident, s_front)
            load(wq_sb[:, :, :], wq.rearrange("(k p) n -> p k n", p=P), s_front)
            load(bqk_sb[:, :], bqk, s_front)
            load_ctx(0)
            load(wk_sb[:, :, :], wk.rearrange("(k p) n -> p k n", p=P), s_front)
            load(wv_sb[:, :, :], wv.rearrange("(k p) n -> p k n", p=P), s_front)
            load(bv_sb[:, :], bv.partition_broadcast(P), s_front)
            load(swap_sb[:, :], swap)
            load(wo_sb[:, :, :], wo.rearrange("(g p) n -> p g n", p=P))
            load_x1(0, xa[:, :, :], s_x)
            sp.dma_start(big[0:3 * BLK, 1, 0:2, :], bias_rows.rearrange("q (a n) -> q a n", a=2)).then_inc(s_brow, 16)
            load(w1_sb[:, :, :], w1.rearrange("(k p) n -> p k n", p=P))
            load(w2_sb[:, :, :], w2.rearrange("(k p) n -> p k n", p=P))
            load(gw_sb[:, :, :], gw.rearrange("(k p) n -> p k n", p=P))
            load(gb_sb[:, :], gb.partition_broadcast(P))
            load(lnp_sb[:, :], lnp)
            load(g2_sb[:, :], g2.partition_broadcast(P))
            load(be2_sb[:, :], be2.partition_broadcast(P))
            load(before_sb[:, :], before.partition_broadcast(P))
            load(ones3_sb[:, :], ones3.bitcast(BF16))

            def turn(b, more):
                if more:
                    sp.wait_ge(s_xt, b * TRB + TRB)
                    load_x1(b + 1, stage, s_stage)
                    sp.wait_ge(s_kv, b * 3 + 3)
                    load_ctx(b + 1)
                    sp.wait_ge(s_r, b * TT + TT)
                    load_x1(b + 1, xa[:, :, :], s_x)
                sp.wait_ge(s_fin, b * TT + TT)
                sp.dma_start(out[bass.ds(b * L, L), :].rearrange("(t p) n -> p t n", p=P), acc[:, :, :]).then_inc(s_out, 16)

            turns(sp, turn)
            sp.wait_ge(s_out, 16 + BATCH * 16)

        @block.tensor
        def _(pe):
            def transposes(src, bank, done):
                for u in range(NL * KT):
                    half, k = u // KT, u % KT
                    for i in range(TG):
                        last = nc.tensor.transpose(ps[:, bank + u, i * P:(i + 1) * P],
                                                   src[:, half * TG + i, k * P:(k + 1) * P], ident_sb[:, :])
                    last.then_inc(done, 1)

            def front(b):
                pe.wait_ge(s_stage, b * 16 + 16)
                transposes(stage, 4, s_xt)
                for u in range(U):
                    g, half = u // NL, u % NL
                    if u == 0:
                        pe.wait_ge(s_xtc, b * TRB + TRB)
                    elif u >= 4:
                        pe.wait_ge(s_qc, b * U + u - 3)
                    for k in range(KT):
                        last = nc.tensor.matmul(ps[:, 4 + u % 4, :], wq_sb[:, k, g * P:(g + 1) * P],
                                                x1T[:, k, half * HALF:(half + 1) * HALF],
                                                start=k == 0, stop=k == KT - 1)
                    last.then_inc(s_q, 1)
                pe.wait_ge(s_ctx, b * 16 + 16)
                pe.wait_ge(s_qc, b * U + U)
                for g in range(G):
                    for k in range(KT):
                        last = nc.tensor.matmul(ps[:, 4 + g // 2, (g % 2) * 256:(g % 2) * 256 + S],
                                                wk_sb[:, k, g * P:(g + 1) * P], ctx_sb[:, k, :],
                                                start=k == 0, stop=k == KT - 1)
                last.then_inc(s_kv, 1)
                for k in range(KT):
                    last = nc.tensor.matmul(ps[:, 6, :], ctx_sb[:, k, 0:SM], wv_sb[:, k, :],
                                            start=k == 0, stop=k == KT - 1)
                last.then_inc(s_kv, 1)
                for j in range(HG):
                    for k in range(KT):
                        last = nc.tensor.matmul(
                            ps[BLK * j:BLK * j + SR, 7, 0:P].rearrange("p (g c) -> p g c", c=BLK),
                            ctx_sb[:, k, SM:S],
                            wv_sb[:, k, :].rearrange("p (g j c) -> p g j c", j=HG, c=BLK)[:, :, j, :],
                            start=k == 0, stop=k == KT - 1)
                last.then_inc(s_kv, 1)

            def maxima(b):
                pe.wait_ge(s_kvc, b * KVB + KVB)
                for u in range(TT * G):
                    t, g = u // G, u % G
                    if u >= 4:
                        pe.wait_ge(s_max, b * TT * G + u - 3)
                    for i in range(2):
                        last = nc.tensor.matmul(ps[:, 2 * (u % 4) + i, 0:2 * S], qT[:, g, t * P:(t + 1) * P],
                                                kTm[:, HG * g + 2 * i:HG * g + 2 * i + 2, :], start=True, stop=True)
                    last.then_inc(s_s1, 1)
                pe.wait_ge(s_max, b * TT * G + TT * G)
                for u in range(U):
                    g, half = u // NL, u % NL
                    for i in range(TG):
                        last = nc.tensor.transpose(ps[:, u, i * P:(i + 1) * P], neg[:, (half * TG + i) * G + g, :],
                                                   ident_sb[:, :])
                    last.then_inc(s_mt, 1)


            def turn(b, more):
                def scores(u):
                    g, half = u // NL, u % NL
                    q = qT[:, g, half * HALF:(half + 1) * HALF]
                    for j in range(HG):
                        if u == 0:
                            pe.wait_ge(s_qm, b * U + j + 1)
                        elif j % 2 == 0:
                            pe.wait_ge(s_exp, b * 3 * U + 3 * (u - 1) + j // 2 + 1)
                        last = nc.tensor.matmul(ps[:, j, :], kTm[:, HG * g + j, 0:SM], q, start=True, stop=True)
                        if j % 2:
                            last.then_inc(s_s2, 1)
                    if u == 0:
                        pe.wait_ge(s_qm, b * U + U)
                    else:
                        pe.wait_ge(s_exp, b * 3 * U + 3 * u)
                    nc.tensor.matmul(ps[:, 4, :], kTr[:, g, :], q, start=True, stop=True).then_inc(s_s2, 1)

                def values(u):
                    g = u // NL
                    pe.wait_ge(s_exp, b * 3 * U + 3 * u + 3)
                    if u >= 2:
                        pe.wait_ge(s_raw, b * U + u - 1)
                    nc.tensor.matmul(ps[:, 5 + u % 2, :], v_rem[:, g, :], pT_rem[:, u % 2, :],
                                     start=True, stop=False, skip_group_check=True)
                    for j in range(HG):
                        last = nc.tensor.matmul(ps[BLK * j:BLK * (j + 1), 5 + u % 2, :], v_sb[:, HG * g + j, :],
                                                pT[:, HG * (u % 2) + j, :], start=False, stop=True,
                                                skip_group_check=True)
                    last.then_inc(s_pv, 1)

                def sums(u):
                    pe.wait_ge(s_raw, b * U + u + 1)
                    if u:
                        pe.wait_ge(s_lnd, b * 2 * U + 2 * u - 1)
                    nc.tensor.matmul(ps[:, 7, :], swap_sb[:, :], raw[:, u % 2, :], start=True, stop=True).then_inc(s_den, 1)

                def project(t, groups):
                    for g in groups:
                        last = nc.tensor.matmul(ps[:, t % 4, 0:DM], oT[:, g, t * P:(t + 1) * P], wo_sb[:, g, :],
                                                start=g == 0, stop=g == G - 1)
                    if g == G - 1:
                        last.then_inc(s_proj, 1)

                for u in range(U + 2):
                    if u < U:
                        scores(u)
                    if 1 <= u <= U:
                        values(u - 1)
                    if u == U + 1:
                        pe.wait_ge(s_o, b * U + U - 2)
                        project(0, range(G - 1))
                    if u >= 2:
                        sums(u - 2)
                for t in range(1, TG):
                    project(t, range(G - 1))
                pe.wait_ge(s_o, b * U + U - 1)
                for t in range(TG):
                    project(t, [G - 1])
                pe.wait_ge(s_o, b * U + U)
                for t in range(TG, TT):
                    pe.wait_ge(s_r, b * TT + t - 3)
                    project(t, range(G))
                if more:
                    front(b + 1)
                pe.wait_ge(s_x2, b * TT + TT)
                transposes(xt, 0, s_yt)
                pe.wait_ge(s_ytc, b * TRB + TRB)
                for t in range(TT):
                    if t >= 2:
                        pe.wait_ge(s_l1c, b * TT + t - 1)
                    for h in range(2):
                        dst = ps[:, 2 * (t % 2) + h, :]
                        nc.tensor.matmul(dst, ones3_sb[:, :], brow[:, h * HALF:(h + 1) * HALF], start=True, stop=False)
                        for k in range(KT):
                            last = nc.tensor.matmul(dst, xT[:, k, t * P:(t + 1) * P], w1_sb[:, k, h * HALF:(h + 1) * HALF],
                                                    start=False, stop=k == KT - 1)
                    last.then_inc(s_l1, 1)
                if more:
                    pe.wait_ge(s_kvc, (b + 1) * KVB + KVB)
                for t in range(TT):
                    for k in range(KT):
                        last = nc.tensor.matmul(ps[:, 7, t * E:(t + 1) * E], xT[:, k, t * P:(t + 1) * P], gw_sb[:, k, :],
                                                start=k == 0, stop=k == KT - 1)
                last.then_inc(s_gate, 1)
                for n in range(NT):
                    pe.wait_ge(s_n1, b * TT + TG * (n + 1))

                    def turn_tiles(c):
                        m = n * E * KT + c
                        if m >= 3:
                            pe.wait_ge(s_hc, b * NT * E * KT + m - 2)
                        for i in range(TG):
                            last = nc.tensor.transpose(ps[:, 4 + m % 3, i * P:(i + 1) * P],
                                                       big[:, n, i, c * P:(c + 1) * P], ident_sb[:, :])
                        last.then_inc(s_h, 1)

                    for c in range(2 * KT):
                        turn_tiles(c)
                    for i in range(TG):
                        t = n * TG + i
                        if t >= 2:
                            pe.wait_ge(s_l2c, b * TT + t - 1)
                        else:
                            pe.wait_ge(s_l1c, b * TT + TT)
                        for e in range(E):
                            dst = ps[:, 2 * (t % 2) + e // 2, (e % 2) * DM:(e % 2 + 1) * DM]
                            if i == 0:
                                pe.wait_ge(s_hc, b * NT * E * KT + E * KT * n + KT * (e + 1))
                            if e % 2 == 0:
                                nc.tensor.matmul(ps[:, 2 * (t % 2) + e // 2, :], ones3_sb[:, :],
                                                 brow[:, E * DM + e * DM:E * DM + (e + 2) * DM],
                                                 start=True, stop=False, skip_group_check=True)
                            for k in range(KT):
                                last = nc.tensor.matmul(dst, hT[:, e * KT + k, i * P:(i + 1) * P],
                                                        w2_sb[:, e * KT + k, :], start=False, stop=k == KT - 1,
                                                        skip_group_check=True)
                            if i == 0 and e + 2 < E:
                                for k in range(KT):
                                    turn_tiles((e + 2) * KT + k)
                        last.then_inc(s_l2, 1)
                if more:
                    pe.wait_ge(s_l2c, b * TT + TT)
                    pe.wait_ge(s_gd, b * GDB + 1)
                    maxima(b + 1)

            pe.wait_ge(s_front, FRONT * 16)
            front(0)
            pe.wait_ge(s_prep, 4)
            maxima(0)
            pe.wait_ge(s_const, LOADS * 16)
            pe.wait_ge(s_split, 6)
            turns(pe, turn)

        @block.scalar
        def _(act):
            def copy_transposed(b, dst, bank, ready, done):
                for u in range(NL * KT):
                    half, k = u // KT, u % KT
                    act.wait_ge(ready, b * TRB + u + 1)
                    nc.scalar.activation(dst[:, k, half * HALF:(half + 1) * HALF], ps[:, bank + u, :],
                                         ACT.Copy).then_inc(done, 1)

            def query(b, u):
                g, half = u // NL, u % NL
                act.wait_ge(s_q, b * U + u + 1)
                nc.scalar.activation(qT[:, g, half * HALF:(half + 1) * HALF], ps[:, 4 + u % 4, :], ACT.Identity,
                                     scale=HD ** -0.5, bias=bqk_sb[:, g:g + 1]).then_inc(s_qc, 1)

            def guess(b, n):
                cols = TT if n in (0, NORMS - 1) else TG * E
                act.wait_ge(s_nw, b * NWB + 5 * n + 1)
                nc.scalar.activation(lnv[:, 0:cols], var[:, 0:cols], ACT.Ln).then_inc(s_ln, 1)
                act.wait_ge(s_ln, b * LNB + 2 * n + 1)
                nc.scalar.activation(rstd[:, 0:cols], lnv[:, 0:cols], ACT.Exp, scale=-0.5).then_inc(s_ln, 1)

            def turn(b, more):
                def exps(u):
                    if u >= 2:
                        act.wait_ge(s_pv, b * U + u - 1)
                    for i in range(2):
                        act.wait_ge(s_s2, b * 3 * U + 3 * u + i + 1)
                        nc.scalar.activation(pT[:, HG * (u % 2) + 2 * i:HG * (u % 2) + 2 * i + 2, :],
                                             ps[:, 2 * i:2 * i + 2, :], ACT.Exp).then_inc(s_exp, 1)
                    act.wait_ge(s_s2, b * 3 * U + 3 * u + 3)
                    nc.scalar.activation(pT_rem[:, u % 2, :], ps[:, 4, :], ACT.Exp).then_inc(s_exp, 1)

                def inverse(u):
                    act.wait_ge(s_den, b * U + u + 1)
                    if u >= 2:
                        act.wait_ge(s_o, b * U + u - 1)
                    nc.scalar.activation(lnd[:, u % 2, :], ps[:, 7, :], ACT.Ln).then_inc(s_lnd, 1)
                    act.wait_ge(s_lnd, b * 2 * U + 2 * u + 1)
                    nc.scalar.activation(lnd[:, u % 2, :], lnd[:, u % 2, :], ACT.Exp, scale=-1.0).then_inc(s_lnd, 1)

                for u in range(U + 2):
                    if u < U:
                        exps(u)
                    if u >= 2:
                        inverse(u - 2)
                if more:
                    copy_transposed(b + 1, x1T, 4, s_xt, s_xtc)
                    for u in range(U):
                        query(b + 1, u)
                        if u == 1:
                            guess(b, 0)
                else:
                    guess(b, 0)
                copy_transposed(b, xT, 0, s_yt, s_ytc)
                for t in range(TT):
                    act.wait_ge(s_l1, b * TT + t + 1)
                    nc.scalar.activation(big[:, t // TG, t % TG, :].rearrange("p (a n) -> p a n", a=2),
                                         ps[:, 2 * (t % 2):2 * (t % 2) + 2, :], ACT.Copy).then_inc(s_l1c, 1)
                    if t == TG - 1:
                        guess(b, 1)
                guess(b, 2)
                for n in range(NT):
                    for c in range(E * KT):
                        m = n * E * KT + c
                        act.wait_ge(s_h, b * NT * E * KT + m + 1)
                        if n:
                            act.wait_ge(s_l2, b * TT + TG * n)
                        nc.scalar.activation(hT[:, c, :], ps[:, 4 + m % 3, :], ACT.Relu, scale=lnp_sb[:, c:c + 1],
                                             bias=lnp_sb[:, E * KT + c:E * KT + c + 1]).then_inc(s_hc, 1)
                    for i in range(TG):
                        t = n * TG + i
                        act.wait_ge(s_l2, b * TT + t + 1)
                        nc.scalar.activation(big[:, n, i, :].rearrange("p (a n) -> p a n", a=2),
                                             ps[:, 2 * (t % 2):2 * (t % 2) + 2, :], ACT.Copy).then_inc(s_l2c, 1)
                        if t == TG + 1:
                            guess(b, 3)
                        if t == 0:
                            act.wait_ge(s_gd, b * GDB + 5)
                            nc.scalar.activation(wgt[:, :, :], wgt[:, :, :], ACT.Exp).then_inc(s_ge, 1)
                guess(b, 4)
                act.wait_ge(s_shift, b + 1)
                for i in range(TG):
                    for e in range(E):
                        c = i * E + e
                        tile = big[:, NT - 1, i, e * DM:(e + 1) * DM]
                        last = nc.scalar.activation(tile, tile, ACT.Identity, scale=scale2[:, c:c + 1],
                                                    bias=shift2[:, c:c + 1])
                    last.then_inc(s_n2, 1)
                guess(b, 5)

            act.wait_ge(s_front, FRONT * 16)
            nc.scalar.preload_act_table_set("natural_log_exp_and_others")
            nc.scalar.mul(bqk_sb[:, 0:G], bqk_sb[:, 0:G], HD ** -0.5).then_inc(s_prep, 1)
            copy_transposed(0, x1T, 4, s_xt, s_xtc)
            act.wait_ge(s_prep, 4)
            for u in range(U):
                query(0, u)
            act.wait_ge(s_const, LOADS * 16)
            turns(act, turn)

        @block.gpsimd
        def _(pool):
            nc.gpsimd.memset(kTm[:, :, :], 0.0).then_inc(s_prep, 1)
            nc.gpsimd.memset(kTr[:, :, :], 0.0).then_inc(s_prep, 1)
            nc.gpsimd.memset(v_rem[:, :, :], 0.0).then_inc(s_prep, 1)
            nc.gpsimd.memset(neg, 0.0).then_inc(s_zero, 1)
            nc.gpsimd.memset(zero[:, :], 0.0).then_inc(s_zero1, 1)
            zeros = zero[:, :].unsqueeze(2).to_broadcast([P, TT * G, P])
            pool.wait_ge(s_zero1, 1)
            pool.wait_ge(s_const, LOADS * 16)

            def turn(b, more):
                if more:
                    pool.wait_ge(s_proj, b * TT + TT)
                    nc.gpsimd.tensor_tensor(neg, zeros, zeros, ALU.add).then_inc(s_zero, 1)
                for t in range(TT):
                    tile = big[:, t // TG, t % TG, :]
                    pool.wait_ge(s_n2, b * TT + t + 1)
                    nc.gpsimd.tensor_tensor(tile, tile, g2_sb[:, :], ALU.mult).then_inc(s_gm, 1)
                    pool.wait_ge(s_gm, b * TT + t + 1)
                    pool.wait_ge(s_acc, b * ACB + ACB)
                    for e in range(E):
                        nc.gpsimd.tensor_tensor(acc[:, t, :], acc[:, t, :], tile[:, e * DM:(e + 1) * DM],
                                                ALU.add).then_inc(s_sum, 1)
                        pool.wait_ge(s_sum, b * TT * E + E * t + e + 1)

            turns(pool, turn)

        @block.vector
        def _(dve):
            COUNTS = [TT] + [TG * E] * (2 * NT) + [TT]

            def aggregate(b, n):
                count, at = COUNTS[n], b * NMB + 6 * n
                m, v, w, st = mean[:, 0:count], var[:, 0:count], newt[:, 0:count], stats[:, 0:count, :]
                dve.wait_ge(s_st, b * MVB + sum(COUNTS[:n + 1]))
                nc.vector.tensor_tensor(m, st[:, :, 1], st[:, :, 4], ALU.add).then_inc(s_mv, 1)
                nc.vector.tensor_tensor(w, st[:, :, 1], st[:, :, 4], ALU.subtract).then_inc(s_mv, 1)
                nc.vector.tensor_tensor(v, st[:, :, 2], st[:, :, 5], ALU.add).then_inc(s_mv, 1)
                dve.wait_ge(s_mv, at + 2)
                nc.vector.tensor_tensor(w, w, w, ALU.mult).then_inc(s_mv, 1)
                dve.wait_ge(s_mv, at + 3)
                nc.vector.tensor_scalar(v, v, 1.0 / DM, LN_EPS, ALU.mult, ALU.add).then_inc(s_mv, 1)
                nc.vector.tensor_scalar(m, m, 0.5, None, ALU.mult).then_inc(s_mv, 1)
                dve.wait_ge(s_mv, at + 5)
                nc.vector.scalar_tensor_tensor(out=v, in0=w, scalar=0.25, in1=v, op0=ALU.mult,
                                               op1=ALU.add).then_inc(s_nw, 1)

            def newton(b, n):
                cols, at = COUNTS[n], b * NWB + 5 * n
                v, r, w = var[:, 0:cols], rstd[:, 0:cols], newt[:, 0:cols]
                dve.wait_ge(s_ln, b * LNB + 2 * n + 2)
                nc.vector.tensor_tensor(w, r, r, ALU.mult).then_inc(s_nw, 1)
                dve.wait_ge(s_nw, at + 2)
                nc.vector.tensor_tensor(w, w, v, ALU.mult).then_inc(s_nw, 1)
                dve.wait_ge(s_nw, at + 3)
                nc.vector.tensor_scalar(w, w, -0.5, 1.5, ALU.mult, ALU.add).then_inc(s_nw, 1)
                dve.wait_ge(s_nw, at + 4)
                nc.vector.tensor_tensor(r, r, w, ALU.mult).then_inc(s_nw, 1)
                dve.wait_ge(s_nw, at + 5)

            def keys_values(b):
                dve.wait_ge(s_kv, b * 3 + 3)
                keys = ps[:, 4:6, :].rearrange("p a (g n) -> p (a g) n", n=256)
                for j in range(HG):
                    rows = slice(BLK * j, BLK * (j + 1))
                    heads = kTm[rows, :, :].rearrange("p (g j) n -> p g j n", j=HG)[:, :, j, :]
                    nc.vector.tensor_tensor(heads, keys[rows, :, 0:S],
                                            bqk_sb[rows, G:2 * G].unsqueeze(2).to_broadcast([BLK, G, S]),
                                            ALU.add).then_inc(s_kvc, 1)
                for j in range(HG):
                    rows = slice(BLK * j, BLK * (j + 1))
                    heads = kTm[rows, :, :].rearrange("p (g j) n -> p g j n", j=HG)[:, :, j, :]
                    dve.wait_ge(s_kvc, b * KVB + 1 + j)
                    nc.vector.tensor_copy(kTr[rows, :, BLK * j:BLK * j + SR], heads[:, :, SM:S]).then_inc(s_kvc, 1)
                nc.vector.tensor_tensor(v_sb[:, :, :].rearrange("p h c -> p (h c)"), ps[:, 6, :], bv_sb[:, :],
                                        ALU.add).then_inc(s_kvc, 1)
                for j in range(HG):
                    rows = slice(BLK * j, BLK * j + SR)
                    nc.vector.tensor_tensor(
                        v_rem[rows, :, BLK * j:BLK * (j + 1)], ps[rows, 7, 0:P].rearrange("p (g c) -> p g c", c=BLK),
                        bv_sb[rows, :].rearrange("p (g j c) -> p g j c", j=HG, c=BLK)[:, :, j, :],
                        ALU.add).then_inc(s_kvc, 1)

            def maxima(b, units=range(TT * G)):
                dve.wait_ge(s_zero, b + 1)
                for u in units:
                    t, g = u // G, u % G
                    dve.wait_ge(s_s1, b * TT * G + u + 1)
                    nc.vector.tensor_reduce(neg[:, u, :].rearrange("p (j c) -> p j c", c=BLK)[:, :, HD],
                                            ps[:, 2 * (u % 4):2 * (u % 4) + 2, 0:2 * S].rearrange("p a (h n) -> p a h n", n=S),
                                            AX.X, ALU.max).then_inc(s_max, 1)

            def subtract_maxima(b):
                for u in range(U):
                    g, half = u // NL, u % NL
                    q = qT[:, g, half * HALF:(half + 1) * HALF]
                    dve.wait_ge(s_mt, b * U + u + 1)
                    nc.vector.tensor_tensor(q, q, ps[:, u, :], ALU.subtract).then_inc(s_qm, 1)


            def measure(b, n, ready):
                for i in range(TG):
                    dve.wait_ge(ready, b * TT + TG * n + i + 1)
                    for e in range(E):
                        nc.vector.bn_stats(stats[:, i * E + e, :], big[:, n, i, e * DM:(e + 1) * DM]).then_inc(s_st, 1)

            def weigh(b, n):
                nc.vector.tensor_tensor(scale2[:, :], rstd[:, :],
                                        wgt[:, TG * n:TG * (n + 1), :].rearrange("p t e -> p (t e)"),
                                        ALU.mult).then_inc(s_scale, 1)
                dve.wait_ge(s_scale, b * NT + n + 1)

            def normalise(n, scales, done):
                for i in range(TG):
                    for e in range(E):
                        c = i * E + e
                        tile = big[:, n, i, e * DM:(e + 1) * DM]
                        last = nc.vector.tensor_scalar(tile, tile, mean[:, c:c + 1], scales[:, c:c + 1],
                                                       ALU.subtract, ALU.mult)
                    last.then_inc(done, 1)

            def turn(b, more):
                def take(u):
                    dve.wait_ge(s_pv, b * U + u + 1)
                    if u >= 2:
                        dve.wait_ge(s_o, b * U + u - 1)
                    nc.vector.tensor_copy(raw[:, u % 2, :], ps[:, 5 + u % 2, :]).then_inc(s_raw, 1)

                def divide(u):
                    g, half = u // NL, u % NL
                    dve.wait_ge(s_lnd, b * 2 * U + 2 * u + 2)
                    nc.vector.tensor_tensor(oT[:, g, half * HALF:(half + 1) * HALF], raw[:, u % 2, :], lnd[:, u % 2, :],
                                            ALU.mult).then_inc(s_o, 1)

                for u in range(U + 2):
                    if u >= 2:
                        divide(u - 2)
                    if u < U:
                        take(u)
                dve.wait_ge(s_x, b * 16 + 16)
                for t in range(TT):
                    dve.wait_ge(s_proj, b * TT + t + 1)
                    nc.vector.tensor_tensor(xt[:, t, :], xa[:, t, :], ps[:, t % 4, 0:DM], ALU.add).then_inc(s_r, 1)
                    dve.wait_ge(s_r, b * TT + t + 1)
                    nc.vector.bn_stats(stats[:, t, :], xt[:, t, :]).then_inc(s_st, 1)
                aggregate(b, 0)
                newton(b, 0)
                for t in range(TT):
                    nc.vector.tensor_scalar(xt[:, t, :], xt[:, t, :], mean[:, t:t + 1], rstd[:, t:t + 1],
                                            ALU.subtract, ALU.mult).then_inc(s_x2, 1)
                if more:
                    keys_values(b + 1)
                for n in range(NT):
                    measure(b, n, s_l1c)
                    aggregate(b, 1 + n)
                    newton(b, 1 + n)
                    normalise(n, rstd, s_n1)
                gd = b * GDB
                dve.wait_ge(s_gate, b + 1)
                nc.vector.tensor_tensor(sc[:, :, :], ps[:, 7, 0:TT * E].rearrange("p (t e) -> p t e", e=E),
                                        gb_sb[:, :].unsqueeze(1).to_broadcast([P, TT, E]), ALU.add).then_inc(s_gd, 1)
                dve.wait_ge(s_gd, gd + 1)
                own = sc[:, :, :].unsqueeze(3).to_broadcast([P, TT, E, E])
                other = sc[:, :, :].unsqueeze(2).to_broadcast([P, TT, E, E])
                nc.vector.tensor_reduce(smax[:, :], sc[:, :, :], AX.X, ALU.max).then_inc(s_gd, 1)
                nc.vector.tensor_tensor(cmp1[:, :, :, :], other, own, ALU.is_gt).then_inc(s_gd, 1)
                nc.vector.tensor_tensor(cmp2[:, :, :, :], other, own, ALU.is_equal).then_inc(s_gd, 1)
                dve.wait_ge(s_gd, gd + 2)
                nc.vector.tensor_tensor(wgt[:, :, :], sc[:, :, :], smax[:, :].unsqueeze(2).to_broadcast([P, TT, E]),
                                        ALU.subtract).then_inc(s_gd, 1)
                flat1 = cmp1[:, :, :, :].rearrange("p t e f -> p t (e f)")
                flat2 = cmp2[:, :, :, :].rearrange("p t e f -> p t (e f)")
                dve.wait_ge(s_gd, gd + 4)
                nc.vector.tensor_tensor(flat2, flat2, before_sb[:, :].unsqueeze(1).to_broadcast([P, TT, E * E]),
                                        ALU.mult).then_inc(s_gd, 1)
                dve.wait_ge(s_gd, gd + 6)
                nc.vector.tensor_tensor(flat1, flat1, flat2, ALU.add).then_inc(s_gd, 1)
                dve.wait_ge(s_gd, gd + 7)
                nc.vector.tensor_reduce(rank[:, :, :].rearrange("p t e -> p (t e)"),
                                        cmp1[:, :, :, :].rearrange("p t e f -> p (t e) f"), AX.X,
                                        ALU.add).then_inc(s_gd, 1)
                dve.wait_ge(s_ge, b + 1)
                dve.wait_ge(s_gd, gd + 8)
                nc.vector.scalar_tensor_tensor(out=wgt[:, :, :], in0=rank[:, :, :], scalar=1.5, in1=wgt[:, :, :],
                                               op0=ALU.is_lt, op1=ALU.mult).then_inc(s_gd, 1)
                dve.wait_ge(s_gd, gd + 9)
                nc.vector.tensor_reduce(wsum[:, :], wgt[:, :, :], AX.X, ALU.add).then_inc(s_gd, 1)
                dve.wait_ge(s_gd, gd + 10)
                nc.vector.reciprocal(wsum[:, :], wsum[:, :]).then_inc(s_gd, 1)
                dve.wait_ge(s_gd, gd + 11)
                nc.vector.tensor_tensor(wgt[:, :, :], wgt[:, :, :], wsum[:, :].unsqueeze(2).to_broadcast([P, TT, E]),
                                        ALU.mult).then_inc(s_gd, 1)
                dve.wait_ge(s_gd, gd + 12)
                dve.wait_ge(s_out, b * 16 + 16)
                for t in range(TT):
                    nc.vector.tensor_scalar(acc[:, t, :], xt[:, t, :], 2.0, None, ALU.mult).then_inc(s_acc, 1)
                for e in range(E):
                    for t in range(TT):
                        dve.wait_ge(s_acc, b * ACB + TT * e + t + 1)
                        nc.vector.scalar_tensor_tensor(out=acc[:, t, :], in0=be2_sb[:, e * DM:(e + 1) * DM],
                                                       scalar=wgt[:, t, e:e + 1], in1=acc[:, t, :], op0=ALU.mult,
                                                       op1=ALU.add).then_inc(s_acc, 1)

                for n in range(NT):
                    measure(b, n, s_l2c)
                    if more and n == NT - 1:
                        maxima(b + 1, range(0, 4))
                    aggregate(b, 1 + NT + n)
                    if more and n == NT - 1:
                        maxima(b + 1, range(4, 8))
                    newton(b, 1 + NT + n)
                    weigh(b, n)
                    if n < NT - 1:
                        normalise(n, scale2, s_n2)
                nc.vector.scalar_tensor_tensor(out=shift2[:, :], in0=mean[:, :], scalar=-1.0, in1=scale2[:, :],
                                               op0=ALU.mult, op1=ALU.mult).then_inc(s_shift, 1)
                if more:
                    maxima(b + 1, range(8, TT * G))
                    subtract_maxima(b + 1)
                for t in range(TT):
                    dve.wait_ge(s_sum, b * TT * E + E * (t + 1))
                    nc.vector.bn_stats(stats[:, t, :], acc[:, t, :]).then_inc(s_st, 1)
                aggregate(b, NORMS - 1)
                newton(b, NORMS - 1)
                for t in range(TT):
                    nc.vector.tensor_scalar(acc[:, t, :], acc[:, t, :], mean[:, t:t + 1], rstd[:, t:t + 1],
                                            ALU.subtract, ALU.mult).then_inc(s_fin, 1)

            dve.sem_inc(s_out, 16)
            dve.wait_ge(s_front, FRONT * 16)
            dve.wait_ge(s_prep, 4)
            keys_values(0)
            maxima(0)
            subtract_maxima(0)
            dve.wait_ge(s_const, LOADS * 16)
            dve.wait_ge(s_brow, 16)
            row = big[0:3 * BLK, 1, 0:2, :].rearrange("p a n -> p (a n)")
            left = big[0:3 * BLK, 1, 2:4, :].rearrange("p a n -> p (a n)")
            nc.vector.tensor_copy(brow[:, :], row).then_inc(s_split, 1)
            dve.wait_ge(s_split, 1)
            nc.vector.tensor_tensor(left, row, brow[:, :], ALU.subtract).then_inc(s_split, 1)
            dve.wait_ge(s_split, 2)
            for q in (1, 2):
                nc.vector.tensor_copy(brow[BLK * q:BLK * q + BLK, :], left[BLK * q:BLK * q + BLK, :]).then_inc(s_split, 1)
            dve.wait_ge(s_split, 4)
            nc.vector.tensor_tensor(left[2 * BLK:3 * BLK, :], left[2 * BLK:3 * BLK, :], brow[2 * BLK:3 * BLK, :],
                                    ALU.subtract).then_inc(s_split, 1)
            dve.wait_ge(s_split, 5)
            nc.vector.tensor_copy(brow[2 * BLK:3 * BLK, :], left[2 * BLK:3 * BLK, :]).then_inc(s_split, 1)
            dve.wait_ge(s_split, 6)
            turns(dve, turn)


def decoder_block(nc, x, xT, w_in, w_x, w_out, par, ident, sel_bc, sel_p, ctxT, wq, wk, wv, wo, bqk, bv, swap,
                  w1, w2, gw, gb, lnp, bias_rows, ones3, g2, be2, before, out):
    c_dram = nc.dram_tensor("c_scratch", (NCH * NS, TC), F32).ap()
    x1 = nc.dram_tensor("x1_scratch", (BATCH * L, DM), F32).ap()
    mamba_block(nc, x, xT, w_in, w_x, w_out, par, ident, sel_bc, sel_p, c_dram, x1)
    attn_ffn_block(nc, x1, ctxT, wq, wk, wv, wo, bqk, bv, ident, swap, w1, w2, gw, gb, lnp, bias_rows, ones3,
                   g2, be2, before, out)


def _constants():
    one = 0x3F80
    sel_bc = np.zeros((PARTS * BC, NS, P), np.uint16)
    for q in range(PARTS):
        for n in range(NS):
            sel_bc[BC * q + n, n, :] = one
    sel_p = np.zeros((PROJ, P), np.float32)
    sel_p[PROJ - 1] = 1
    swap = np.zeros((P, P), np.float32)
    for j in range(HG):
        for i in range(HD):
            swap[BLK * j + HD + i, BLK * j + i] = 1
            swap[BLK * j + HD + i, BLK * j + HD + i] = 1
    ones3 = np.zeros((3 * BLK, P), np.uint16)
    ones3[0::BLK] = one
    before = np.tri(E, k=-1, dtype=np.float32).reshape(E * E)
    return dict(ident=np.eye(P, dtype=np.float32), sel_bc=sel_bc, sel_p=sel_p, swap=swap, ones3=ones3, before=before)


def _layout(inputs):
    f32 = np.float32
    attn = lambda n: np.asarray(inputs["L0_attn_" + n])
    xatt = lambda n: np.asarray(inputs["L0_xattn_" + n])
    ffn = lambda n: np.asarray(inputs["L0_ffn_" + n])
    per_channel = lambda a: a.reshape(CT, P, -1).transpose(1, 0, 2).reshape(P, -1)

    def heads(w, spare=0):
        o = np.zeros(w.shape[:-1] + (BLK,), f32)
        o[..., :HD] = w
        if spare:
            o[..., HD:HD + spare] = 1
        return o.reshape(w.shape[:-2] + (NH * BLK,))

    x = np.asarray(inputs["x"]).reshape(BATCH * L, DM)
    par = np.zeros((P, PAR_COLS), f32)
    par[:, 0:PAR_COLS] = np.concatenate([per_channel(attn(n)) for n in
                                         ("A_log", "conv_w", "conv_b", "D_param", "W_dt", "b_dt")], 1)
    w_x = attn("W_x").T
    wo = np.zeros((NH, BLK, DM), f32)
    wo[:, :HD] = xatt("Wo")
    wo[0, HD] = xatt("bo")
    bias_rows = np.zeros((3 * BLK, 2 * E * DM), f32)
    bias_rows[0::BLK] = np.concatenate([ffn("b1").reshape(-1), ffn("b2").reshape(-1)])
    return dict(
        x=x, xT=x.T, w_in=attn("W_in").T,
        w_x=np.concatenate([w_x[:, :BC]] * PARTS + [w_x[:, BC:]], 1), w_out=attn("W_out").T, par=par,
        ctxT=np.asarray(inputs["ctx_1024"]).reshape(BATCH * S, DM).T,
        wq=heads(xatt("Wq")), wk=heads(xatt("Wk")), wv=heads(xatt("Wv")), wo=wo.reshape(NH * BLK, DM),
        bqk=np.concatenate([heads(xatt("bq")).reshape(G, P).T, heads(xatt("bk"), 1).reshape(G, P).T], 1),
        bv=heads(xatt("bv"), HD),
        w1=ffn("W1").transpose(1, 0, 2).reshape(DM, E * DM), w2=ffn("W2").reshape(E * DM, DM),
        gw=ffn("gate_W"), gb=ffn("gate_b"),
        lnp=np.concatenate([ffn("g1").reshape(E * KT, P).T, ffn("be1").reshape(E * KT, P).T], 1),
        bias_rows=bias_rows, g2=ffn("g2").reshape(-1), be2=ffn("be2").reshape(-1), **_constants())


_ARGS = ["x", "xT", "w_in", "w_x", "w_out", "par", "ident", "sel_bc", "sel_p", "ctxT", "wq", "wk", "wv", "wo",
         "bqk", "bv", "swap", "w1", "w2", "gw", "gb", "lnp", "bias_rows", "ones3", "g2", "be2", "before"]


def kernel(**inputs):
    import concourse.bacc as bacc
    from concourse.bass_utils import run_bass_kernel_spmd
    nc = bacc.Bacc("TRN2", target_bir_lowering=False, num_devices=1)
    data = _layout(inputs)
    arrays, args = {}, []
    for name in _ARGS:
        a = np.ascontiguousarray(data[name])
        arrays["in_" + name] = a
        args.append(nc.dram_tensor("in_" + name, a.shape, mybir.dt.from_np(a.dtype), kind="ExternalInput").ap())
    out = nc.dram_tensor("out_x", (BATCH * L, DM), F32, kind="ExternalOutput").ap()
    decoder_block(nc, *args, out)
    r = run_bass_kernel_spmd(nc, [arrays], core_ids=[0])
    return r.results[0]["out_x"].reshape(BATCH, L, DM)
```

```python
import concourse.bass as bass
from concourse import mybir
from contextlib import ExitStack
import numpy as np

F32 = mybir.dt.float32
BF16 = mybir.dt.bfloat16
ALU = mybir.AluOpType
ACT = mybir.ActivationFunctionType
AX = mybir.AxisListType

P = 128
BATCH, L, DM = 4, 1024, 256
DI, NS, TAPS = 512, 16, 4
CT = DI // P
KT = DM // P
HALF = 512
TT = L // P
TC = 256
HALO = TAPS - 1
CPB = L // TC
NCH = BATCH * CPB
CTT = TC // P
PARTS = 3
BC = 2 * NS
PROJ = PARTS * BC + 1
LN_EPS = 1e-5

PAR = {"A_log": (0, NS), "conv_w": (64, TAPS), "conv_b": (80, 1), "D": (84, 1), "W_dt": (88, 1), "b_dt": (92, 1)}
PAR_COLS = 96
NL = L // HALF
NH, HD, S = 16, 16, 154
BLK = 32
HG = P // BLK
G = NH // HG
SM = P
SR = S - SM
E = 4
TG = 4


def mamba_block(nc, x, xT, w_in, w_x, w_out, par, ident_sb, ident, sel_bc, sel_p, c_dram, x1, ahead, s_ahead):
    with ExitStack() as ctx:
        def sb(name, shape, dt=F32):
            return ctx.enter_context(nc.sbuf_tensor(name, shape, dt))

        def sem(name):
            return ctx.enter_context(nc.semaphore(name))

        RING = 4
        LAG = 2

        w_in_sb = sb("w_in_sb", [P, KT, 2 * DI])
        w_x_sb = sb("w_x_sb", [P, CT, PROJ])
        w_out_sb = sb("w_out_sb", [P, CT, DM])
        par_sb = sb("par_sb", [P, PAR_COLS])
        negA = sb("negA", [P, CT * NS])
        diag_D = sb("diag_D", [P, CT, P])
        sel_bc_sb = sb("sel_bc_sb", [PARTS * BC, NS, P], BF16)
        sel_p_sb = sb("sel_p_sb", [PROJ, P])
        xT_sb = sb("xT_sb", [P, 2, KT, HALO + TC])
        xs = sb("xs", [P, 2, CT, TC])
        x_raw = sb("x_raw", [P, CT, HALO + TC])
        tnh = sb("tnh", [P, CT, TC])
        tnh_z = sb("tnh_z", [P, CT, TC])
        gate = sb("gate", [P, 2, CT, TC])
        relu = sb("relu", [P, CT, TC])
        dt_sb = sb("dt_sb", [P, 2, CT, TC])
        u_sb = sb("u_sb", [P, 2, CT, TC])
        c_bc = sb("c_bc", [P, 2, NS, TC])
        decay = sb("decay", [P, RING, CT, TC])
        state = sb("state", [P, RING, CT, TC])
        state_c = sb("state_c", [P, RING, CT, TC])
        carry = sb("carry", [P, NS, CT])
        rest = sb("rest", [PARTS * BC, TC])
        proj = sb("proj", [PROJ, 2, TC])
        parts = sb("parts", [PARTS * BC, 2, TC], BF16)
        y_sb = sb("y_sb", [P, CT, TC])
        res = sb("res", [P, 2, CTT, DM])
        stats = sb("stats", [P, CTT, 6])
        mean = sb("mean", [P, CTT])
        var = sb("var", [P, CTT])
        lnv = sb("lnv", [P, CTT])
        rstd = sb("rstd", [P, CTT])
        newt = sb("newt", [P, CTT])
        shift_sb = sb("shift_sb", [P, CTT])
        coef = sb("coef", [P, 5, CTT])

        def bank(name, n=1):
            return ctx.enter_context(nc.psum_tensor(name, [P, n * HALF], F32))

        b_ps = [bank("b_ps0"), bank("b_ps1")]
        bu_ps = [bank(f"bu_ps{k}") for k in range(3)]
        y_ps = bank("y_ps", 2)
        w_ps = bank("w_ps")

        def col(name, j, k=0):
            first, per = PAR[name]
            return par_sb[:, first + j * per + k:first + j * per + k + 1]

        s_in_w = sem("s_in_w")
        s_const = sem("s_const")
        s_xT = [sem(f"s_xT{q}") for q in range(2)]
        s_res = [sem(f"s_res{q}") for q in range(2)]
        s_cb = [[sem(f"s_cb{q}{h}") for h in range(2)] for q in range(2)]
        s_x1 = [sem(f"s_x1{q}") for q in range(2)]
        s_cst = sem("s_cst")
        s_par = sem("s_par")
        s_coef = sem("s_coef")
        s_in = sem("s_in")
        s_conv0 = sem("s_conv0")
        s_conv = sem("s_conv")
        s_tanh = sem("s_tanh")
        s_silu = sem("s_silu")
        s_gate = sem("s_gate")
        s_proj = sem("s_proj")
        s_projc = sem("s_projc")
        s_split = sem("s_split")
        s_step = sem("s_step")
        s_abs = sem("s_abs")
        s_sp = sem("s_sp")
        s_dt = sem("s_dt")
        s_u = sem("s_u")
        s_b = sem("s_b")
        s_decay = sem("s_decay")
        s_bu = sem("s_bu")
        s_scan = sem("s_scan")
        s_carry = sem("s_carry")
        s_sc = sem("s_sc")
        s_sum = sem("s_sum")
        s_y = sem("s_y")
        s_out = sem("s_out")
        s_r = sem("s_r")
        s_st = sem("s_st")
        s_mv = sem("s_mv")
        s_nw = sem("s_nw")
        s_ln = sem("s_ln")
        s_norm = sem("s_norm")

        def at(i, per, more=0):
            b, r = i
            return r * per + more if b is None else b * (CPB * per) + (r * per + more)

        def shift(i, n):
            return (i[0], i[1] + n)

        def is_first(i):
            return i[0] is None and i[1] == 0

        def loads(i):
            b, r = i
            n = 16 * (r // 2 + 1)
            return n if b is None else b * (16 * CPB // 2) + n

        def tokens(i, more=0, count=TC):
            return bass.ds(at(i, TC, more), count)

        def turns(eng, turn):
            turn((None, 0), prepare=True, finish=False, settle=False)
            turn((None, 1), prepare=True, finish=True, settle=False)
            with eng.Fori(0, BATCH - 1) as b:
                for r in range(2, CPB + 2):
                    turn((b, r), prepare=True, finish=True, settle=True)
            for r in range(NCH - CPB + 2, NCH):
                turn((None, r), prepare=r + 1 < NCH, finish=True, settle=True)

        block = ctx.enter_context(nc.Block())

        @block.sync
        def _(sp):
            def load_xT(k):
                q, skip = k[1] % 2, HALO if k[1] % CPB == 0 else 0
                sp.dma_start(xT_sb[:, q, :, skip:],
                             xT[:, tokens(k, skip - HALO, HALO + TC - skip)].rearrange("(k p) n -> p k n", p=P))\
                  .then_inc(s_xT[q], 16)

            def load_res(k):
                q = k[1] % 2
                sp.dma_start(res[:, q, :, :], x[tokens(k), :].rearrange("(t p) n -> p t n", p=P)).then_inc(s_res[q], 16)

            def load_c(k):
                q = k[1] % 2
                sp.wait_ge(s_projc, at(k, 2, 1))
                sp.dma_start(c_dram[bass.ds(at(k, NS), NS), :], proj[NS:BC, q, :]).then_inc(s_cst, 16)
                count = at(k, 16, 16)
                sp.wait_ge(s_cst, count)
                sp.wait_ge(s_y, count)
                for h in range(2):
                    n = NS // 2
                    sp.dma_start(c_bc[:, q, h * n:(h + 1) * n, :],
                                 c_dram[bass.ds(at(k, NS, h * n), n), :].partition_broadcast(P)).then_inc(s_cb[q][h], 16)

            def turn(i, prepare, finish, settle):
                k = shift(i, 1)
                if i[0] is not None or i[1] + 2 < NCH:
                    sp.wait_ge(s_in, at(i, 6, 6))
                    load_xT(shift(i, 2))
                if prepare:
                    load_c(k)
                if settle:
                    store_x1(shift(i, -2))
                    sp.wait_ge(s_x1[i[1] % 2], loads(shift(i, -2)))
                    load_res(i)

            def store_x1(k):
                q = k[1] % 2
                sp.wait_ge(s_norm, at(k, CTT, 2 * CTT))
                sp.dma_start(x1[tokens(k), :].rearrange("(t p) n -> p t n", p=P), res[:, q, :, :]).then_inc(s_x1[q], 16)

            sp.dma_start(w_in_sb[:, :, :], w_in.rearrange("(k p) n -> p k n", p=P)).then_inc(s_in_w, 16)
            load_xT((None, 0))
            sp.dma_start(par_sb[:, :], par).then_inc(s_in_w, 16)
            sp.dma_start(w_x_sb[:, :, :], w_x.rearrange("(k p) n -> p k n", p=P)).then_inc(s_const, 16)
            sp.dma_start(sel_p_sb[:, :], sel_p).then_inc(s_const, 16)
            sp.dma_start(sel_bc_sb[:, :, :], sel_bc.bitcast(BF16)).then_inc(s_const, 16)
            sp.dma_start(ident_sb[:, :], ident).then_inc(s_const, 16)
            sp.dma_start(w_out_sb[:, :, :], w_out.rearrange("(k p) n -> p k n", p=P)).then_inc(s_const, 16)
            load_xT((None, 1))
            load_res((None, 0))
            load_res((None, 1))
            load_c((None, 0))
            for dst, src in ahead:
                sp.dma_start(dst, src).then_inc(s_ahead, 16)
            turns(sp, turn)
            store_x1((None, NCH - 2))
            store_x1((None, NCH - 1))
            sp.wait_ge(s_x1[0], 16 * NCH // 2)
            sp.wait_ge(s_x1[1], 16 * NCH // 2)

        @block.tensor
        def _(pe):
            def x_tile(k, j):
                q, skip = k[1] % 2, HALO if k[1] % CPB == 0 else 0
                if j == 0:
                    pe.wait_ge(s_xT[q], loads(k))
                    if not is_first(k):
                        pe.wait_ge(s_abs, at(k, 2 * CT, 0))
                        pe.wait_ge(s_r, at(k, CTT, 0))
                else:
                    pe.wait_ge(s_conv0, at(k, 2 * CT, 2 * j))
                for c in range(KT):
                    last = nc.tensor.matmul(w_ps[:, skip:HALO + TC], w_in_sb[:, c, j * P:(j + 1) * P],
                                            xT_sb[:, q, c, skip:HALO + TC], start=c == 0, stop=c == KT - 1)
                last.then_inc(s_in, 1)

            def z_pair(k, h):
                if h == 0:
                    pe.wait_ge(s_conv0, at(k, 2 * CT, 2 * CT))
                else:
                    pe.wait_ge(s_gate, at(k, 2, 1))
                for e in range(2):
                    m = CT + 2 * h + e
                    for c in range(KT):
                        last = nc.tensor.matmul(w_ps[:, e * TC:(e + 1) * TC], w_in_sb[:, c, m * P:(m + 1) * P],
                                                xT_sb[:, k[1] % 2, c, HALO:HALO + TC], start=c == 0, stop=c == KT - 1)
                last.then_inc(s_in, 1)

            def project(k):
                pe.wait_ge(s_silu, at(k, 1, 1))
                pe.wait_ge(s_gate, at(k, 2, 2))
                for j in range(CT):
                    last = nc.tensor.matmul(w_ps[0:PROJ, 0:TC], w_x_sb[:, j, :], xs[:, k[1] % 2, j, :],
                                            start=j == 0, stop=j == CT - 1)
                last.then_inc(s_proj, 1)

            def step_row(k):
                pe.wait_ge(s_projc, at(k, 2, 2))
                nc.tensor.matmul(w_ps[:, 0:TC], sel_p_sb[:, :], proj[:, k[1] % 2, :], start=True, stop=True)\
                  .then_inc(s_step, 1)

            def out_tile(k, t):
                if t == 0:
                    more = k[0] is not None or k[1] + 2 < NCH
                    pe.wait_ge(s_y, at(k, 16, 48))
                    pe.wait_ge(s_abs, at(k, 2 * CT, 6 * CT) if more else 2 * CT * NCH)
                else:
                    pe.wait_ge(s_r, at(k, CTT, 2 * CTT + 1))
                for j in range(CT):
                    nc.tensor.matmul(w_ps[:, 0:DM], y_sb[:, j, t * P:(t + 1) * P], w_out_sb[:, j, :],
                                     start=j == 0, stop=False)
                if t == 0:
                    pe.wait_ge(s_res[k[1] % 2], loads(k))
                nc.tensor.matmul(w_ps[:, 0:DM], ident_sb[:, :], res[:, k[1] % 2, t, :], start=False, stop=True)\
                  .then_inc(s_out, 1)

            def b_row(i, n):
                if n == 0:
                    pe.wait_ge(s_split, at(i, 5, 5))
                pe.wait_ge(s_bu, at(i, 2 * NS, 2 * n + 2))
                nc.tensor.matmul(b_ps[n % 2][:, 0:TC], sel_bc_sb[:, n, :], parts[:, i[1] % 2, :], start=True, stop=True)\
                  .then_inc(s_b, 1)

            def add_state(i, n):
                if n == 0:
                    pe.wait_ge(s_y, at(i, 16, 32))
                if n == 1:
                    for j in range(CT):
                        nc.tensor.matmul(y_ps[:, j * TC:(j + 1) * TC], diag_D[:, j, :], xs[:, i[1] % 2, j, :],
                                         start=False, stop=False, skip_group_check=True)
                pe.wait_ge(s_sc, at(i, NS, RING + n + 1))
                for h in range(2):
                    last = nc.tensor.matmul(y_ps[:, h * HALF:(h + 1) * HALF], ident_sb[:, :],
                                            state_c[:, n % RING, 2 * h:2 * h + 2, :],
                                            start=n == 0, stop=n == NS - 1)
                last.then_inc(s_sum, 1)

            def turn(i, prepare, finish, settle):
                k, last = shift(i, 1), shift(i, -1)
                for n in range(NS):
                    if n + 2 < NS:
                        b_row(i, n + 2)
                    elif prepare:
                        b_row(k, n + 2 - NS)
                    if n >= LAG:
                        add_state(i, n - LAG)
                    elif finish:
                        add_state(last, NS + n - LAG)
                    if prepare:
                        if n < CT:
                            x_tile(k, n)
                        if n == 4:
                            z_pair(k, 0)
                        if n == 6:
                            z_pair(k, 1)
                        if n == 8:
                            project(k)
                            step_row(k)
                    if finish:
                        if n == 11:
                            out_tile(last, 0)
                        if n == 12:
                            out_tile(last, 1)

            pe.sem_inc(s_r, 2 * CTT)
            pe.wait_ge(s_in_w, 2 * 16)
            first = (None, 0)
            for j in range(CT):
                x_tile(first, j)
            z_pair(first, 0)
            z_pair(first, 1)
            pe.wait_ge(s_const, 5 * 16)
            project(first)
            step_row(first)
            b_row(first, 0)
            b_row(first, 1)
            pe.wait_ge(s_par, 3 + CT)
            turns(pe, turn)
            for n in range(NS - LAG, NS):
                add_state((None, NCH - 1), n)
            out_tile((None, NCH - 1), 0)
            out_tile((None, NCH - 1), 1)

        @block.scalar
        def _(act):
            def first_tap(k, j):
                act.wait_ge(s_in, at(k, 6, j + 1))
                if j == 0 and (k[0] is not None or k[1] >= 2):
                    act.wait_ge(s_sum, at(k, NS, RING + 2 - 2 * NS))
                if not is_first(k):
                    act.wait_ge(s_conv, at(k, 3 * CT, 3 * (j + 1 - CT)))
                skip = HALO if k[1] % CPB == 0 else 0
                nc.scalar.activation(x_raw[:, j, skip:], w_ps[:, skip:HALO + TC], ACT.Copy).then_inc(s_conv0, 1)
                nc.scalar.activation(xs[:, k[1] % 2, j, :], w_ps[:, HALO:HALO + TC], ACT.Identity,
                                     scale=col("conv_w", j, TAPS - 1), bias=col("conv_b", j)).then_inc(s_conv0, 1)

            def tanh_x(k):
                act.wait_ge(s_conv, at(k, 3 * CT, 3 * CT))
                if not is_first(k):
                    act.wait_ge(s_silu, at(k, 1, 0))
                nc.scalar.activation(tnh[:, :, :], xs[:, k[1] % 2, :, :], ACT.Tanh).then_inc(s_tanh, 1)
                act.wait_ge(s_tanh, at(k, 4, 2))
                nc.scalar.activation(tnh[:, :, :], tnh[:, :, :], ACT.Copy, bias=1.0).then_inc(s_tanh, 1)

            def tanh_z(k, h):
                if h == 0:
                    nc.scalar.preload_act_table_set("exp_and_others")
                act.wait_ge(s_in, at(k, 6, CT + h + 1))
                nc.scalar.activation(tnh_z[:, 2 * h:2 * h + 2, :], w_ps[:, :], ACT.Tanh, scale=0.5).then_inc(s_tanh, 1)

            def copies(k):
                act.wait_ge(s_proj, at(k, 1, 1))
                nc.scalar.activation(proj[:, k[1] % 2, :], w_ps[0:PROJ, 0:TC], ACT.Copy).then_inc(s_projc, 1)
                nc.scalar.activation(parts[:, k[1] % 2, :], w_ps[0:PARTS * BC, 0:TC], ACT.Copy).then_inc(s_projc, 1)

            def terms(k, j):
                if j == 0:
                    act.wait_ge(s_step, at(k, 1, 1))
                nc.scalar.activation(dt_sb[:, k[1] % 2, j, :], w_ps[:, 0:TC], ACT.Abs,
                                     scale=col("W_dt", j), bias=col("b_dt", j)).then_inc(s_abs, 1)
                nc.scalar.activation(relu[:, j, :], w_ps[:, 0:TC], ACT.Relu,
                                     scale=col("W_dt", j), bias=col("b_dt", j)).then_inc(s_abs, 1)

            def softplus(k):
                d = dt_sb[:, k[1] % 2, :, :]
                act.wait_ge(s_abs, at(k, 2 * CT, 2 * CT))
                nc.scalar.activation(d, d, ACT.Exp, scale=-1.0).then_inc(s_sp, 1)
                nc.scalar.preload_act_table_set("natural_log_exp_and_others")
                act.wait_ge(s_sp, at(k, 2, 1))
                nc.scalar.activation(d, d, ACT.Ln, bias=1.0).then_inc(s_sp, 1)

            def take_sum(k, t):
                act.wait_ge(s_out, at(k, CTT, t + 1))
                nc.scalar.activation(res[:, k[1] % 2, t, :], w_ps[:, 0:DM], ACT.Copy).then_inc(s_r, 1)

            def normalise(k):
                act.wait_ge(s_nw, at(k, 7, 7))
                for t in range(CTT):
                    tile = res[:, k[1] % 2, t, :]
                    nc.scalar.activation(tile, tile, ACT.Identity, scale=rstd[:, t:t + 1],
                                         bias=shift_sb[:, t:t + 1]).then_inc(s_norm, 1)

            def guess(k):
                act.wait_ge(s_nw, at(k, 7, 1))
                nc.scalar.activation(lnv[:, :], var[:, :], ACT.Ln).then_inc(s_ln, 1)
                act.wait_ge(s_ln, at(k, 2, 1))
                nc.scalar.activation(rstd[:, :], lnv[:, :], ACT.Exp, scale=-0.5).then_inc(s_ln, 1)

            def step(i, n):
                for j in range(CT):
                    if j == 0:
                        if n == 0:
                            act.wait_ge(s_dt, at(i, 1, 1))
                        act.wait_ge(s_scan, at(i, NS * CT, n * CT + CT))
                        if n >= RING or not is_first(i):
                            nc.scalar.activation(carry[:, (n - RING) % NS, :], state[:, n % RING, :, TC - 1],
                                                 ACT.Copy).then_inc(s_carry, 1)
                    nc.scalar.activation(decay[:, n % RING, j, :], dt_sb[:, i[1] % 2, j, :], ACT.Exp,
                                         scale=negA[:, j * NS + n:j * NS + n + 1]).then_inc(s_decay, 1)

            def turn(i, prepare, finish, settle):
                k = shift(i, 1)
                for n in range(NS):
                    step(i, n)
                    if prepare:
                        if 3 <= n < 3 + CT:
                            first_tap(k, n - 3)
                        if n == 7:
                            tanh_z(k, 0)
                            tanh_x(k)
                        if n == 9:
                            tanh_z(k, 1)
                        if n == 12:
                            copies(k)
                            for j in range(CT):
                                terms(k, j)
                            softplus(k)
                    if settle:
                        if n == 2:
                            guess(shift(i, -2))
                        if n == 8:
                            normalise(shift(i, -2))
                    if finish:
                        if n == 14:
                            take_sum(shift(i, -1), 0)
                        if n == 15:
                            take_sum(shift(i, -1), 1)

            act.sem_inc(s_scan, RING * CT)
            act.sem_inc(s_y, 32)
            act.wait_ge(s_in_w, 2 * 16)
            nc.scalar.activation(negA[:, :], par_sb[:, 0:CT * NS], ACT.Exp).then_inc(s_par, 1)
            act.wait_ge(s_par, 3)
            first = (None, 0)
            for j in range(CT):
                first_tap(first, j)
            tanh_z(first, 0)
            tanh_x(first)
            tanh_z(first, 1)
            copies(first)
            for j in range(CT):
                terms(first, j)
            softplus(first)
            turns(act, turn)
            guess((None, NCH - 2))
            normalise((None, NCH - 2))
            for t in range(CTT):
                take_sum((None, NCH - 1), t)
            guess((None, NCH - 1))
            normalise((None, NCH - 1))

        @block.gpsimd
        def _(pool):
            def make_dt(k):
                q = k[1] % 2
                pool.wait_ge(s_sp, at(k, 2, 2))
                nc.gpsimd.tensor_tensor(dt_sb[:, q, :, :], dt_sb[:, q, :, :], relu[:, :, :], ALU.add).then_inc(s_dt, 1)

            def make_u(k):
                q = k[1] % 2
                pool.wait_ge(s_dt, at(k, 1, 1))
                nc.gpsimd.tensor_tensor(u_sb[:, q, :, :], dt_sb[:, q, :, :], xs[:, q, :, :], ALU.mult).then_inc(s_u, 1)

            def silu_x(k):
                pool.wait_ge(s_tanh, at(k, 4, 3))
                nc.gpsimd.tensor_tensor(xs[:, k[1] % 2, :, :], xs[:, k[1] % 2, :, :], tnh[:, :, :], ALU.mult)\
                  .then_inc(s_silu, 1)

            def variance(k):
                pool.wait_ge(s_norm, at(k, CTT, CTT))
                pool.wait_ge(s_st, at(k, CTT, CTT))
                nc.gpsimd.tensor_tensor(mean[:, :], stats[:, :, 1], stats[:, :, 4], ALU.add).then_inc(s_mv, 1)
                nc.gpsimd.tensor_tensor(newt[:, :], stats[:, :, 1], stats[:, :, 4], ALU.subtract).then_inc(s_mv, 1)
                nc.gpsimd.tensor_tensor(var[:, :], stats[:, :, 2], stats[:, :, 5], ALU.add).then_inc(s_mv, 1)
                pool.wait_ge(s_mv, at(k, 8, 3))
                nc.gpsimd.tensor_tensor(newt[:, :], newt[:, :], half, ALU.mult).then_inc(s_mv, 1)
                nc.gpsimd.tensor_tensor(mean[:, :], mean[:, :], minus_half, ALU.mult).then_inc(s_mv, 1)
                nc.gpsimd.tensor_tensor(var[:, :], var[:, :], per_dm, ALU.mult).then_inc(s_mv, 1)
                pool.wait_ge(s_mv, at(k, 8, 6))
                nc.gpsimd.tensor_tensor(newt[:, :], newt[:, :], newt[:, :], ALU.mult).then_inc(s_mv, 1)
                nc.gpsimd.tensor_tensor(var[:, :], var[:, :], eps, ALU.add).then_inc(s_mv, 1)
                pool.wait_ge(s_mv, at(k, 8, 8))
                nc.gpsimd.tensor_tensor(var[:, :], newt[:, :], var[:, :], ALU.add).then_inc(s_nw, 1)

            def newton(k):
                pool.wait_ge(s_ln, at(k, 2, 2))
                nc.gpsimd.tensor_tensor(newt[:, :], rstd[:, :], rstd[:, :], ALU.mult).then_inc(s_nw, 1)
                pool.wait_ge(s_nw, at(k, 7, 2))
                nc.gpsimd.tensor_tensor(newt[:, :], newt[:, :], var[:, :], ALU.mult).then_inc(s_nw, 1)
                pool.wait_ge(s_nw, at(k, 7, 3))
                nc.gpsimd.tensor_tensor(newt[:, :], newt[:, :], half, ALU.mult).then_inc(s_nw, 1)
                pool.wait_ge(s_nw, at(k, 7, 4))
                nc.gpsimd.tensor_tensor(newt[:, :], one_half, newt[:, :], ALU.subtract).then_inc(s_nw, 1)
                pool.wait_ge(s_nw, at(k, 7, 5))
                nc.gpsimd.tensor_tensor(rstd[:, :], rstd[:, :], newt[:, :], ALU.mult).then_inc(s_nw, 1)
                pool.wait_ge(s_nw, at(k, 7, 6))
                nc.gpsimd.tensor_tensor(shift_sb[:, :], mean[:, :], rstd[:, :], ALU.mult).then_inc(s_nw, 1)

            def turn(i, prepare, finish, settle):
                k, last, q = shift(i, 1), shift(i, -1), i[1] % 2
                for n in range(NS):
                    if n % (NS // 2) == 0:
                        pool.wait_ge(s_cb[q][n // (NS // 2)], loads(i))
                    pool.wait_ge(s_scan, at(i, NS * CT, (RING + n + 1) * CT))
                    pool.wait_ge(s_sum, at(i, NS, n + 1))
                    nc.gpsimd.tensor_tensor(state_c[:, n % RING, :, :], state[:, n % RING, :, :],
                                            c_bc[:, q, n, :].unsqueeze(1).to_broadcast([P, CT, TC]),
                                            ALU.mult).then_inc(s_sc, 1)
                    if prepare:
                        if n == 6:
                            silu_x(k)
                        if n == 11:
                            make_dt(k)
                        if n == 12:
                            make_u(k)
                    if settle:
                        if n == 2:
                            newton(shift(i, -2))
                    if finish:
                        if n == 14:
                            variance(last)

            for c, value in enumerate((0.5, 1.5, 1.0 / DM, LN_EPS, -0.5)):
                nc.gpsimd.memset(coef[:, c, :], value).then_inc(s_coef, 1)
            half, one_half, per_dm, eps, minus_half = (coef[:, c, :] for c in range(5))
            pool.sem_inc(s_sum, RING)
            pool.sem_inc(s_norm, CTT)
            pool.wait_ge(s_coef, 5)
            turns(pool, turn)
            newton((None, NCH - 2))
            variance((None, NCH - 1))
            newton((None, NCH - 1))

        @block.vector
        def _(dve):
            def tap(k, j, back):
                if back == 1:
                    dve.wait_ge(s_conv0, at(k, 2 * CT, 2 * j + 2))
                else:
                    dve.wait_ge(s_conv, at(k, 3 * CT, 3 * j + back - 1))
                skip = back if k[1] % CPB == 0 else 0
                out = xs[:, k[1] % 2, j, skip:TC]
                nc.vector.scalar_tensor_tensor(out=out, in0=x_raw[:, j, HALO + skip - back:HALO + TC - back],
                                               scalar=col("conv_w", j, TAPS - 1 - back), in1=out,
                                               op0=ALU.mult, op1=ALU.add).then_inc(s_conv, 1)

            def gate_z(k, h):
                if h == 0 and (k[0] is not None or k[1] >= 2):
                    dve.wait_ge(s_y, at(k, 16, 16))
                dve.wait_ge(s_tanh, at(k, 4, 3 * h + 1))
                nc.vector.scalar_tensor_tensor(out=gate[:, k[1] % 2, 2 * h:2 * h + 2, :].rearrange("p j n -> p (j n)"),
                                               in0=tnh_z[:, 2 * h:2 * h + 2, :].rearrange("p j n -> p (j n)"), scalar=1.0,
                                               in1=w_ps[:, :], op0=ALU.add, op1=ALU.mult).then_inc(s_gate, 1)

            def split(k, step):
                q = k[1] % 2
                mid, low = slice(BC, 2 * BC), slice(2 * BC, 3 * BC)
                if step == 0:
                    dve.wait_ge(s_projc, at(k, 2, 2))
                    nc.vector.tensor_tensor(rest[:, :], proj[0:PARTS * BC, q, :], parts[:, q, :], ALU.subtract)\
                      .then_inc(s_split, 1)
                elif step == 1:
                    dve.wait_ge(s_split, at(k, 5, 1))
                    nc.vector.tensor_copy(parts[mid, q, :], rest[mid, :]).then_inc(s_split, 1)
                    nc.vector.tensor_copy(parts[low, q, :], rest[low, :]).then_inc(s_split, 1)
                elif step == 2:
                    dve.wait_ge(s_split, at(k, 5, 3))
                    nc.vector.tensor_tensor(rest[low, :], rest[low, :], parts[low, q, :], ALU.subtract).then_inc(s_split, 1)
                else:
                    dve.wait_ge(s_split, at(k, 5, 4))
                    nc.vector.tensor_copy(parts[low, q, :], rest[low, :]).then_inc(s_split, 1)

            def take_y(k):
                q = k[1] % 2
                dve.wait_ge(s_sum, at(k, NS, RING + NS))
                nc.vector.scalar_tensor_tensor(out=y_sb[:, :, :].rearrange("p j n -> p (j n)"), in0=y_ps[:, :], scalar=0.5,
                                               in1=gate[:, q, :, :].rearrange("p j n -> p (j n)"),
                                               op0=ALU.mult, op1=ALU.mult).then_inc(s_y, 16)

            def moments(k, t):
                q = k[1] % 2
                dve.wait_ge(s_r, at(k, CTT, 2 * CTT + t + 1))
                nc.vector.bn_stats(stats[:, t, :], res[:, q, t, :]).then_inc(s_st, 1)

            def make_bu(i, n, h):
                m = 2 * n + h
                if m == 0:
                    dve.wait_ge(s_u, at(i, 1, 1))
                if h == 0:
                    dve.wait_ge(s_b, at(i, NS, n + 1))
                dve.wait_ge(s_scan, at(i, NS * CT, RING * CT + 2 * (m - (1 if m < 2 else 2))))
                nc.vector.tensor_tensor(bu_ps[m % 3][:, :].rearrange("p (j n) -> p j n", j=2),
                                        u_sb[:, i[1] % 2, 2 * h:2 * h + 2, :],
                                        b_ps[n % 2][:, 0:TC].unsqueeze(1).to_broadcast([P, 2, TC]),
                                        ALU.mult).then_inc(s_bu, 1)

            def scans(i, n, h):
                m, c = 2 * n + h, i[1] % CPB
                if h == 0:
                    dve.wait_ge(s_sc, at(i, NS, n + 1))
                    if c:
                        dve.wait_ge(s_carry, at(i, NS, n + 1 - NS))
                dve.wait_ge(s_bu, at(i, 2 * NS, 4 + m + 1))
                for e in range(2):
                    j = 2 * h + e
                    dve.wait_ge(s_decay, at(i, NS * CT, n * CT + j + 1))
                    nc.vector.tensor_tensor_scan(state[:, n % RING, j, :], decay[:, n % RING, j, :],
                                                 bu_ps[m % 3][:, e * TC:(e + 1) * TC],
                                                 carry[:, n, j:j + 1] if c else 0.0, ALU.mult, ALU.add).then_inc(s_scan, 1)

            def step(i, n, prepare, between):
                make_bu(i, n, 1)
                between(4 * n)
                scans(i, n, 0)
                between(4 * n + 1)
                if n + 1 < NS:
                    make_bu(i, n + 1, 0)
                elif prepare:
                    make_bu(shift(i, 1), 0, 0)
                between(4 * n + 2)
                scans(i, n, 1)
                between(4 * n + 3)

            def turn(i, prepare, finish, settle):
                k, last = shift(i, 1), shift(i, -1)

                def between(place):
                    if prepare:
                        for j in range(CT):
                            for back in (1, 2, 3):
                                if place == 4 * j + 7 + back:
                                    tap(k, j, back)
                        if place == 4 * 7:
                            gate_z(k, 0)
                        if place == 4 * 8 + 3:
                            gate_z(k, 1)
                        if 4 * 10 + 1 <= place <= 4 * 11:
                            split(k, place - (4 * 10 + 1))
                    if finish:
                        if place == 4 * 2 + 1:
                            take_y(last)
                        if place == 4 * 13 + 2:
                            moments(last, 0)
                        if place == 4 * 14 + 3:
                            moments(last, 1)

                for n in range(NS):
                    step(i, n, prepare, between)

            dve.sem_inc(s_bu, 4)
            dve.sem_inc(s_sc, RING)
            dve.wait_ge(s_par, 1)
            nc.vector.tensor_scalar(negA[:, :], negA[:, :], -1.0, None, ALU.mult).then_inc(s_par, 1)
            first_col, end_col = PAR["conv_w"][0], PAR["D"][0]
            nc.vector.tensor_scalar(par_sb[:, first_col:end_col], par_sb[:, first_col:end_col], 0.5, None,
                                    ALU.mult).then_inc(s_par, 1)
            dve.wait_ge(s_par, 3)
            first = (None, 0)
            for j in range(CT):
                for back in (1, 2, 3):
                    tap(first, j, back)
            gate_z(first, 0)
            dve.wait_ge(s_tanh, 3)
            nc.vector.tensor_tensor(xs[:, 0, :, :], xs[:, 0, :, :], tnh[:, :, :], ALU.mult).then_inc(s_silu, 1)
            gate_z(first, 1)
            for m in range(4):
                split(first, m)
            dve.wait_ge(s_const, 5 * 16)
            for j in range(CT):
                nc.vector.tensor_scalar(diag_D[:, j, :], ident_sb[:, :], col("D", j), None, ALU.mult).then_inc(s_par, 1)
            dve.wait_ge(s_sp, 2)
            nc.vector.tensor_tensor(dt_sb[:, 0, :, :], dt_sb[:, 0, :, :], relu[:, :, :], ALU.add).then_inc(s_dt, 1)
            dve.wait_ge(s_dt, 1)
            nc.vector.tensor_tensor(u_sb[:, 0, :, :], dt_sb[:, 0, :, :], xs[:, 0, :, :], ALU.mult).then_inc(s_u, 1)
            make_bu(first, 0, 0)
            turns(dve, turn)
            last = (None, NCH - 1)
            take_y(last)
            for t in range(CTT):
                moments(last, t)


def attn_ffn_block(nc, x1, ctxT, ident_sb, w, ahead, s_ahead, be2, bias_rows, before, out):
    U = G * NL
    NT = TT // TG

    with ExitStack() as ctx:
        def sb(name, shape, dt=F32):
            return ctx.enter_context(nc.sbuf_tensor(name, shape, dt))

        def sem(name):
            return ctx.enter_context(nc.semaphore(name))

        wq_sb, wk_sb, wv_sb, wo_sb, w1_sb, w2_sb = (w[n] for n in ("wq", "wk", "wv", "wo", "w1", "w2"))
        bqk_sb, bv_sb, swap_sb, gw_sb, gb_sb = (w[n] for n in ("bqk", "bv", "swap", "gw", "gb"))
        lnp_sb, g2_sb, ones3_sb = (w[n] for n in ("lnp", "g2", "ones3"))
        be2_sb = sb("be2_sb", [P, E * DM])
        before_sb = sb("before_sb", [P, E * E])
        brow = sb("brow", [3 * BLK, 2 * E * DM], BF16)
        xa = sb("xa", [P, TT, DM])
        xt = sb("xt", [P, TT, DM])
        x1T = sb("x1T_sb", [P, KT, L])
        xT = sb("xT2_sb", [P, KT, L])
        ctx_sb = sb("ctx_sb", [P, KT, S])
        qT = sb("qT", [P, G, L])
        kTm = sb("kTm", [P, NH, S])
        kTr = sb("kTr", [P, G, P])
        v_sb = sb("v_sb", [P, NH, BLK])
        v_rem = sb("v_rem", [P, G, P])
        big = sb("big", [P, 2, TG, E * DM])
        stage = big[:, 0, 0:2, :].rearrange("p a (t n) -> p (a t) n", n=DM)
        pT_rem = sb("pT_rem", [P, 2, HALF])
        oT = sb("oT", [P, G, L])
        neg = oT[:, :, :].rearrange("p g (t c) -> p (g t) c", c=P)
        hT = sb("hT", [P, E * KT, HALF])
        pT = hT
        raw = sb("raw", [P, 2, HALF])
        lnd = sb("lnd", [P, 2, HALF])
        stats = sb("stats2", [P, TG * E, 6])
        mean = sb("mean2", [P, TG * E])
        var = sb("var2", [P, TG * E])
        lnv = sb("lnv2", [P, TG * E])
        rstd = sb("rstd2", [P, TG * E])
        newt = sb("newt2", [P, TG * E])
        sc = sb("sc", [P, TT, E])
        smax = sb("smax", [P, TT])
        cmp1 = sb("cmp1", [P, TT, E, E])
        cmp2 = sb("cmp2", [P, TT, E, E])
        rank = sb("rank", [P, TT, E])
        wgt = sb("wgt", [P, TT, E])
        wsum = sb("wsum", [P, TT])
        acc = sb("acc", [P, TT, DM])
        scale2 = sb("scale2", [P, TG * E])
        zero = sb("zero", [P, TT * G])
        shift2 = sb("shift2", [P, TG * E])

        ps = ctx.enter_context(nc.psum_tensor("ps", [P, 8, HALF], F32))

        s_const = sem("a_const")
        s_prep = sem("a_prep")
        s_split = sem("a_split")
        s_brow = sem("a_brow")
        s_x = sem("a_x")
        s_stage = sem("a_stage")
        s_zero = sem("a_zero")
        s_zero1 = sem("a_zero1")
        s_ctx = sem("a_ctx")
        s_xt = sem("a_xt")
        s_xtc = sem("a_xtc")
        s_yt = sem("a_yt")
        s_ytc = sem("a_ytc")
        s_kv = sem("a_kv")
        s_kvc = sem("a_kvc")
        s_q = sem("a_q")
        s_qc = sem("a_qc")
        s_s1 = sem("a_s1")
        s_max = sem("a_max")
        s_mt = sem("a_mt")
        s_qm = sem("a_qm")
        s_s2 = sem("a_s2")
        s_exp = sem("a_exp")
        s_pv = sem("a_pv")
        s_raw = sem("a_raw")
        s_den = sem("a_den")
        s_lnd = sem("a_lnd")
        s_o = sem("a_o")
        s_proj = sem("a_proj")
        s_r = sem("a_r")
        s_st = sem("a_st")
        s_mv = sem("a_mv")
        s_nw = sem("a_nw")
        s_ln = sem("a_ln")
        s_x2 = sem("a_x2")
        s_gate = sem("a_gate")
        s_gd = sem("a_gd")
        s_ge = sem("a_ge")
        s_l1 = sem("a_l1")
        s_l1c = sem("a_l1c")
        s_n1 = sem("a_n1")
        s_h = sem("a_h")
        s_hc = sem("a_hc")
        s_l2 = sem("a_l2")
        s_l2c = sem("a_l2c")
        s_n2 = sem("a_n2")
        s_shift = sem("a_shift")
        s_tail = sem("a_tail")
        s_scale = sem("a_scale")
        s_gm = sem("a_gm")
        s_acc = sem("a_acc")
        s_sum = sem("a_sum")
        s_fin = sem("a_fin")
        s_out = sem("a_out")

        TRB, NWB, LNB = KT * NL, 5 * (2 + 2 * NT), 2 * (2 + 2 * NT)
        MVB = TT + 2 * TT * E + TT
        NORMS = 2 + 2 * NT
        NMB = 6 * NORMS
        KVB, GDB, ACB = 1 + 3 * HG, 12, TT * (E + 1)

        block = ctx.enter_context(nc.Block())
        LOADS = 2
        SHARED = 1

        def turns(eng, turn):
            with eng.Fori(0, BATCH - 1) as b:
                turn(b, True)
            turn(BATCH - 1, False)

        @block.sync
        def _(sp):
            def load_x1(b, dst, ready):
                sp.dma_start(dst, x1[bass.ds(b * L, L), :].rearrange("(t p) n -> p t n", p=P)).then_inc(ready, 16)

            def load_ctx(b):
                sp.dma_start(ctx_sb[:, :, :], ctxT[:, bass.ds(b * S, S)].rearrange("(k p) n -> p k n", p=P)).then_inc(s_ctx, 16)

            load_ctx(0)
            load_x1(0, stage, s_stage)
            sp.dma_start(big[0:3 * BLK, 1, 0:2, :], bias_rows.rearrange("q (a n) -> q a n", a=2)).then_inc(s_brow, 16)
            load_x1(0, xa[:, :, :], s_x)
            sp.dma_start(be2_sb[:, :], be2.partition_broadcast(P)).then_inc(s_const, 16)
            sp.dma_start(before_sb[:, :], before.partition_broadcast(P)).then_inc(s_const, 16)

            def turn(b, more):
                if more:
                    sp.wait_ge(s_xt, b * TRB + TRB)
                    load_x1(b + 1, stage, s_stage)
                    sp.wait_ge(s_kv, b * 3 + 3)
                    load_ctx(b + 1)
                    sp.wait_ge(s_r, b * TT + TT)
                    load_x1(b + 1, xa[:, :, :], s_x)
                sp.wait_ge(s_fin, b * TT + TT)
                sp.dma_start(out[bass.ds(b * L, L), :].rearrange("(t p) n -> p t n", p=P), acc[:, :, :]).then_inc(s_out, 16)

            turns(sp, turn)
            sp.wait_ge(s_out, 16 + BATCH * 16)

        @block.tensor
        def _(pe):
            def transposes(src, bank, done):
                for u in range(NL * KT):
                    half, k = u // KT, u % KT
                    for i in range(TG):
                        last = nc.tensor.transpose(ps[:, bank + u, i * P:(i + 1) * P],
                                                   src[:, half * TG + i, k * P:(k + 1) * P], ident_sb[:, :])
                    last.then_inc(done, 1)

            def keys_values(b, bank):
                pe.wait_ge(s_ctx, b * 16 + 16)
                for g in range(G):
                    for k in range(KT):
                        last = nc.tensor.matmul(ps[:, bank + g // 2, (g % 2) * 256:(g % 2) * 256 + S],
                                                wk_sb[:, k, g * P:(g + 1) * P], ctx_sb[:, k, :],
                                                start=k == 0, stop=k == KT - 1)
                last.then_inc(s_kv, 1)
                for k in range(KT):
                    last = nc.tensor.matmul(ps[:, bank + 2, :], ctx_sb[:, k, 0:SM], wv_sb[:, k, :],
                                            start=k == 0, stop=k == KT - 1)
                last.then_inc(s_kv, 1)
                for j in range(HG):
                    for k in range(KT):
                        last = nc.tensor.matmul(
                            ps[BLK * j:BLK * j + SR, bank + 3, 0:P].rearrange("p (g c) -> p g c", c=BLK),
                            ctx_sb[:, k, SM:S],
                            wv_sb[:, k, :].rearrange("p (g j c) -> p g j c", j=HG, c=BLK)[:, :, j, :],
                            start=k == 0, stop=k == KT - 1)
                last.then_inc(s_kv, 1)

            def queries(b):
                pe.wait_ge(s_stage, b * 16 + 16)
                transposes(stage, 4, s_xt)
                for u in range(U):
                    g, half = u // NL, u % NL
                    if u == 0:
                        pe.wait_ge(s_xtc, b * TRB + TRB)
                    elif u >= 4:
                        pe.wait_ge(s_qc, b * U + u - 3)
                    for k in range(KT):
                        last = nc.tensor.matmul(ps[:, 4 + u % 4, :], wq_sb[:, k, g * P:(g + 1) * P],
                                                x1T[:, k, half * HALF:(half + 1) * HALF],
                                                start=k == 0, stop=k == KT - 1)
                    last.then_inc(s_q, 1)

            def maxima(b):
                pe.wait_ge(s_kvc, b * KVB + KVB)
                for u in range(TT * G):
                    t, g = u // G, u % G
                    if u >= 4:
                        pe.wait_ge(s_max, b * TT * G + u - 3)
                    for i in range(2):
                        last = nc.tensor.matmul(ps[:, 2 * (u % 4) + i, 0:2 * S], qT[:, g, t * P:(t + 1) * P],
                                                kTm[:, HG * g + 2 * i:HG * g + 2 * i + 2, :], start=True, stop=True)
                    last.then_inc(s_s1, 1)
                pe.wait_ge(s_max, b * TT * G + TT * G)
                for u in range(U):
                    g, half = u // NL, u % NL
                    for i in range(TG):
                        last = nc.tensor.transpose(ps[:, u, i * P:(i + 1) * P], neg[:, (half * TG + i) * G + g, :],
                                                   ident_sb[:, :])
                    last.then_inc(s_mt, 1)


            def turn(b, more):
                def scores(u):
                    g, half = u // NL, u % NL
                    q = qT[:, g, half * HALF:(half + 1) * HALF]
                    for j in range(HG):
                        if u == 0:
                            pe.wait_ge(s_qm, b * U + j + 1)
                        elif j % 2 == 0:
                            pe.wait_ge(s_exp, b * 3 * U + 3 * (u - 1) + j // 2 + 1)
                        last = nc.tensor.matmul(ps[:, j, :], kTm[:, HG * g + j, 0:SM], q, start=True, stop=True)
                        if j % 2:
                            last.then_inc(s_s2, 1)
                    if u == 0:
                        pe.wait_ge(s_qm, b * U + U)
                    else:
                        pe.wait_ge(s_exp, b * 3 * U + 3 * u)
                    nc.tensor.matmul(ps[:, 4, :], kTr[:, g, :], q, start=True, stop=True).then_inc(s_s2, 1)

                def values(u):
                    g = u // NL
                    pe.wait_ge(s_exp, b * 3 * U + 3 * u + 3)
                    if u >= 2:
                        pe.wait_ge(s_raw, b * U + u - 1)
                    nc.tensor.matmul(ps[:, 5 + u % 2, :], v_rem[:, g, :], pT_rem[:, u % 2, :],
                                     start=True, stop=False, skip_group_check=True)
                    for j in range(HG):
                        last = nc.tensor.matmul(ps[BLK * j:BLK * (j + 1), 5 + u % 2, :], v_sb[:, HG * g + j, :],
                                                pT[:, HG * (u % 2) + j, :], start=False, stop=True,
                                                skip_group_check=True)
                    last.then_inc(s_pv, 1)

                def sums(u):
                    pe.wait_ge(s_raw, b * U + u + 1)
                    if u:
                        pe.wait_ge(s_lnd, b * 2 * U + 2 * u - 1)
                    nc.tensor.matmul(ps[:, 7, :], swap_sb[:, :], raw[:, u % 2, :], start=True, stop=True).then_inc(s_den, 1)

                def project(t, groups):
                    for g in groups:
                        last = nc.tensor.matmul(ps[:, t % 4, 0:DM], oT[:, g, t * P:(t + 1) * P], wo_sb[:, g, :],
                                                start=g == 0, stop=g == G - 1)
                    if g == G - 1:
                        last.then_inc(s_proj, 1)

                for u in range(U + 2):
                    if u < U:
                        scores(u)
                    if 1 <= u <= U:
                        values(u - 1)
                    if u == U + 1:
                        pe.wait_ge(s_o, b * U + U - 2)
                        project(0, range(G - 1))
                    if u >= 2:
                        sums(u - 2)
                for t in range(1, TG):
                    project(t, range(G - 1))
                pe.wait_ge(s_o, b * U + U - 1)
                for t in range(TG):
                    project(t, [G - 1])
                pe.wait_ge(s_o, b * U + U)
                for t in range(TG, TT):
                    pe.wait_ge(s_r, b * TT + t - 3)
                    project(t, range(G))
                if more:
                    queries(b + 1)
                    pe.wait_ge(s_qc, (b + 1) * U + U)
                    keys_values(b + 1, 4)
                pe.wait_ge(s_x2, b * TT + TT)
                transposes(xt, 0, s_yt)
                pe.wait_ge(s_ytc, b * TRB + TRB)
                for t in range(TT):
                    if t >= 2:
                        pe.wait_ge(s_l1c, b * TT + t - 1)
                    for h in range(2):
                        dst = ps[:, 2 * (t % 2) + h, :]
                        nc.tensor.matmul(dst, ones3_sb[:, :], brow[:, h * HALF:(h + 1) * HALF], start=True, stop=False)
                        for k in range(KT):
                            last = nc.tensor.matmul(dst, xT[:, k, t * P:(t + 1) * P], w1_sb[:, k, h * HALF:(h + 1) * HALF],
                                                    start=False, stop=k == KT - 1)
                    last.then_inc(s_l1, 1)
                if more:
                    pe.wait_ge(s_kvc, (b + 1) * KVB + KVB)
                for t in range(TT):
                    for k in range(KT):
                        last = nc.tensor.matmul(ps[:, 7, t * E:(t + 1) * E], xT[:, k, t * P:(t + 1) * P], gw_sb[:, k, :],
                                                start=k == 0, stop=k == KT - 1)
                last.then_inc(s_gate, 1)
                for n in range(NT):
                    pe.wait_ge(s_n1, b * TT + TG * (n + 1))

                    def turn_tiles(c):
                        m = n * E * KT + c
                        if m >= 3:
                            pe.wait_ge(s_hc, b * NT * E * KT + m - 2)
                        for i in range(TG):
                            last = nc.tensor.transpose(ps[:, 4 + m % 3, i * P:(i + 1) * P],
                                                       big[:, n, i, c * P:(c + 1) * P], ident_sb[:, :])
                        last.then_inc(s_h, 1)

                    for c in range(2 * KT):
                        turn_tiles(c)
                    for i in range(TG):
                        t = n * TG + i
                        if t >= 2:
                            pe.wait_ge(s_l2c, b * TT + t - 1)
                        else:
                            pe.wait_ge(s_l1c, b * TT + TT)
                        for e in range(E):
                            dst = ps[:, 2 * (t % 2) + e // 2, (e % 2) * DM:(e % 2 + 1) * DM]
                            if i == 0:
                                pe.wait_ge(s_hc, b * NT * E * KT + E * KT * n + KT * (e + 1))
                            if e % 2 == 0:
                                nc.tensor.matmul(ps[:, 2 * (t % 2) + e // 2, :], ones3_sb[:, :],
                                                 brow[:, E * DM + e * DM:E * DM + (e + 2) * DM],
                                                 start=True, stop=False, skip_group_check=True)
                            for k in range(KT):
                                last = nc.tensor.matmul(dst, hT[:, e * KT + k, i * P:(i + 1) * P],
                                                        w2_sb[:, e * KT + k, :], start=False, stop=k == KT - 1,
                                                        skip_group_check=True)
                            if i == 0 and e + 2 < E:
                                for k in range(KT):
                                    turn_tiles((e + 2) * KT + k)
                        last.then_inc(s_l2, 1)
                if more:
                    pe.wait_ge(s_l2c, b * TT + TT)
                    pe.wait_ge(s_gd, b * GDB + 1)
                    maxima(b + 1)

            pe.wait_ge(s_ahead, len(ahead) * 16)
            pe.wait_ge(s_prep, 4)
            keys_values(0, 0)
            queries(0)
            pe.wait_ge(s_qc, U)
            maxima(0)
            pe.wait_ge(s_const, LOADS * 16)
            pe.wait_ge(s_split, 6)
            turns(pe, turn)

        @block.scalar
        def _(act):
            def copy_transposed(b, dst, bank, ready, done):
                for u in range(NL * KT):
                    half, k = u // KT, u % KT
                    act.wait_ge(ready, b * TRB + u + 1)
                    nc.scalar.activation(dst[:, k, half * HALF:(half + 1) * HALF], ps[:, bank + u, :],
                                         ACT.Copy).then_inc(done, 1)

            def query(b, u):
                g, half = u // NL, u % NL
                act.wait_ge(s_q, b * U + u + 1)
                nc.scalar.activation(qT[:, g, half * HALF:(half + 1) * HALF], ps[:, 4 + u % 4, :], ACT.Identity,
                                     scale=HD ** -0.5, bias=bqk_sb[:, g:g + 1]).then_inc(s_qc, 1)

            def guess(b, n):
                cols = TT if n in (0, NORMS - 1) else TG * E
                act.wait_ge(s_nw, b * NWB + 5 * n + 1)
                nc.scalar.activation(lnv[:, 0:cols], var[:, 0:cols], ACT.Ln).then_inc(s_ln, 1)
                act.wait_ge(s_ln, b * LNB + 2 * n + 1)
                nc.scalar.activation(rstd[:, 0:cols], lnv[:, 0:cols], ACT.Exp, scale=-0.5).then_inc(s_ln, 1)

            def turn(b, more):
                def exps(u):
                    if u >= 2:
                        act.wait_ge(s_pv, b * U + u - 1)
                    for i in range(2):
                        act.wait_ge(s_s2, b * 3 * U + 3 * u + i + 1)
                        nc.scalar.activation(pT[:, HG * (u % 2) + 2 * i:HG * (u % 2) + 2 * i + 2, :],
                                             ps[:, 2 * i:2 * i + 2, :], ACT.Exp).then_inc(s_exp, 1)
                    act.wait_ge(s_s2, b * 3 * U + 3 * u + 3)
                    nc.scalar.activation(pT_rem[:, u % 2, :], ps[:, 4, :], ACT.Exp).then_inc(s_exp, 1)

                def inverse(u):
                    act.wait_ge(s_den, b * U + u + 1)
                    if u >= 2:
                        act.wait_ge(s_o, b * U + u - 1)
                    nc.scalar.activation(lnd[:, u % 2, :], ps[:, 7, :], ACT.Ln).then_inc(s_lnd, 1)
                    act.wait_ge(s_lnd, b * 2 * U + 2 * u + 1)
                    nc.scalar.activation(lnd[:, u % 2, :], lnd[:, u % 2, :], ACT.Exp, scale=-1.0).then_inc(s_lnd, 1)

                for u in range(U + 2):
                    if u < U:
                        exps(u)
                    if u >= 2:
                        inverse(u - 2)
                if more:
                    copy_transposed(b + 1, x1T, 4, s_xt, s_xtc)
                    for u in range(U):
                        query(b + 1, u)
                        if u == 1:
                            guess(b, 0)
                else:
                    guess(b, 0)
                copy_transposed(b, xT, 0, s_yt, s_ytc)
                for t in range(TT):
                    act.wait_ge(s_l1, b * TT + t + 1)
                    nc.scalar.activation(big[:, t // TG, t % TG, :].rearrange("p (a n) -> p a n", a=2),
                                         ps[:, 2 * (t % 2):2 * (t % 2) + 2, :], ACT.Copy).then_inc(s_l1c, 1)
                    if t == TG - 1:
                        guess(b, 1)
                guess(b, 2)
                for n in range(NT):
                    for c in range(E * KT):
                        m = n * E * KT + c
                        act.wait_ge(s_h, b * NT * E * KT + m + 1)
                        if n:
                            act.wait_ge(s_l2, b * TT + TG * n)
                        nc.scalar.activation(hT[:, c, :], ps[:, 4 + m % 3, :], ACT.Relu, scale=lnp_sb[:, c:c + 1],
                                             bias=lnp_sb[:, E * KT + c:E * KT + c + 1]).then_inc(s_hc, 1)
                    for i in range(TG):
                        t = n * TG + i
                        act.wait_ge(s_l2, b * TT + t + 1)
                        nc.scalar.activation(big[:, n, i, :].rearrange("p (a n) -> p a n", a=2),
                                             ps[:, 2 * (t % 2):2 * (t % 2) + 2, :], ACT.Copy).then_inc(s_l2c, 1)
                        if t == TG + 1:
                            guess(b, 3)
                        if t == 0:
                            act.wait_ge(s_gd, b * GDB + 5)
                            nc.scalar.activation(wgt[:, :, :], wgt[:, :, :], ACT.Exp).then_inc(s_ge, 1)
                guess(b, 4)
                act.wait_ge(s_shift, b + 1)
                for i in range(TG if more else SHARED):
                    for e in range(E):
                        c = i * E + e
                        tile = big[:, NT - 1, i, e * DM:(e + 1) * DM]
                        last = nc.scalar.activation(tile, tile, ACT.Identity, scale=scale2[:, c:c + 1],
                                                    bias=shift2[:, c:c + 1])
                    last.then_inc(s_n2, 1)
                guess(b, 5)

            act.wait_ge(s_ahead, len(ahead) * 16)
            nc.scalar.preload_act_table_set("natural_log_exp_and_others")
            nc.scalar.mul(bqk_sb[:, 0:G], bqk_sb[:, 0:G], HD ** -0.5).then_inc(s_prep, 1)
            copy_transposed(0, x1T, 4, s_xt, s_xtc)
            act.wait_ge(s_prep, 4)
            for u in range(U):
                query(0, u)
            act.wait_ge(s_const, LOADS * 16)
            turns(act, turn)

        @block.gpsimd
        def _(pool):
            nc.gpsimd.memset(kTm[:, :, :], 0.0).then_inc(s_prep, 1)
            nc.gpsimd.memset(kTr[:, :, :], 0.0).then_inc(s_prep, 1)
            nc.gpsimd.memset(v_rem[:, :, :], 0.0).then_inc(s_prep, 1)
            nc.gpsimd.memset(neg, 0.0).then_inc(s_zero, 1)
            nc.gpsimd.memset(zero[:, :], 0.0).then_inc(s_zero1, 1)
            zeros = zero[:, :].unsqueeze(2).to_broadcast([P, TT * G, P])
            pool.wait_ge(s_zero1, 1)
            pool.wait_ge(s_const, LOADS * 16)

            def turn(b, more):
                if more:
                    pool.wait_ge(s_proj, b * TT + TT)
                    nc.gpsimd.tensor_tensor(neg, zeros, zeros, ALU.add).then_inc(s_zero, 1)
                for t in range(TT if more else TT - TG + SHARED):
                    tile = big[:, t // TG, t % TG, :]
                    pool.wait_ge(s_n2, b * TT + t + 1)
                    nc.gpsimd.tensor_tensor(tile, tile, g2_sb[:, :], ALU.mult).then_inc(s_gm, 1)
                    pool.wait_ge(s_gm, b * TT + t + 1)
                    pool.wait_ge(s_acc, b * ACB + ACB)
                    for e in range(E):
                        nc.gpsimd.tensor_tensor(acc[:, t, :], acc[:, t, :], tile[:, e * DM:(e + 1) * DM],
                                                ALU.add).then_inc(s_sum, 1)
                        pool.wait_ge(s_sum, b * TT * E + E * t + e + 1)

            turns(pool, turn)

        @block.vector
        def _(dve):
            COUNTS = [TT] + [TG * E] * (2 * NT) + [TT]

            def aggregate(b, n):
                count, at = COUNTS[n], b * NMB + 6 * n
                m, v, w, st = mean[:, 0:count], var[:, 0:count], newt[:, 0:count], stats[:, 0:count, :]
                dve.wait_ge(s_st, b * MVB + sum(COUNTS[:n + 1]))
                nc.vector.tensor_tensor(m, st[:, :, 1], st[:, :, 4], ALU.add).then_inc(s_mv, 1)
                nc.vector.tensor_tensor(w, st[:, :, 1], st[:, :, 4], ALU.subtract).then_inc(s_mv, 1)
                nc.vector.tensor_tensor(v, st[:, :, 2], st[:, :, 5], ALU.add).then_inc(s_mv, 1)
                dve.wait_ge(s_mv, at + 2)
                nc.vector.tensor_tensor(w, w, w, ALU.mult).then_inc(s_mv, 1)
                dve.wait_ge(s_mv, at + 3)
                nc.vector.tensor_scalar(v, v, 1.0 / DM, LN_EPS, ALU.mult, ALU.add).then_inc(s_mv, 1)
                nc.vector.tensor_scalar(m, m, 0.5, None, ALU.mult).then_inc(s_mv, 1)
                dve.wait_ge(s_mv, at + 5)
                nc.vector.scalar_tensor_tensor(out=v, in0=w, scalar=0.25, in1=v, op0=ALU.mult,
                                               op1=ALU.add).then_inc(s_nw, 1)

            def newton(b, n):
                cols, at = COUNTS[n], b * NWB + 5 * n
                v, r, w = var[:, 0:cols], rstd[:, 0:cols], newt[:, 0:cols]
                dve.wait_ge(s_ln, b * LNB + 2 * n + 2)
                nc.vector.tensor_tensor(w, r, r, ALU.mult).then_inc(s_nw, 1)
                dve.wait_ge(s_nw, at + 2)
                nc.vector.tensor_tensor(w, w, v, ALU.mult).then_inc(s_nw, 1)
                dve.wait_ge(s_nw, at + 3)
                nc.vector.tensor_scalar(w, w, -0.5, 1.5, ALU.mult, ALU.add).then_inc(s_nw, 1)
                dve.wait_ge(s_nw, at + 4)
                nc.vector.tensor_tensor(r, r, w, ALU.mult).then_inc(s_nw, 1)
                dve.wait_ge(s_nw, at + 5)

            def keys_values(b, bank):
                dve.wait_ge(s_kv, b * 3 + 3)
                keys = ps[:, bank:bank + 2, :].rearrange("p a (g n) -> p (a g) n", n=256)
                for j in range(HG):
                    rows = slice(BLK * j, BLK * (j + 1))
                    heads = kTm[rows, :, :].rearrange("p (g j) n -> p g j n", j=HG)[:, :, j, :]
                    nc.vector.tensor_tensor(heads, keys[rows, :, 0:S],
                                            bqk_sb[rows, G:2 * G].unsqueeze(2).to_broadcast([BLK, G, S]),
                                            ALU.add).then_inc(s_kvc, 1)
                for j in range(HG):
                    rows = slice(BLK * j, BLK * (j + 1))
                    heads = kTm[rows, :, :].rearrange("p (g j) n -> p g j n", j=HG)[:, :, j, :]
                    dve.wait_ge(s_kvc, b * KVB + 1 + j)
                    nc.vector.tensor_copy(kTr[rows, :, BLK * j:BLK * j + SR], heads[:, :, SM:S]).then_inc(s_kvc, 1)
                nc.vector.tensor_tensor(v_sb[:, :, :].rearrange("p h c -> p (h c)"), ps[:, bank + 2, :], bv_sb[:, :],
                                        ALU.add).then_inc(s_kvc, 1)
                for j in range(HG):
                    rows = slice(BLK * j, BLK * j + SR)
                    nc.vector.tensor_tensor(
                        v_rem[rows, :, BLK * j:BLK * (j + 1)], ps[rows, bank + 3, 0:P].rearrange("p (g c) -> p g c", c=BLK),
                        bv_sb[rows, :].rearrange("p (g j c) -> p g j c", j=HG, c=BLK)[:, :, j, :],
                        ALU.add).then_inc(s_kvc, 1)

            def maxima(b, units=range(TT * G)):
                dve.wait_ge(s_zero, b + 1)
                for u in units:
                    t, g = u // G, u % G
                    dve.wait_ge(s_s1, b * TT * G + u + 1)
                    nc.vector.tensor_reduce(neg[:, u, :].rearrange("p (j c) -> p j c", c=BLK)[:, :, HD],
                                            ps[:, 2 * (u % 4):2 * (u % 4) + 2, 0:2 * S].rearrange("p a (h n) -> p a h n", n=S),
                                            AX.X, ALU.max).then_inc(s_max, 1)

            def subtract_maxima(b):
                for u in range(U):
                    g, half = u // NL, u % NL
                    q = qT[:, g, half * HALF:(half + 1) * HALF]
                    dve.wait_ge(s_mt, b * U + u + 1)
                    nc.vector.tensor_tensor(q, q, ps[:, u, :], ALU.subtract).then_inc(s_qm, 1)


            def measure(b, n, ready):
                for i in range(TG):
                    dve.wait_ge(ready, b * TT + TG * n + i + 1)
                    for e in range(E):
                        nc.vector.bn_stats(stats[:, i * E + e, :], big[:, n, i, e * DM:(e + 1) * DM]).then_inc(s_st, 1)

            def weigh(b, n):
                nc.vector.tensor_tensor(scale2[:, :], rstd[:, :],
                                        wgt[:, TG * n:TG * (n + 1), :].rearrange("p t e -> p (t e)"),
                                        ALU.mult).then_inc(s_scale, 1)
                dve.wait_ge(s_scale, b * NT + n + 1)

            def normalise(n, scales, done):
                for i in range(TG):
                    for e in range(E):
                        c = i * E + e
                        tile = big[:, n, i, e * DM:(e + 1) * DM]
                        last = nc.vector.tensor_scalar(tile, tile, mean[:, c:c + 1], scales[:, c:c + 1],
                                                       ALU.subtract, ALU.mult)
                    last.then_inc(done, 1)

            def turn(b, more):
                def take(u):
                    dve.wait_ge(s_pv, b * U + u + 1)
                    if u >= 2:
                        dve.wait_ge(s_o, b * U + u - 1)
                    nc.vector.tensor_copy(raw[:, u % 2, :], ps[:, 5 + u % 2, :]).then_inc(s_raw, 1)

                def divide(u):
                    g, half = u // NL, u % NL
                    dve.wait_ge(s_lnd, b * 2 * U + 2 * u + 2)
                    nc.vector.tensor_tensor(oT[:, g, half * HALF:(half + 1) * HALF], raw[:, u % 2, :], lnd[:, u % 2, :],
                                            ALU.mult).then_inc(s_o, 1)

                for u in range(U + 2):
                    if u >= 2:
                        divide(u - 2)
                    if u < U:
                        take(u)
                dve.wait_ge(s_x, b * 16 + 16)
                for t in range(TT):
                    dve.wait_ge(s_proj, b * TT + t + 1)
                    nc.vector.tensor_tensor(xt[:, t, :], xa[:, t, :], ps[:, t % 4, 0:DM], ALU.add).then_inc(s_r, 1)
                    dve.wait_ge(s_r, b * TT + t + 1)
                    nc.vector.bn_stats(stats[:, t, :], xt[:, t, :]).then_inc(s_st, 1)
                aggregate(b, 0)
                newton(b, 0)
                for t in range(TT):
                    nc.vector.tensor_scalar(xt[:, t, :], xt[:, t, :], mean[:, t:t + 1], rstd[:, t:t + 1],
                                            ALU.subtract, ALU.mult).then_inc(s_x2, 1)
                if more:
                    keys_values(b + 1, 4)
                for n in range(NT):
                    measure(b, n, s_l1c)
                    aggregate(b, 1 + n)
                    newton(b, 1 + n)
                    normalise(n, rstd, s_n1)
                gd = b * GDB
                dve.wait_ge(s_gate, b + 1)
                nc.vector.tensor_tensor(sc[:, :, :], ps[:, 7, 0:TT * E].rearrange("p (t e) -> p t e", e=E),
                                        gb_sb[:, :].unsqueeze(1).to_broadcast([P, TT, E]), ALU.add).then_inc(s_gd, 1)
                dve.wait_ge(s_gd, gd + 1)
                own = sc[:, :, :].unsqueeze(3).to_broadcast([P, TT, E, E])
                other = sc[:, :, :].unsqueeze(2).to_broadcast([P, TT, E, E])
                nc.vector.tensor_reduce(smax[:, :], sc[:, :, :], AX.X, ALU.max).then_inc(s_gd, 1)
                nc.vector.tensor_tensor(cmp1[:, :, :, :], other, own, ALU.is_gt).then_inc(s_gd, 1)
                nc.vector.tensor_tensor(cmp2[:, :, :, :], other, own, ALU.is_equal).then_inc(s_gd, 1)
                dve.wait_ge(s_gd, gd + 2)
                nc.vector.tensor_tensor(wgt[:, :, :], sc[:, :, :], smax[:, :].unsqueeze(2).to_broadcast([P, TT, E]),
                                        ALU.subtract).then_inc(s_gd, 1)
                flat1 = cmp1[:, :, :, :].rearrange("p t e f -> p t (e f)")
                flat2 = cmp2[:, :, :, :].rearrange("p t e f -> p t (e f)")
                dve.wait_ge(s_gd, gd + 4)
                nc.vector.tensor_tensor(flat2, flat2, before_sb[:, :].unsqueeze(1).to_broadcast([P, TT, E * E]),
                                        ALU.mult).then_inc(s_gd, 1)
                dve.wait_ge(s_gd, gd + 6)
                nc.vector.tensor_tensor(flat1, flat1, flat2, ALU.add).then_inc(s_gd, 1)
                dve.wait_ge(s_gd, gd + 7)
                nc.vector.tensor_reduce(rank[:, :, :].rearrange("p t e -> p (t e)"),
                                        cmp1[:, :, :, :].rearrange("p t e f -> p (t e) f"), AX.X,
                                        ALU.add).then_inc(s_gd, 1)
                dve.wait_ge(s_ge, b + 1)
                dve.wait_ge(s_gd, gd + 8)
                nc.vector.scalar_tensor_tensor(out=wgt[:, :, :], in0=rank[:, :, :], scalar=1.5, in1=wgt[:, :, :],
                                               op0=ALU.is_lt, op1=ALU.mult).then_inc(s_gd, 1)
                dve.wait_ge(s_gd, gd + 9)
                nc.vector.tensor_reduce(wsum[:, :], wgt[:, :, :], AX.X, ALU.add).then_inc(s_gd, 1)
                dve.wait_ge(s_gd, gd + 10)
                nc.vector.reciprocal(wsum[:, :], wsum[:, :]).then_inc(s_gd, 1)
                dve.wait_ge(s_gd, gd + 11)
                nc.vector.tensor_tensor(wgt[:, :, :], wgt[:, :, :], wsum[:, :].unsqueeze(2).to_broadcast([P, TT, E]),
                                        ALU.mult).then_inc(s_gd, 1)
                dve.wait_ge(s_gd, gd + 12)
                dve.wait_ge(s_out, b * 16 + 16)
                for t in range(TT):
                    nc.vector.tensor_scalar(acc[:, t, :], xt[:, t, :], 2.0, None, ALU.mult).then_inc(s_acc, 1)
                for e in range(E):
                    for t in range(TT):
                        dve.wait_ge(s_acc, b * ACB + TT * e + t + 1)
                        nc.vector.scalar_tensor_tensor(out=acc[:, t, :], in0=be2_sb[:, e * DM:(e + 1) * DM],
                                                       scalar=wgt[:, t, e:e + 1], in1=acc[:, t, :], op0=ALU.mult,
                                                       op1=ALU.add).then_inc(s_acc, 1)

                for n in range(NT):
                    measure(b, n, s_l2c)
                    if more and n == NT - 1:
                        maxima(b + 1, range(0, 4))
                    aggregate(b, 1 + NT + n)
                    if more and n == NT - 1:
                        maxima(b + 1, range(4, 8))
                    newton(b, 1 + NT + n)
                    weigh(b, n)
                    if n < NT - 1:
                        normalise(n, scale2, s_n2)
                nc.vector.scalar_tensor_tensor(out=shift2[:, :], in0=mean[:, :], scalar=-1.0, in1=scale2[:, :],
                                               op0=ALU.mult, op1=ALU.mult).then_inc(s_shift, 1)
                if more:
                    maxima(b + 1, range(8, TT * G))
                    subtract_maxima(b + 1)
                pooled = TT if more else TT - TG + SHARED
                left = TT - pooled
                for t in range(pooled, TT):
                    i = t % TG
                    for e in range(E):
                        tile, c = big[:, NT - 1, i, e * DM:(e + 1) * DM], i * E + e
                        nc.vector.tensor_scalar(tile, tile, mean[:, c:c + 1], scale2[:, c:c + 1],
                                                ALU.subtract, ALU.mult).then_inc(s_tail, 1)
                    dve.wait_ge(s_tail, (t - pooled) * (E + 1) + E)
                    tile = big[:, NT - 1, i, :]
                    nc.vector.tensor_tensor(tile, tile, g2_sb[:, :], ALU.mult).then_inc(s_tail, 1)
                for e in range(E if left else 0):
                    dve.wait_ge(s_tail, left * (E + 1 + e))
                    for t in range(pooled, TT):
                        nc.vector.tensor_tensor(acc[:, t, :], acc[:, t, :], big[:, NT - 1, t % TG, e * DM:(e + 1) * DM],
                                                ALU.add).then_inc(s_tail, 1)
                if left:
                    dve.wait_ge(s_tail, left * (2 * E + 1))
                for t in list(range(pooled, TT)) + list(range(pooled)):
                    if t < pooled:
                        dve.wait_ge(s_sum, b * TT * E + E * (t + 1))
                    nc.vector.bn_stats(stats[:, t, :], acc[:, t, :]).then_inc(s_st, 1)
                aggregate(b, NORMS - 1)
                newton(b, NORMS - 1)
                for t in range(TT):
                    nc.vector.tensor_scalar(acc[:, t, :], acc[:, t, :], mean[:, t:t + 1], rstd[:, t:t + 1],
                                            ALU.subtract, ALU.mult).then_inc(s_fin, 1)

            dve.sem_inc(s_out, 16)
            dve.wait_ge(s_ahead, len(ahead) * 16)
            dve.wait_ge(s_prep, 4)
            keys_values(0, 0)
            dve.wait_ge(s_brow, 16)
            row = big[0:3 * BLK, 1, 0:2, :].rearrange("p a n -> p (a n)")
            left = big[0:3 * BLK, 1, 2:4, :].rearrange("p a n -> p (a n)")
            nc.vector.tensor_copy(brow[:, :], row).then_inc(s_split, 1)
            dve.wait_ge(s_split, 1)
            nc.vector.tensor_tensor(left, row, brow[:, :], ALU.subtract).then_inc(s_split, 1)
            dve.wait_ge(s_split, 2)
            for q in (1, 2):
                nc.vector.tensor_copy(brow[BLK * q:BLK * q + BLK, :], left[BLK * q:BLK * q + BLK, :]).then_inc(s_split, 1)
            dve.wait_ge(s_split, 4)
            nc.vector.tensor_tensor(left[2 * BLK:3 * BLK, :], left[2 * BLK:3 * BLK, :], brow[2 * BLK:3 * BLK, :],
                                    ALU.subtract).then_inc(s_split, 1)
            dve.wait_ge(s_split, 5)
            nc.vector.tensor_copy(brow[2 * BLK:3 * BLK, :], left[2 * BLK:3 * BLK, :]).then_inc(s_split, 1)
            dve.wait_ge(s_split, 6)
            maxima(0)
            subtract_maxima(0)
            dve.wait_ge(s_const, LOADS * 16)
            turns(dve, turn)


def decoder_block(nc, x, xT, w_in, w_x, w_out, par, ident, sel_bc, sel_p, ctxT, wq, wk, wv, wo, bqk, bv, swap,
                  w1, w2, gw, gb, lnp, bias_rows, ones3, g2, be2, before, out):
    c_dram = nc.dram_tensor("c_scratch", (NCH * NS, TC), F32).ap()
    x1 = nc.dram_tensor("x1_scratch", (BATCH * L, DM), F32).ap()
    channels = lambda a: a.rearrange("(k p) n -> p k n", p=P)
    with ExitStack() as ctx:
        ident_sb = ctx.enter_context(nc.sbuf_tensor("ident_sb", [P, P], F32))
        s_ahead = ctx.enter_context(nc.semaphore("s_ahead"))
        w, ahead = {}, []
        for name, shape, source in (
                ("wq", [P, KT, G * P], channels(wq)), ("bqk", [P, 2 * G], bqk), ("wk", [P, KT, G * P], channels(wk)),
                ("wv", [P, KT, G * P], channels(wv)), ("bv", [P, G * P], bv.partition_broadcast(P)),
                ("swap", [P, P], swap), ("wo", [P, G, DM], channels(wo)), ("w1", [P, KT, E * DM], channels(w1)),
                ("w2", [P, E * KT, DM], channels(w2)), ("gw", [P, KT, E], channels(gw)),
                ("gb", [P, E], gb.partition_broadcast(P)),
                ("lnp", [P, 2 * E * KT], lnp),
                ("g2", [P, E * DM], g2.partition_broadcast(P)),
                ("ones3", [3 * BLK, P], ones3.bitcast(BF16))):
            w[name] = ctx.enter_context(nc.sbuf_tensor(name + "_sb", shape, BF16 if name == "ones3" else F32))
            ahead.append((w[name][tuple(slice(None) for _ in shape)], source))
        mamba_block(nc, x, xT, w_in, w_x, w_out, par, ident_sb, ident, sel_bc, sel_p, c_dram, x1, ahead, s_ahead)
        attn_ffn_block(nc, x1, ctxT, ident_sb, w, ahead, s_ahead, be2, bias_rows, before, out)


def _constants():
    one = 0x3F80
    sel_bc = np.zeros((PARTS * BC, NS, P), np.uint16)
    for q in range(PARTS):
        for n in range(NS):
            sel_bc[BC * q + n, n, :] = one
    sel_p = np.zeros((PROJ, P), np.float32)
    sel_p[PROJ - 1] = 1
    swap = np.zeros((P, P), np.float32)
    for j in range(HG):
        for i in range(HD):
            swap[BLK * j + HD + i, BLK * j + i] = 1
            swap[BLK * j + HD + i, BLK * j + HD + i] = 1
    ones3 = np.zeros((3 * BLK, P), np.uint16)
    ones3[0::BLK] = one
    before = np.tri(E, k=-1, dtype=np.float32).reshape(E * E)
    return dict(ident=np.eye(P, dtype=np.float32), sel_bc=sel_bc, sel_p=sel_p, swap=swap, ones3=ones3, before=before)


def _layout(inputs):
    f32 = np.float32
    attn = lambda n: np.asarray(inputs["L0_attn_" + n])
    xatt = lambda n: np.asarray(inputs["L0_xattn_" + n])
    ffn = lambda n: np.asarray(inputs["L0_ffn_" + n])
    per_channel = lambda a: a.reshape(CT, P, -1).transpose(1, 0, 2).reshape(P, -1)

    def heads(w, spare=0):
        o = np.zeros(w.shape[:-1] + (BLK,), f32)
        o[..., :HD] = w
        if spare:
            o[..., HD:HD + spare] = 1
        return o.reshape(w.shape[:-2] + (NH * BLK,))

    x = np.asarray(inputs["x"]).reshape(BATCH * L, DM)
    par = np.zeros((P, PAR_COLS), f32)
    par[:, 0:PAR_COLS] = np.concatenate([per_channel(attn(n)) for n in
                                         ("A_log", "conv_w", "conv_b", "D_param", "W_dt", "b_dt")], 1)
    w_x = attn("W_x").T
    wo = np.zeros((NH, BLK, DM), f32)
    wo[:, :HD] = xatt("Wo")
    wo[0, HD] = xatt("bo")
    bias_rows = np.zeros((3 * BLK, 2 * E * DM), f32)
    bias_rows[0::BLK] = np.concatenate([ffn("b1").reshape(-1), ffn("b2").reshape(-1)])
    return dict(
        x=x, xT=x.T, w_in=attn("W_in").T,
        w_x=np.concatenate([w_x[:, :BC]] * PARTS + [w_x[:, BC:]], 1), w_out=attn("W_out").T, par=par,
        ctxT=np.asarray(inputs["ctx_1024"]).reshape(BATCH * S, DM).T,
        wq=heads(xatt("Wq")), wk=heads(xatt("Wk")), wv=heads(xatt("Wv")), wo=wo.reshape(NH * BLK, DM),
        bqk=np.concatenate([heads(xatt("bq")).reshape(G, P).T, heads(xatt("bk"), 1).reshape(G, P).T], 1),
        bv=heads(xatt("bv"), HD),
        w1=ffn("W1").transpose(1, 0, 2).reshape(DM, E * DM), w2=ffn("W2").reshape(E * DM, DM),
        gw=ffn("gate_W"), gb=ffn("gate_b"),
        lnp=np.concatenate([ffn("g1").reshape(E * KT, P).T, ffn("be1").reshape(E * KT, P).T], 1),
        bias_rows=bias_rows, g2=ffn("g2").reshape(-1), be2=ffn("be2").reshape(-1), **_constants())


_ARGS = ["x", "xT", "w_in", "w_x", "w_out", "par", "ident", "sel_bc", "sel_p", "ctxT", "wq", "wk", "wv", "wo",
         "bqk", "bv", "swap", "w1", "w2", "gw", "gb", "lnp", "bias_rows", "ones3", "g2", "be2", "before"]


def kernel(**inputs):
    import concourse.bacc as bacc
    from concourse.bass_utils import run_bass_kernel_spmd
    nc = bacc.Bacc("TRN2", target_bir_lowering=False, num_devices=1)
    data = _layout(inputs)
    arrays, args = {}, []
    for name in _ARGS:
        a = np.ascontiguousarray(data[name])
        arrays["in_" + name] = a
        args.append(nc.dram_tensor("in_" + name, a.shape, mybir.dt.from_np(a.dtype), kind="ExternalInput").ap())
    out = nc.dram_tensor("out_x", (BATCH * L, DM), F32, kind="ExternalOutput").ap()
    decoder_block(nc, *args, out)
    r = run_bass_kernel_spmd(nc, [arrays], core_ids=[0])
    return r.results[0]["out_x"].reshape(BATCH, L, DM)
```
